# Optimizing a Trainium2 kernel written in Bass

```python
import numpy as np
import jax
import jax.numpy as jnp

def _softmax(x, axis=-1):
    return jax.nn.softmax(x, axis=axis)

def _gelu(x):
    return jax.nn.gelu(x, approximate=True)

def _silu(x):
    return jax.nn.silu(x)

def _sigmoid(x):
    return jax.nn.sigmoid(x)

def _layernorm(x, axis=-1, eps=1e-05):
    m = jnp.mean(x, axis=axis, keepdims=True)
    v = jnp.var(x, axis=axis, keepdims=True)
    return (x - m) / jnp.sqrt(v + eps)

def _scatter_add(tgt, idx, src, axis=0):
    return tgt.at[idx].add(src)

def _segment_sum(src, seg, n):
    return jax.ops.segment_sum(src, seg, n)
kernel_name = 'mk_adaln_d2_jaxref_r8_bd7122'

def setup_inputs(seed: int=0):
    np.random.seed(seed)
    _w = jnp.asarray

    def _L0_attn_setup():
        import jax, jax.numpy as jnp
        import numpy as np
        import math
        DIM = 128
        HEADS = 16
        HEAD_DIM = DIM // HEADS
        B, N = (1, 512)
        key = jax.random.key(seed)
        k1, k2, k3, k4 = jax.random.split(key, 4)
        content = jax.random.normal(k1, (B, N, DIM), dtype=jnp.float32)
        Wq = jnp.eye(DIM, dtype=jnp.float32) + 0.02 * jax.random.normal(k2, (DIM, DIM), dtype=jnp.float32)
        Wk = jnp.eye(DIM, dtype=jnp.float32) + 0.02 * jax.random.normal(k3, (DIM, DIM), dtype=jnp.float32)
        Wv = jnp.eye(DIM, dtype=jnp.float32) + 0.02 * jax.random.normal(k4, (DIM, DIM), dtype=jnp.float32)
        return {'content': content, 'Wq': Wq, 'Wk': Wk, 'Wv': Wv}
    _L0_attn_in = _L0_attn_setup()

    def _L0_ffn_setup():
        import jax, jax.numpy as jnp
        import numpy as np
        B, S, D, F, E, TOPK = (4, 256, 128, 512, 8, 2)

        def _moe_forward(x, W_router, W_gate, W_up, W_down):
            logits = jnp.einsum('bsd,ed->bse', x, W_router)
            probs = jax.nn.softmax(logits, axis=-1)
            gates, indices = jax.lax.top_k(probs, TOPK)
            gates = gates / jnp.sum(gates, axis=-1, keepdims=True)
            weights = jnp.sum(gates[..., None] * jax.nn.one_hot(indices, E, dtype=x.dtype), axis=-2)
            weights_e = jnp.moveaxis(weights, -1, 0)

            def body(acc, params):
                wg, wu, wd, wt = params
                gate = jax.nn.silu(jnp.einsum('bsd,fd->bsf', x, wg))
                up = jnp.einsum('bsd,fd->bsf', x, wu)
                y = jnp.einsum('bsf,df->bsd', gate * up, wd)
                return (acc + wt[..., None] * y, None)
            out, _ = jax.lax.scan(body, jnp.zeros_like(x), (W_gate, W_up, W_down, weights_e))
            return out
        key = jax.random.key(seed)
        k1, k2, k3, k4, k5 = jax.random.split(key, 5)
        x = jax.random.normal(k1, (B, S, D), dtype=jnp.float32)
        W_router = jax.random.normal(k2, (E, D), dtype=jnp.float32) / np.sqrt(D)
        W_gate = jax.random.normal(k3, (E, F, D), dtype=jnp.float32) / np.sqrt(D)
        W_up = jax.random.normal(k4, (E, F, D), dtype=jnp.float32) / np.sqrt(D)
        W_down = jax.random.normal(k5, (E, D, F), dtype=jnp.float32) / np.sqrt(F)
        return {'x': x, 'W_router': W_router, 'W_gate': W_gate, 'W_up': W_up, 'W_down': W_down}
    _L0_ffn_in = _L0_ffn_setup()
    _L0_c = _w((lambda *s: np.random.randn(*s).astype(np.float32) * 0.05)(8, 128))
    _L0_wmod = _w((lambda *s: np.random.randn(*s).astype(np.float32) * 0.05)(128, 6 * 128) * 128 ** (-0.5))

    def _L1_attn_setup():
        import jax, jax.numpy as jnp
        import numpy as np
        NUM_HEADS = 16
        D_MODEL = 128
        D_K = D_MODEL // NUM_HEADS
        MAX_SEQ_LEN = 512
        ROPE_BASE = 10000.0
        BATCH = 2
        SEQ_LEN = 256

        def _rope_tables(seq_len, d_k, base=ROPE_BASE):
            theta = 1.0 / base ** (jnp.arange(0, d_k, 2, dtype=jnp.float32) / d_k)
            m = jnp.arange(seq_len, dtype=jnp.float32)
            m_theta = jnp.outer(m, theta)
            ang = jnp.concatenate([m_theta, m_theta], axis=-1)
            return (jnp.cos(ang), jnp.sin(ang))

        def _apply_rope(x, cos, sin):
            d2 = x.shape[-1] // 2
            x1, x2 = (x[..., :d2], x[..., d2:])
            x_flip = jnp.concatenate([-x2, x1], axis=-1)
            return x * cos + x_flip * sin
        key = jax.random.key(seed)
        kx, kq, kk, kv, ko = jax.random.split(key, 5)
        s = 1.0 / np.sqrt(D_MODEL)
        x = jax.random.normal(kx, (BATCH, SEQ_LEN, D_MODEL), dtype=jnp.float32)
        W_Q = jax.random.uniform(kq, (D_MODEL, D_MODEL), jnp.float32, -s, s)
        W_K = jax.random.uniform(kk, (D_MODEL, D_MODEL), jnp.float32, -s, s)
        W_V = jax.random.uniform(kv, (D_MODEL, D_MODEL), jnp.float32, -s, s)
        W_O = jax.random.uniform(ko, (D_MODEL, D_MODEL), jnp.float32, -s, s)
        return {'x': x, 'W_Q': W_Q, 'W_K': W_K, 'W_V': W_V, 'W_O': W_O}
    _L1_attn_in = _L1_attn_setup()

    def _L1_ffn_setup():
        import jax, jax.numpy as jnp
        import numpy as np
        D_MODEL = 128
        M = 64
        INNER = 16
        key = jax.random.key(seed)
        ks = jax.random.split(key, 9)

        def init(k, shape, fan_in):
            bound = 1.0 / np.sqrt(fan_in)
            return jax.random.uniform(k, shape, jnp.float32, -bound, bound)
        x = jax.random.normal(ks[0], (16, 512, D_MODEL), dtype=jnp.float32)
        Win = init(ks[1], (D_MODEL, M), D_MODEL)
        bin_ = init(ks[2], (M,), D_MODEL)
        W1 = init(ks[3], (M, INNER), 1)
        b1 = init(ks[4], (M, INNER), 1)
        W2 = init(ks[5], (M, INNER), INNER)
        b2 = init(ks[6], (M,), INNER)
        Wout = init(ks[7], (M, D_MODEL), M)
        bout = init(ks[8], (D_MODEL,), M)
        return {'x': x, 'Win': Win, 'bin_': bin_, 'W1': W1, 'b1': b1, 'W2': W2, 'b2': b2, 'Wout': Wout, 'bout': bout}
    _L1_ffn_in = _L1_ffn_setup()
    _L1_c = _w((lambda *s: np.random.randn(*s).astype(np.float32) * 0.05)(8, 128))
    _L1_wmod = _w((lambda *s: np.random.randn(*s).astype(np.float32) * 0.05)(128, 6 * 128) * 128 ** (-0.5))
    _d = {'L0_attn_content': _L0_attn_in['content'], 'L0_attn_Wq': _L0_attn_in['Wq'], 'L0_attn_Wk': _L0_attn_in['Wk'], 'L0_attn_Wv': _L0_attn_in['Wv'], 'L0_ffn_W_router': _L0_ffn_in['W_router'], 'L0_ffn_W_gate': _L0_ffn_in['W_gate'], 'L0_ffn_W_up': _L0_ffn_in['W_up'], 'L0_ffn_W_down': _L0_ffn_in['W_down'], 'L0_c': _L0_c, 'L0_wmod': _L0_wmod, 'L1_attn_W_Q': _L1_attn_in['W_Q'], 'L1_attn_W_K': _L1_attn_in['W_K'], 'L1_attn_W_V': _L1_attn_in['W_V'], 'L1_attn_W_O': _L1_attn_in['W_O'], 'L1_ffn_Win': _L1_ffn_in['Win'], 'L1_ffn_bin_': _L1_ffn_in['bin_'], 'L1_ffn_W1': _L1_ffn_in['W1'], 'L1_ffn_b1': _L1_ffn_in['b1'], 'L1_ffn_W2': _L1_ffn_in['W2'], 'L1_ffn_b2': _L1_ffn_in['b2'], 'L1_ffn_Wout': _L1_ffn_in['Wout'], 'L1_ffn_bout': _L1_ffn_in['bout'], 'L1_c': _L1_c, 'L1_wmod': _L1_wmod}
    _x0 = _d['L0_attn_content']
    _d['L0_attn_content'] = jax.random.normal(jax.random.fold_in(jax.random.key(seed), 1), (8, 512, 128), dtype=_x0.dtype)
    del _x0
    return _d

def reference(L0_attn_content, L0_attn_Wq, L0_attn_Wk, L0_attn_Wv, L0_ffn_W_router, L0_ffn_W_gate, L0_ffn_W_up, L0_ffn_W_down, L0_c, L0_wmod, L1_attn_W_Q, L1_attn_W_K, L1_attn_W_V, L1_attn_W_O, L1_ffn_Win, L1_ffn_bin_, L1_ffn_W1, L1_ffn_b1, L1_ffn_W2, L1_ffn_b2, L1_ffn_Wout, L1_ffn_bout, L1_c, L1_wmod):

    def _L0_attn_ref(content, Wq, Wk, Wv):
        import jax, jax.numpy as jnp
        import numpy as np
        import math
        DIM = 128
        HEADS = 16
        HEAD_DIM = DIM // HEADS
        B, N = (1, 512)
        b, n, d = content.shape
        Q = (content @ Wq).reshape(b, n, HEADS, HEAD_DIM)
        K = (content @ Wk).reshape(b, n, HEADS, HEAD_DIM)
        V = (content @ Wv).reshape(b, n, HEADS, HEAD_DIM)
        scores = jnp.einsum('bqhd,bkhd->bhqk', Q, K) / math.sqrt(HEAD_DIM)
        alpha = jax.nn.softmax(scores, axis=-1)
        causal = jnp.tril(jnp.ones((n, n), dtype=bool))
        alpha = jnp.where(causal, alpha, jnp.zeros((), dtype=alpha.dtype))
        Y = jnp.einsum('bhqk,bkhd->bqhd', alpha, V).reshape(b, n, d)
        return Y

    def _L0_ffn_ref(x, W_router, W_gate, W_up, W_down):
        import jax, jax.numpy as jnp
        import numpy as np
        B, S, D, F, E, TOPK = (4, 256, 128, 512, 8, 2)

        def _moe_forward(x, W_router, W_gate, W_up, W_down):
            logits = jnp.einsum('bsd,ed->bse', x, W_router)
            probs = jax.nn.softmax(logits, axis=-1)
            gates, indices = jax.lax.top_k(probs, TOPK)
            gates = gates / jnp.sum(gates, axis=-1, keepdims=True)
            weights = jnp.sum(gates[..., None] * jax.nn.one_hot(indices, E, dtype=x.dtype), axis=-2)
            weights_e = jnp.moveaxis(weights, -1, 0)

            def body(acc, params):
                wg, wu, wd, wt = params
                gate = jax.nn.silu(jnp.einsum('bsd,fd->bsf', x, wg))
                up = jnp.einsum('bsd,fd->bsf', x, wu)
                y = jnp.einsum('bsf,df->bsd', gate * up, wd)
                return (acc + wt[..., None] * y, None)
            out, _ = jax.lax.scan(body, jnp.zeros_like(x), (W_gate, W_up, W_down, weights_e))
            return out
        return _moe_forward(x, W_router, W_gate, W_up, W_down)

    def _L1_attn_ref(x, W_Q, W_K, W_V, W_O):
        import jax, jax.numpy as jnp
        import numpy as np
        NUM_HEADS = 16
        D_MODEL = 128
        D_K = D_MODEL // NUM_HEADS
        MAX_SEQ_LEN = 512
        ROPE_BASE = 10000.0
        BATCH = 2
        SEQ_LEN = 256

        def _rope_tables(seq_len, d_k, base=ROPE_BASE):
            theta = 1.0 / base ** (jnp.arange(0, d_k, 2, dtype=jnp.float32) / d_k)
            m = jnp.arange(seq_len, dtype=jnp.float32)
            m_theta = jnp.outer(m, theta)
            ang = jnp.concatenate([m_theta, m_theta], axis=-1)
            return (jnp.cos(ang), jnp.sin(ang))

        def _apply_rope(x, cos, sin):
            d2 = x.shape[-1] // 2
            x1, x2 = (x[..., :d2], x[..., d2:])
            x_flip = jnp.concatenate([-x2, x1], axis=-1)
            return x * cos + x_flip * sin
        B, S, _ = x.shape

        def proj(W):
            y = jnp.einsum('bsd,ed->bse', x, W)
            return y.reshape(B, S, NUM_HEADS, D_K).transpose(0, 2, 1, 3)
        Q, K, V = (proj(W_Q), proj(W_K), proj(W_V))
        cos, sin = _rope_tables(S, D_K)
        Q = _apply_rope(Q, cos, sin)
        K = _apply_rope(K, cos, sin)
        scores = jnp.einsum('bhsd,bhtd->bhst', Q, K) / jnp.sqrt(jnp.float32(D_K))
        causal = jnp.tril(jnp.ones((S, S), dtype=bool))
        scores = jnp.where(causal[None, None], scores, -jnp.inf)
        attn = jax.nn.softmax(scores, axis=-1)
        out = jnp.einsum('bhst,bhtd->bhsd', attn, V)
        out = out.transpose(0, 2, 1, 3).reshape(B, S, D_MODEL)
        return jnp.einsum('bsd,ed->bse', out, W_O)

    def _L1_ffn_ref(x, Win, bin_, W1, b1, W2, b2, Wout, bout):
        import jax, jax.numpy as jnp
        import numpy as np
        D_MODEL = 128
        M = 64
        INNER = 16
        s = jnp.einsum('btd,dm->btm', x, Win) + bin_
        h = jax.nn.relu(s[..., None] * W1 + b1)
        g = jnp.einsum('btmh,mh->btm', h, W2) + b2
        out = jnp.einsum('btm,md->btd', g, Wout) + bout
        return out
    x = L0_attn_content
    mod = (_silu(L0_c) @ L0_wmod).reshape(L0_c.shape[0], 6, 1, -1)
    sa, ca, ga, sb, cb, gb = (mod[:, 0], mod[:, 1], mod[:, 2], mod[:, 3], mod[:, 4], mod[:, 5])
    ga = (2 * (ga >= 0) - 1) * jnp.maximum(jnp.abs(ga), 0.25)
    gb = (2 * (gb >= 0) - 1) * jnp.maximum(jnp.abs(gb), 0.25)
    h = _layernorm(x, axis=-1) * (1 + ca) + sa
    x = x + ga * _L0_attn_ref(h, L0_attn_Wq, L0_attn_Wk, L0_attn_Wv)
    h = _layernorm(x, axis=-1) * (1 + cb) + sb
    x = x + gb * _L0_ffn_ref(h, L0_ffn_W_router, L0_ffn_W_gate, L0_ffn_W_up, L0_ffn_W_down)
    mod = (_silu(L1_c) @ L1_wmod).reshape(L1_c.shape[0], 6, 1, -1)
    sa, ca, ga, sb, cb, gb = (mod[:, 0], mod[:, 1], mod[:, 2], mod[:, 3], mod[:, 4], mod[:, 5])
    ga = (2 * (ga >= 0) - 1) * jnp.maximum(jnp.abs(ga), 0.25)
    gb = (2 * (gb >= 0) - 1) * jnp.maximum(jnp.abs(gb), 0.25)
    h = _layernorm(x, axis=-1) * (1 + ca) + sa
    x = x + ga * _L1_attn_ref(h, L1_attn_W_Q, L1_attn_W_K, L1_attn_W_V, L1_attn_W_O)
    h = _layernorm(x, axis=-1) * (1 + cb) + sb
    x = x + gb * _L1_ffn_ref(h, L1_ffn_Win, L1_ffn_bin_, L1_ffn_W1, L1_ffn_b1, L1_ffn_W2, L1_ffn_b2, L1_ffn_Wout, L1_ffn_bout)
    return x

_drawn_inputs = setup_inputs


def setup_inputs(seed=0):
    import zlib

    import numpy as np

    out = dict(_drawn_inputs(seed))
    spreads = {}
    factors = {'L1_attn_W_Q': 8.0,
     'L1_attn_W_K': 8.0,
     'L1_attn_W_V': 5.63,
     'L1_attn_W_O': 5.659,
     'L1_ffn_Win': 3.361,
     'L1_ffn_bin_': 27.177,
     'L1_ffn_W1': 3.306,
     'L1_ffn_bout': 8.069,
     'L1_ffn_b1': 4.786,
     'L1_ffn_b2': 6.128}
    for name, (base, spread) in spreads.items():
        noise = np.random.default_rng([zlib.crc32(name.encode()), seed]).standard_normal(out[name].shape)
        drawn = base * np.exp(spread * noise) if base else spread * noise
        out[name] = jnp.asarray(drawn.astype(out[name].dtype))
    for name, factor in factors.items():
        out[name] = (out[name] * factor).astype(out[name].dtype)
    return out
```

```python
from contextlib import ExitStack, contextmanager

import numpy as np

import concourse.bass as bass
from concourse import mybir

F32 = mybir.dt.float32
BF16 = mybir.dt.bfloat16
ALU = mybir.AluOpType
ACT = mybir.ActivationFunctionType
AX = mybir.AxisListType

P = 128
B, T, D = 8, 512, 128
NT = T // P
H = 16
HD = D // H
HG = 4
NG = H // HG
E, F = 8, 512
FT = F // P
M, INNER = 64, 16
NJ = M * INNER // P
EPS = 1e-5
GATE_MIN = 0.25
MASKED = -1e30
SCALE = float(HD) ** -0.5
ROWS = 9 * HD
SHIFT = ROWS
LEAD = 6
MODS = 6
NORM1, NORM2 = (0, 1, 2), (3, 4, 5)


def constants():
    f32 = {}
    f32["ident"] = np.eye(P, dtype=np.float32)
    perm = np.zeros((P, P), np.float32)
    rot = np.zeros((P, P), np.float32)
    half = HD // 2
    for h in range(H):
        for d in range(HD):
            perm[h * HD + d, d * H + h] = 1.0
            if d < half:
                rot[h * HD + d + half, d * H + h] = -1.0
            else:
                rot[h * HD + d - half, d * H + h] = 1.0
    f32["perm"], f32["rot"] = perm, rot
    theta = (np.float32(1.0) / np.float32(10000.0) ** (np.arange(0, HD, 2, dtype=np.float32) / np.float32(HD))).astype(np.float32)
    angle = np.outer(np.arange(T, dtype=np.float32), theta).astype(np.float32)
    angle = np.concatenate([angle, angle], axis=-1)
    f32["cos"] = np.repeat(np.cos(angle).T.astype(np.float32), H, axis=0)
    f32["sin"] = np.repeat(np.sin(angle).T.astype(np.float32), H, axis=0)
    den = np.zeros((P, 32), np.float32)
    den[:, HD] = 1.0
    f32["den_col"] = den
    before = (np.arange(E)[None, :] < np.arange(E)[:, None]).astype(np.float32)
    f32["before"] = np.broadcast_to(before.reshape(1, -1), (P, E * E))
    k = np.arange(P)
    f32["causal_t"] = (k[:, None] <= k[None, :]).astype(np.float32)
    unit = np.zeros((P, NJ * P), np.float32)
    unit[(np.arange(NJ * P) // INNER), np.arange(NJ * P)] = 1.0
    f32["unit_of"] = unit
    off, cols = {}, 0
    for name, a in f32.items():
        off[name] = (cols, a.shape[1])
        cols += a.shape[1]
    packed = np.ascontiguousarray(np.concatenate(list(f32.values()), axis=1), dtype=np.float32)
    later = k[None, :] > k[:, None]
    bf = np.concatenate([np.eye(P), np.where(later, MASKED, 0.0), np.where(later.T, MASKED, 0.0)], axis=1)
    return packed, off, bf.astype(mybir.dt.np(BF16))


def adaln_kernel(nc, a, out, const_off):
    with ExitStack() as ctx:
        k = Kernel(nc, ctx, a, out, const_off)
        setup_phase(k)
        attention_phase(k, 0)
        experts_phase(k)
        attention_phase(k, 1)
        units_phase(k)


class Kernel:

    def __init__(self, nc, ctx, a, out, const_off):
        self.nc, self.ctx, self.a, self.out = nc, ctx, a, out
        self.x = self.sb("x_res", [P, B * NT, D], F32)
        width = sum(w for _, w in const_off.values())
        self.const = self.sb("consts", [P, width], F32)
        self.c = {n: self.const[:, o:o + w] for n, (o, w) in const_off.items()}
        self.cbf = self.sb("consts_bf16", [P, 3, P], BF16)
        self.eps = self.sb("eps", [P, NT], F32)
        self.minus_half = self.sb("minus_half", [P, NT], F32)
        self.mod = [self.sb(f"mod{l}", [P, 4, B], F32) for l in range(2)]
        self.gate = [self.sb(f"gate{l}", [P, 2, B, D], F32) for l in range(2)]
        self.w_qkv0 = self.sb("w_qkv0", [P, 3, D], F32)
        self.w_qk0 = self.sb("w_qk0", [P, 2, D], F32)
        self.w1 = self.sb("w1_proj", [P, 6, D], F32)
        self.router = self.sb("router_t", [P, E], F32)
        self.win_rep = self.sb("win_rep", [P, M, INNER], F32)
        self.w1c = self.sb("w1_col", [P, NJ], F32)
        self.b1c = self.sb("b1_col", [P, NJ], F32)
        self.wout_rep = self.sb("wout_rep", [P, NJ, D], F32)
        self.bout = self.sb("bout_all", [P, D], F32)

    def sb(self, name, shape, dt, ctx=None):
        return (ctx or self.ctx).enter_context(self.nc.sbuf_tensor(name, shape, dt))


MOD_ROWS = {"attn": (0, 1), "ffn": (2, 3)}


def setup_phase(k):
    nc, a = k.nc, k.a
    with ExitStack() as ctx:
        def sb(name, shape, dt=F32):
            return k.sb(name, shape, dt, ctx)

        def sem(name):
            return ctx.enter_context(nc.semaphore(name))

        ps = [ctx.enter_context(nc.psum_tensor(f"su_ps{i}", [P, 512], F32)) for i in range(4)]
        c_raw = sb("c_raw", [B, 2, D])
        wmod = sb("wmod", [P, 2, MODS * D])
        c_t = sb("c_t", [P, 2, B])
        c_e = sb("c_e", [P, 2, B])
        c_silu = sb("c_silu", [P, 2, B])
        c_all = sb("c_all", [P, 2, B, P])
        g_sign = sb("g_sign", [P, 2 * B * D])
        g_abs = sb("g_abs", [P, 2 * B * D])
        w_raw = sb("w_raw", [P, 4, D])
        router_raw = sb("router_raw", [E, D])
        win_raw = sb("win_raw", [P, M])
        wout_raw = sb("wout_raw", [M, D + 1])
        b2_raw = sb("b2_raw", [M, 1])
        unit_raw = sb("unit_raw", [NJ, 3, P])
        unit_col = sb("unit_col", [P, 3, NJ])
        bout_raw = sb("bout_raw", [P, D])

        s_const, s_c, s_wmod, s_x, s_w, s_kan = (sem(n) for n in ("su_const", "su_c", "su_wmod", "su_x", "su_w", "su_kan"))
        pe_done, dve_done, act_done, pool_done = (sem(n) for n in ("su_pe", "su_dve", "su_act", "su_pool"))

        with nc.Block() as block:
            @block.sync
            def _(sp):
                sp.dma_start(c_raw[:, 0, :], a["L0_c"]).then_inc(s_c, 16)
                sp.dma_start(c_raw[:, 1, :], a["L1_c"]).then_inc(s_c, 16)
                sp.dma_start(k.const[:], a["const_f32"]).then_inc(s_const, 16)
                sp.dma_start(wmod[:, 0, :], a["L0_wmod"]).then_inc(s_wmod, 16)
                sp.dma_start(wmod[:, 1, :], a["L1_wmod"]).then_inc(s_wmod, 16)
                for i, n in enumerate(("Q", "K", "V", "O")):
                    sp.dma_start(w_raw[:, i, :], a[f"L1_attn_W_{n}"]).then_inc(s_w, 16)
                sp.dma_start(router_raw[:], a["L0_ffn_W_router"]).then_inc(s_w, 16)
                for i, n in enumerate("qkv"):
                    sp.dma_start(k.w_qkv0[:, i, :], a[f"L0_attn_W{n}"]).then_inc(s_w, 16)
                sp.dma_start(k.cbf[:], a["const_bf16"].rearrange("p (i c) -> p i c", i=3)).then_inc(s_const, 16)
                sp.dma_start(k.x[:], a["L0_attn_content"].rearrange("b (t p) d -> p (b t) d", p=P)).then_inc(s_x, 16)
                sp.wait_ge(s_x, 16)

            @block.scalar
            def _(act):
                act.dma_start(win_raw[:], a["L1_ffn_Win"]).then_inc(s_kan, 16)
                act.dma_start(wout_raw[:, 0:D], a["L1_ffn_Wout"]).then_inc(s_kan, 16)
                act.dma_start(wout_raw[:, D:D + 1], a["L1_ffn_bin_"].rearrange("(m o) -> m o", o=1)).then_inc(s_kan, 16)
                act.dma_start(b2_raw[:], a["L1_ffn_b2"].rearrange("(m o) -> m o", o=1)).then_inc(s_kan, 16)
                for i, n in enumerate(("W1", "b1", "W2")):
                    act.dma_start(unit_raw[:, i, :], a[f"L1_ffn_{n}"].rearrange("(j a) h -> j (a h)", j=NJ)).then_inc(s_kan, 16)
                act.dma_start(bout_raw[:], a["L1_ffn_bout"].partition_broadcast(P)).then_inc(s_kan, 16)
                act.wait_ge(dve_done, 1)
                nc.scalar.activation(c_e[:], c_t[:], ACT.Exp, scale=-1.0).then_inc(act_done, 1)

            @block.gpsimd
            def _(pool):
                nc.gpsimd.memset(k.eps[:], EPS)
                nc.gpsimd.memset(k.minus_half[:], -0.5).then_inc(pool_done, 1)
                pool.wait_ge(s_kan, 128)
                nc.gpsimd.tensor_copy(k.win_rep[:], win_raw[:, :, None].to_broadcast([P, M, INNER])).then_inc(pool_done, 1)

            @block.tensor
            def _(pe):
                pe.wait_ge(s_const, 32)
                pe.wait_ge(s_c, 32)
                for l in range(2):
                    last = nc.tensor.transpose(ps[0][:, l * B:(l + 1) * B], c_raw[:, l, :], k.c["ident"][0:B, 0:B])
                last.then_inc(pe_done, 1)
                pe.wait_ge(s_w, 128)
                for n, (i, m) in enumerate(((0, "perm"), (0, "rot"), (1, "perm"), (1, "rot"))):
                    last = nc.tensor.matmul(ps[1][:, n * D:(n + 1) * D], w_raw[:, i, :], k.c[m], start=True, stop=True)
                last.then_inc(pe_done, 1)
                for n, i in enumerate((2, 3)):
                    nc.tensor.transpose(ps[2][:, n * D:(n + 1) * D], w_raw[:, i, :], k.c["ident"])
                nc.tensor.transpose(ps[2][:, 2 * D:2 * D + E], router_raw[:], k.c["ident"][0:E, 0:E])
                pe.wait_ge(s_kan, 128)
                for i in range(3):
                    last = nc.tensor.transpose(ps[2][:, 2 * D + E + i * NJ:2 * D + E + (i + 1) * NJ], unit_raw[:, i, :],
                                               k.c["ident"][0:NJ, 0:NJ])
                last.then_inc(pe_done, 1)
                for j in range(NJ):
                    if j >= 2:
                        pe.wait_ge(dve_done, 7 + 2 * (j - 2))
                    else:
                        pe.wait_ge(dve_done, 5)
                    nc.tensor.matmul(ps[1 + j % 2][:, 0:D + 1], k.c["unit_of"][0:M, j * P:(j + 1) * P], wout_raw[:],
                                     start=True, stop=True).then_inc(pe_done, 1)
                nc.tensor.matmul(ps[3][:, 0:D], b2_raw[:, 0:1].to_broadcast([M, P]), wout_raw[:, 0:D],
                                 start=True, stop=True).then_inc(pe_done, 1)
                pe.wait_ge(dve_done, 26)
                pe.wait_ge(s_wmod, 32)
                for l in range(2):
                    for n, j in enumerate((0, 1, 3, 4)):
                        last = nc.tensor.matmul(ps[0][:, (l * 4 + n) * B:(l * 4 + n + 1) * B], wmod[:, l, j * D:(j + 1) * D],
                                                c_silu[:, l, :], start=True, stop=True)
                last.then_inc(pe_done, 1)
                n = 0
                for l in range(2):
                    for gi, j in enumerate((2, 5)):
                        for hb in range(2):
                            pe.wait_ge(dve_done, 27 if n < 2 else 30 + n)
                            for q in range(4):
                                b = hb * 4 + q
                                last = nc.tensor.matmul(ps[1 + n % 2][:, q * D:(q + 1) * D], c_all[:, l, b, :],
                                                        wmod[:, l, j * D:(j + 1) * D], start=True, stop=True)
                            last.then_inc(pe_done, 1)
                            n += 1

            @block.vector
            def _(dve):
                n = [0]

                def link(ins):
                    n[0] += 1
                    ins.then_inc(dve_done, 1)
                    dve.wait_ge(dve_done, n[0])

                dve.wait_ge(pe_done, 1)
                link(nc.vector.tensor_copy(c_t[:], ps[0][:, 0:2 * B].rearrange("p (l b) -> p l b", l=2)))
                dve.wait_ge(pe_done, 3)
                link(nc.vector.tensor_copy(k.w1[:, 0:4, :], ps[1][:].rearrange("p (i d) -> p i d", i=4)))
                link(nc.vector.tensor_copy(k.w1[:, 4:6, :], ps[2][:, 0:2 * D].rearrange("p (i d) -> p i d", i=2)))
                link(nc.vector.tensor_copy(k.router[:], ps[2][:, 2 * D:2 * D + E]))
                link(nc.vector.tensor_copy(unit_col[:], ps[2][:, 2 * D + E:2 * D + E + 3 * NJ].rearrange("p (i j) -> p i j", i=3)))
                for j in range(NJ):
                    dve.wait_ge(pe_done, 4 + j)
                    pj = ps[1 + j % 2]
                    link(nc.vector.tensor_scalar(k.b1c[:, j:j + 1], pj[:, D:D + 1], unit_col[:, 0, j:j + 1], unit_col[:, 1, j:j + 1],
                                                 ALU.mult, ALU.add))
                    link(nc.vector.tensor_scalar(k.wout_rep[:, j, :], pj[:, 0:D], unit_col[:, 2, j:j + 1], None, ALU.mult))
                dve.wait_ge(pe_done, 4 + NJ)
                dve.wait_ge(s_kan, 128)
                link(nc.vector.tensor_copy(k.w1c[:], unit_col[:, 0, :]))
                link(nc.vector.tensor_tensor(k.bout[:], ps[3][:, 0:D], bout_raw[:], ALU.add))
                dve.wait_ge(act_done, 1)
                link(nc.vector.tensor_scalar(c_e[:], c_e[:], 1.0, None, ALU.add))
                link(nc.vector.reciprocal(c_e[:], c_e[:]))
                link(nc.vector.tensor_tensor(c_silu[:], c_t[:], c_e[:], ALU.mult))
                link(nc.vector.tensor_copy(c_all[:], c_silu[:, :, :, None].to_broadcast([P, 2, B, P])))
                dve.wait_ge(pe_done, 5 + NJ)
                for l in range(2):
                    v = ps[0][:, l * 4 * B:(l + 1) * 4 * B].rearrange("p (n b) -> p n b", n=4)
                    link(nc.vector.tensor_copy(k.mod[l][:], v))
                    link(nc.vector.tensor_scalar(k.mod[l][:, 1:4:2, :], k.mod[l][:, 1:4:2, :], 1.0, None, ALU.add))
                for n8 in range(8):
                    l, gi, hb = n8 // 4, n8 // 2 % 2, n8 % 2
                    dve.wait_ge(pe_done, 6 + NJ + n8)
                    link(nc.vector.tensor_copy(k.gate[l][:, gi, hb * 4:hb * 4 + 4, :],
                                               ps[1 + n8 % 2][:].rearrange("p (b d) -> p b d", b=4)))
                dve.wait_ge(s_w, 128)
                for i in range(2):
                    link(nc.vector.tensor_copy(k.w_qk0[:, i, :].rearrange("p (d h) -> p d h", h=H),
                                               k.w_qkv0[:, i, :].rearrange("p (h d) -> p d h", h=H)))
                for l in range(2):
                    g = k.gate[l][:].rearrange("p w b d -> p (w b d)")
                    link(nc.vector.tensor_scalar(g_sign[:], g, 0.0, 2.0, ALU.is_ge, ALU.mult))
                    link(nc.vector.scalar_tensor_tensor(g_abs[:], g, -1.0, g, ALU.mult, ALU.max))
                    link(nc.vector.tensor_scalar(g_abs[:], g_abs[:], GATE_MIN, None, ALU.max))
                    link(nc.vector.scalar_tensor_tensor(g, g_sign[:], -1.0, g_abs[:], ALU.add, ALU.mult))


class Norm:

    def __init__(self, k, ctx, tag):
        self.k = k

        def sem(name):
            return ctx.enter_context(k.nc.semaphore(f"{tag}_{name}"))

        self.stats = k.sb(f"{tag}_stats", [P, NT, 6], F32, ctx)
        self.mv = k.sb(f"{tag}_mean_var", [P, NT, 2], F32, ctx)
        self.rstd = k.sb(f"{tag}_rstd", [P, NT], F32, ctx)
        self.var_eps = k.sb(f"{tag}_var_eps", [P, NT], F32, ctx)
        self.hn = k.sb(f"{tag}_normed", [P, NT, D], F32, ctx)
        self.stats_seen = sem("stats_seen")
        self.stats_ready, self.mv_ready, self.eps_added, self.rstd_ready, self.hn_ready, self.hn_transposed = (
            sem(n) for n in ("stats", "mv", "eps", "rstd", "hn", "hn_transposed"))

    def moments(self, dve, b):
        nc, k = self.k.nc, self.k
        for t in range(NT):
            nc.vector.bn_stats(self.stats[:, t, :], k.x[:, b * NT + t, :]).then_inc(self.stats_ready, 1)
        dve.wait_ge(self.stats_ready, (b + 1) * NT)
        dve.sem_inc(self.stats_seen, 1)
        for t in range(NT):
            nc.vector.bn_aggr(self.mv[:, t, :], self.stats[:, t, :]).then_inc(self.mv_ready, 1)

    def inverse_deviation(self, pool, b):
        nc, k = self.k.nc, self.k
        pool.wait_ge(self.mv_ready, (b + 1) * NT)
        nc.gpsimd.tensor_tensor(self.var_eps[:], self.mv[:, :, 1], k.eps[:], ALU.add).then_inc(self.eps_added, 1)
        pool.wait_ge(self.eps_added, b + 1)
        nc.gpsimd.tensor_tensor(self.rstd[:], self.var_eps[:], k.minus_half[:], ALU.pow).then_inc(self.rstd_ready, 1)

    def normalise(self, dve, b):
        nc, k = self.k.nc, self.k
        dve.wait_ge(self.rstd_ready, b + 1)
        if not (isinstance(b, int) and b == 0):
            dve.wait_ge(self.hn_transposed, b)
        for t in range(NT):
            nc.vector.tensor_scalar(self.hn[:, t, :], k.x[:, b * NT + t, :], self.mv[:, t, 0:1], self.rstd[:, t:t + 1],
                                    ALU.subtract, ALU.mult).then_inc(self.hn_ready, 1)

    def transpose(self, pe, b, bank):
        nc, k = self.k.nc, self.k
        pe.wait_ge(self.hn_ready, (b + 1) * NT)
        for t in range(NT):
            last = nc.tensor.transpose(bank[:, t * P:(t + 1) * P], self.hn[:, t, :], k.c["ident"])
        last.then_inc(self.hn_transposed, 1)


def attention_phase(k, layer):
    nc = k.nc
    causal = layer == 1
    L = f"l{layer}"
    with ExitStack() as ctx:
        def sb(name, shape, dt=F32):
            return k.sb(f"{L}_{name}", shape, dt, ctx)

        def sem(name):
            return ctx.enter_context(nc.semaphore(f"{L}_{name}"))

        def bank(name):
            return ctx.enter_context(nc.psum_tensor(f"{L}_{name}", [P, 512], F32))

        score_ps = [bank(f"score{i}") for i in range(2)]
        shifted_ps = [bank(f"shifted{i}") for i in range(2)]
        o_ps = bank("o")
        proj_ps = bank("proj")
        turn_ps = bank("turn")
        v_ps = bank("v")

        q_stack = sb("q_stack", [P, H, T], BF16)
        k_stack = sb("k_stack", [P, H, T], BF16)
        hT = sb("hT", [P, T])
        parts = sb("parts", [P, 2, 3, T], BF16)
        rest = sb("rest", [P, 2, T])
        v_aug = sb("v_aug", [P, NT, H, 32])
        probs = sb("probs", [P, NT, HG, T])
        mx = sb("mx", [P, 2, HG * NT])
        shift = sb("shift", [HG * NT, 3, P], BF16)
        shift_rest = sb("shift_rest", [HG * NT, P])
        o_sb = sb("o_sb", [P, T])
        rden = sb("rden", [P, NT, HG])
        y = sb("y", [P, NT, D])
        gy = sb("gy", [P, NT, D])
        if causal:
            rope_a = sb("rope_a", [P, 2, T])
            rope_b = sb("rope_b", [P, 2, T])
            turned = sb("turned", [P, 2, T])
            yT = sb("yT", [P, NT, P])
        else:
            masked = sb("masked", [P, NT, HG, P])
        parts_dram = nc.dram_tensor(f"{L}_parts_dram", [B, 2, 5, P, T], BF16).ap()
        norm = Norm(k, ctx, L)

        init_done = sem("init_done")
        hT_ready = sem("hT_ready")
        proj_ready = sem("proj_ready")
        proj_taken = sem("proj_taken")
        v_ready = sem("v_ready")
        v_stored = sem("v_stored")
        hi_ready = sem("hi_ready")
        rest_ready = sem("rest_ready")
        mid_ready = sem("mid_ready")
        lo_ready = sem("lo_ready")
        roped_a = sem("roped_a")
        roped_b = sem("roped_b")
        roped = sem("roped")
        parts_stored = sem("parts_stored")
        stacked = [sem(f"stacked{g}") for g in range(NG)]
        score_ready = sem("score_ready")
        max_taken = sem("max_taken")
        max_turned = sem("max_turned")
        shift_hi, shift_left, shift_mid, shift_ready = (sem(n) for n in ("shift_hi", "shift_left", "shift_mid", "shift_ready"))
        shift_stacked = [sem(f"shift_stacked{g}") for g in range(NG)]
        shifted_ready = sem("shifted_ready")
        exp_done = sem("exp_done")
        diag_masked = sem("diag_masked")
        summed = sem("summed")
        o_taken = sem("o_taken")
        o_turned = sem("o_turned")
        rden_ready = sem("rden_ready")
        y_ready = sem("y_ready")
        y_turned = sem("y_turned")
        yT_ready = sem("yT_ready")
        out_ready = sem("out_ready")
        gy_ready = sem("gy_ready")
        x_updated = sem("x_updated")

        NPROJ = 4 if causal else 2
        UNITS, GROUPS, TILES = H * NT, NG, NG * NT

        def lead_head(b, g, j, following):
            h = HG * g + j + LEAD
            if h < H:
                return b, h
            return (b + 1, h - H) if following else None

        def lead_group(b, g, following):
            if g + 1 < NG:
                return b, g + 1
            return (b + 1, 0) if following else None

        def run(engine, first, slot, finish):
            first(0)
            slot(0, 0, False, True)
            with engine.Fori(0, B - 1) as b:
                for g in range(1, NG):
                    slot(b, g, True, True)
                slot(b + 1, 0, True, True)
            for g in range(1, NG):
                slot(B - 1, g, True, False)
            finish(B - 1)

        def before(b, g):
            return b * GROUPS + g

        block = ctx.enter_context(nc.Block())

        @block.sync
        def _(sp):
            def store_parts(b):
                sp.wait_ge(lo_ready, (b + 1) * 2)
                sp.dma_start(parts_dram[b, 0, 0:3].rearrange("c p t -> p c t"), parts[:, 0]).then_inc(parts_stored, 16)
                sp.dma_start(parts_dram[b, 1, 0:3].rearrange("c p t -> p c t"), parts[:, 1]).then_inc(parts_stored, 16)
                sp.dma_start(parts_dram[b, 1, 3:5].rearrange("c p t -> p c t"), parts[:, 1, 0:2]).then_inc(parts_stored, 16)
                sp.wait_ge(parts_stored, (b + 1) * 48)

            def stack(b, g, prior):
                if prior:
                    sp.wait_ge(exp_done, (b - 1) * UNITS + (g + 1) * HG * NT)
                rows = 3 * HD
                for s in range(3):
                    for side, dst, first in ((0, q_stack, 0), (1, k_stack, s)):
                        src = parts_dram[b, side].rearrange("c (d h) t -> (c d) h t", d=HD)
                        sp.dma_start(dst[rows * s:rows * (s + 1), HG * g:HG * (g + 1), :],
                                     src[HD * first:HD * first + rows, HG * g:HG * (g + 1), :]).then_inc(stacked[g], 16)

            def stack_shift(b, g):
                sp.wait_ge(shift_ready, before(b, g) + 1)
                for c in range(3):
                    sp.dma_start(q_stack[SHIFT + c:SHIFT + c + 1, HG * g:HG * (g + 1), :].rearrange("c h (q t) -> c (h q) t", t=P),
                                 shift[:, c, :]).then_inc(shift_stacked[g], 16)

            def first(b):
                sp.wait_ge(init_done, 3)
                store_parts(b)
                for g in range(NG - 1):
                    stack(b, g, False)
                stack_shift(b, 0)

            def slot(b, g, prev, following):
                if g == 0:
                    stack(b, NG - 1, prev)
                if g == 1 and following:
                    store_parts(b + 1)
                if g >= 1 and following:
                    stack(b + 1, g - 1, True)
                led = lead_group(b, g, following)
                if led:
                    stack_shift(*led)

            run(sp, first, slot, lambda b: None)

        @block.tensor
        def _(pe):
            def project(w, taken_before):
                pe.wait_ge(proj_taken, taken_before)
                nc.tensor.matmul(proj_ps[:], w, hT[:], start=True, stop=True).then_inc(proj_ready, 1)

            if causal:
                weights = [k.w1[:, i, :] for i in range(4)]
                wv = k.w1[:, 4, :]
            else:
                weights = [k.w_qk0[:, i, :] for i in range(2)]
                wv = k.w_qkv0[:, 2, :]

            def turn_norm(b, prior):
                if prior:
                    pe.wait_ge(proj_taken, b * NPROJ)
                norm.transpose(pe, b, proj_ps)

            def project_qk(b, which):
                if which == 0:
                    pe.wait_ge(hT_ready, b + 1)
                    nc.tensor.matmul(proj_ps[:], weights[0], hT[:], start=True, stop=True).then_inc(proj_ready, 1)
                else:
                    project(weights[which], b * NPROJ + which)

            def project_v(b):
                for t in range(NT):
                    last = nc.tensor.matmul(v_ps[:, t * P:(t + 1) * P], hT[:, t * P:(t + 1) * P], wv, start=True, stop=True)
                last.then_inc(v_ready, 1)

            def score(b, h, qt, warm):
                n = b * UNITS + h * NT + qt
                if h % HG == 0 and qt == 0:
                    pe.wait_ge(stacked[h // HG], (b + 1) * 96)
                if warm:
                    pe.wait_ge(max_taken, n - 1)
                cols = (qt + 1) * P if causal else T
                nc_out = score_ps[qt % 2]
                last = nc.tensor.matmul(nc_out[:, 0:cols], q_stack[0:ROWS, h, qt * P:(qt + 1) * P], k_stack[0:ROWS, h, 0:cols],
                                        start=True, stop=not causal)
                if causal:
                    last = nc.tensor.matmul(nc_out[:, qt * P:cols], k.cbf[:, 0, :], k.cbf[:, 1, :],
                                            start=False, stop=True)
                last.then_inc(score_ready, 1)

            def shifted(b, g, kt, i, warm):
                n = b * UNITS + g * HG * NT + kt * HG + i
                h = HG * g + i
                if kt == 0 and i == 0:
                    pe.wait_ge(shift_stacked[g], (b + 1) * 48)
                if warm:
                    pe.wait_ge(exp_done, n - 1)
                lo = kt * P if causal else 0
                dst = shifted_ps[i % 2]
                last = nc.tensor.matmul(dst[:, lo:T], k_stack[0:SHIFT + 3, h, kt * P:(kt + 1) * P], q_stack[0:SHIFT + 3, h, lo:T],
                                        start=True, stop=not causal)
                if causal:
                    last = nc.tensor.matmul(dst[:, lo:lo + P], k.cbf[:, 0, :], k.cbf[:, 2, :], start=False, stop=True)
                last.then_inc(shifted_ready, 1)

            def sum_tile(b, g, kt):
                u = b * TILES + g * NT + kt
                if kt == 0:
                    if g > 0 or not isinstance(b, int) or b > 0:
                        pe.wait_ge(o_taken, before(b, g))
                    if g == 0:
                        pe.wait_ge(v_stored, b + 1)
                pe.wait_ge(exp_done, (u + 1) * HG)

                def heads(lhs, rhs, lo, hi, m, start, stop):
                    for i in range(HG):
                        ins = nc.tensor.matmul(o_ps[32 * i:32 * i + m, lo:hi], lhs(i), rhs(i), start=start, stop=stop,
                                               skip_group_check=True, tile_position=(0, 32 * i))
                    return ins

                def values(i):
                    return v_aug[:, kt, HG * g + i, :]

                diag = kt * P
                if causal:
                    last = heads(values, lambda i: probs[:, kt, i, diag:T], diag, T, 32, kt == 0, kt == NT - 1)
                else:
                    last = heads(lambda i: k.c["den_col"], lambda i: probs[:, kt, i, 0:diag + P], 0, diag + P, 32, kt == 0, False)
                    if kt + 1 < NT:
                        last = heads(values, lambda i: probs[:, kt, i, diag + P:T], diag + P, T, 32, False, False)
                    pe.wait_ge(diag_masked, u + 1)
                    last = heads(lambda i: v_aug[:, kt, HG * g + i, 0:HD], lambda i: masked[:, kt, i, :], diag, diag + P, HD,
                                 False, kt == NT - 1)
                last.then_inc(summed, 1)

            def turn_max(b, g):
                pe.wait_ge(max_taken, b * UNITS + (g + 1) * HG * NT)
                if not (isinstance(b, int) and b == 0 and g <= 1):
                    pe.wait_ge(y_ready, before(b, g) - 1)
                nc.tensor.transpose(turn_ps[0:HG * NT, 0:P], mx[:, g % 2, :], k.c["ident"]).then_inc(max_turned, 1)

            def turn_sums(b, g):
                pe.wait_ge(o_taken, before(b, g) + 1)
                if isinstance(b, int) and b == B - 1 and g == NG - 1:
                    pe.wait_ge(y_ready, before(b, g))
                else:
                    pe.wait_ge(shift_ready, before(b, g) + 2)
                for t in range(NT):
                    last = nc.tensor.transpose(turn_ps[:, t * P:(t + 1) * P], o_sb[:, t * P:(t + 1) * P], k.c["ident"])
                last.then_inc(o_turned, 1)

            def turn_y(b):
                pe.wait_ge(y_ready, (b + 1) * GROUPS)
                if not (isinstance(b, int) and b == 0):
                    pe.wait_ge(proj_taken, (b + 1) * NPROJ)
                for t in range(NT):
                    last = nc.tensor.transpose(proj_ps[:, t * P:(t + 1) * P], y[:, t, :], k.c["ident"])
                last.then_inc(y_turned, 1)

            def project_out(b):
                pe.wait_ge(yT_ready, b + 1)
                for t in range(NT):
                    last = nc.tensor.matmul(proj_ps[:, t * P:(t + 1) * P], yT[:, t, :], k.w1[:, 5, :], start=True, stop=True)
                last.then_inc(out_ready, 1)

            def front(b, g, j):
                if (g, j) == (1, 1):
                    turn_norm(b, True)
                elif (g, j) == (1, 2):
                    project_qk(b, 0)
                    if causal:
                        project_qk(b, 1)
                elif (g, j) == (1, 3):
                    for which in range(NPROJ // 2, NPROJ):
                        project_qk(b, which)
                elif (g, j) == (2, 0):
                    project_v(b)

            def first(b):
                pe.wait_ge(init_done, 3)
                turn_norm(b, False)
                for which in range(NPROJ):
                    project_qk(b, which)
                project_v(b)
                for h in range(LEAD):
                    for qt in range(NT):
                        score(b, h, qt, h * NT + qt >= 2)
                turn_max(b, 0)

            def slot(b, g, prev, following):
                for j in range(NT):
                    warm = prev or j > 0
                    led = lead_head(b, g, j, following)

                    def lead(qt):
                        if led:
                            score(*led, qt, True)

                    shifted(b, g, j, 0, warm)
                    shifted(b, g, j, 1, warm)
                    lead(0)
                    shifted(b, g, j, 2, True)
                    lead(1)
                    shifted(b, g, j, 3, True)
                    if j > 0:
                        sum_tile(b, g, j - 1)
                    lead(2)
                    lead(3)
                    if prev and j == 1:
                        turn_sums(*((b, g - 1) if g else (b - 1, NG - 1)))
                    if j == 2 and lead_group(b, g, following):
                        turn_max(*lead_group(b, g, following))
                    if following:
                        front(b + 1, g, j)
                    if causal and prev and g == 0:
                        if j == 2:
                            turn_y(b - 1)
                        if j == 3:
                            project_out(b - 1)
                sum_tile(b, g, NT - 1)

            def finish(b):
                turn_sums(b, NG - 1)
                if causal:
                    turn_y(b)
                    project_out(b)

            run(pe, first, slot, finish)

        @block.scalar
        def _(act):
            def store_hT(b):
                lo = MOD_ROWS["attn"]
                act.wait_ge(norm.hn_transposed, b + 1)
                nc.scalar.activation(hT[:], proj_ps[:], ACT.Identity, bias=k.mod[layer][:, lo[0], bass.ds(b, 1)],
                                     scale=k.mod[layer][:, lo[1], bass.ds(b, 1)]).then_inc(hT_ready, 1)

            def high_part(b, side):
                if causal:
                    act.wait_ge(roped, b * 2 + side + 1)
                    nc.scalar.copy(parts[:, side, 0, :], turned[:, side, :]).then_inc(hi_ready, 1)
                else:
                    act.wait_ge(proj_ready, b * NPROJ + side + 1)
                    nc.scalar.copy(parts[:, side, 0, :], proj_ps[:]).then_inc(hi_ready, 1)

            def store_v(b):
                act.wait_ge(v_ready, b + 1)
                nc.scalar.copy(v_aug[:, :, :, 0:HD], v_ps[:].rearrange("p (t h d) -> p t h d", t=NT, h=H)).then_inc(v_stored, 1)

            def take_sums(b, g):
                act.wait_ge(summed, (before(b, g) + 1) * NT)
                nc.scalar.copy(o_sb[:], o_ps[:]).then_inc(o_taken, 1)

            def exponential(b, g, kt, i, warm):
                n = b * UNITS + g * HG * NT + kt * HG + i
                if i == 0 and warm:
                    act.wait_ge(summed, before(b, g) * NT + kt - NT + 1)
                act.wait_ge(shifted_ready, n + 1)
                lo = kt * P if causal else 0
                nc.scalar.activation(probs[:, kt, i, lo:T], shifted_ps[i % 2][:, lo:T], ACT.Exp,
                                     scale=SCALE).then_inc(exp_done, 1)

            def store_yT(b):
                act.wait_ge(y_turned, b + 1)
                nc.scalar.copy(yT[:], proj_ps[:].rearrange("p (t q) -> p t q", t=NT)).then_inc(yT_ready, 1)

            def first(b):
                store_hT(b)
                high_part(b, 0)
                high_part(b, 1)

            def slot(b, g, prev, following):
                if g == 0:
                    if prev:
                        take_sums(b - 1, NG - 1)
                    store_v(b)
                elif prev:
                    take_sums(b, g - 1)
                for j in range(NT):
                    for i in range(HG):
                        exponential(b, g, j, i, prev)
                    if following:
                        if (g, j) == (1, 1):
                            store_hT(b + 1)
                        if (g, j) == (1, 2):
                            high_part(b + 1, 0)
                        if (g, j) == (1, 3):
                            high_part(b + 1, 1)
                    if causal and prev and (g, j) == (0, 2):
                        store_yT(b - 1)

            def finish(b):
                take_sums(b, NG - 1)
                if causal:
                    store_yT(b)

            run(act, first, slot, finish)

        @block.vector
        def _(dve):
            def row_max(b, h, qt):
                dve.wait_ge(score_ready, b * UNITS + h * NT + qt + 1)
                cols = (qt + 1) * P if causal else T
                g, i = h // HG, h % HG
                nc.vector.tensor_reduce(mx[:, g % 2, i * NT + qt:i * NT + qt + 1], score_ps[qt % 2][:, 0:cols],
                                        AX.X, ALU.max).then_inc(max_taken, 1)

            def split_shift(b, g, prior):
                n = before(b, g)
                dve.wait_ge(max_turned, n + 1)
                if prior:
                    prior_b, prior_g = (b, g - 1) if g else (b - 1, NG - 1)
                    dve.wait_ge(shift_stacked[prior_g], (prior_b + 1) * 48)
                m = turn_ps[0:HG * NT, 0:P]
                nc.vector.tensor_scalar(shift[:, 0, :], m, -1.0, None, ALU.mult).then_inc(shift_hi, 1)
                dve.wait_ge(shift_hi, n + 1)
                nc.vector.scalar_tensor_tensor(shift_rest[:], m, -1.0, shift[:, 0, :], ALU.mult,
                                               ALU.subtract).then_inc(shift_left, 1)
                dve.wait_ge(shift_left, n + 1)
                nc.vector.tensor_copy(shift[:, 1, :], shift_rest[:]).then_inc(shift_mid, 1)
                dve.wait_ge(shift_mid, n + 1)
                nc.vector.tensor_tensor(shift[:, 2, :], shift_rest[:], shift[:, 1, :], ALU.subtract).then_inc(shift_ready, 1)

            def divide(b, g):
                n = before(b, g)
                dve.wait_ge(o_turned, n + 1)
                s = turn_ps[:].rearrange("p (t i r) -> p t i r", t=NT, i=HG)
                nc.vector.reciprocal(rden[:], s[:, :, :, HD]).then_inc(rden_ready, 1)
                dve.wait_ge(rden_ready, n + 1)
                nc.vector.tensor_tensor(y[:].rearrange("p t (h d) -> p t h d", h=H)[:, :, HG * g:HG * (g + 1), :], s[:, :, :, 0:HD],
                                        rden[:, :, :, None].to_broadcast([P, NT, HG, HD]), ALU.mult).then_inc(y_ready, 1)

            def what_is_left(b, side):
                n = b * 2 + side
                if causal:
                    dve.wait_ge(proj_ready, b * NPROJ + 2 * side + 1)
                    nc.vector.tensor_tensor(rope_a[:, side, :], proj_ps[:], k.c["cos"], ALU.mult).then_inc(proj_taken, 1)
                    dve.wait_ge(proj_ready, b * NPROJ + 2 * side + 2)
                    nc.vector.tensor_tensor(rope_b[:, side, :], proj_ps[:], k.c["sin"], ALU.mult).then_inc(proj_taken, 1)
                else:
                    dve.wait_ge(hi_ready, n + 1)
                    nc.vector.tensor_tensor(rest[:, side, :], proj_ps[:], parts[:, side, 0, :], ALU.subtract).then_inc(proj_taken, 1)

            def middle_part(b, side):
                n = b * 2 + side
                if causal:
                    dve.wait_ge(rest_ready, n + 1)
                else:
                    dve.wait_ge(proj_taken, n + 1)
                nc.vector.tensor_copy(parts[:, side, 1, :], rest[:, side, :]).then_inc(mid_ready, 1)

            def scale_out(b):
                dve.wait_ge(out_ready, b + 1)
                nc.vector.tensor_tensor(gy[:], proj_ps[:].rearrange("p (t d) -> p t d", t=NT),
                                        k.gate[layer][:, 0, bass.ds(b, 1), :].to_broadcast([P, NT, D]), ALU.mult).then_inc(gy_ready, 1)

            def first(b):
                nc.vector.memset(q_stack[64:96], 0.0).then_inc(init_done, 1)
                nc.vector.memset(k_stack[64:96], 1.0).then_inc(init_done, 1)
                norm.moments(dve, b)
                norm.normalise(dve, b)
                for side in range(2):
                    what_is_left(b, side)
                    middle_part(b, side)
                for h in range(LEAD):
                    for qt in range(NT):
                        row_max(b, h, qt)
                split_shift(b, 0, False)

            def slot(b, g, prev, following):
                for j in range(NT):
                    led = lead_head(b, g, j, following)
                    for qt in range(NT):
                        if led:
                            row_max(*led, qt)
                    if prev and j == 1:
                        divide(*((b, g - 1) if g else (b - 1, NG - 1)))
                    if j == 2 and lead_group(b, g, following):
                        split_shift(*lead_group(b, g, following), True)
                    if following and g == 1:
                        if j == 0:
                            norm.moments(dve, b + 1)
                            norm.normalise(dve, b + 1)
                        if j == 2:
                            what_is_left(b + 1, 0)
                            middle_part(b + 1, 0)
                        if j == 3:
                            what_is_left(b + 1, 1)
                            middle_part(b + 1, 1)
                    if prev and (g, j) == (0, 3):
                        if causal:
                            scale_out(b - 1)
                        else:
                            dve.wait_ge(gy_ready, b)

            def finish(b):
                divide(b, NG - 1)
                if causal:
                    dve.wait_ge(x_updated, b)
                    scale_out(b)

            run(dve, first, slot, finish)

        @block.gpsimd
        def _(pool):
            def mask_diagonal(b, g, kt):
                pool.wait_ge(exp_done, (b * TILES + g * NT + kt + 1) * HG)
                nc.gpsimd.tensor_tensor(masked[:, kt], probs[:, kt, :, kt * P:(kt + 1) * P],
                                        k.c["causal_t"][:, None, :].to_broadcast([P, HG, P]), ALU.mult).then_inc(diag_masked, 1)

            def low_part(b, side):
                n = b * 2 + side
                pool.wait_ge(mid_ready, n + 1)
                nc.gpsimd.tensor_tensor(parts[:, side, 2, :], rest[:, side, :], parts[:, side, 1, :], ALU.subtract).then_inc(lo_ready, 1)

            def rope_sum(b, side):
                n = b * 2 + side
                pool.wait_ge(proj_taken, b * NPROJ + 2 * side + 2)
                nc.gpsimd.tensor_tensor(turned[:, side, :], rope_a[:, side, :], rope_b[:, side, :], ALU.add).then_inc(roped, 1)
                pool.wait_ge(hi_ready, n + 1)
                nc.gpsimd.tensor_tensor(rest[:, side, :], turned[:, side, :], parts[:, side, 0, :], ALU.subtract).then_inc(rest_ready, 1)

            def update_x(b):
                xb = k.x[:, bass.ds(b * NT, NT), :]
                if not causal:
                    pool.wait_ge(y_ready, (b + 1) * GROUPS)
                    nc.gpsimd.tensor_tensor(gy[:], y[:], k.gate[layer][:, 0, bass.ds(b, 1), :].to_broadcast([P, NT, D]),
                                            ALU.mult).then_inc(gy_ready, 1)
                pool.wait_ge(gy_ready, b + 1)
                nc.gpsimd.tensor_tensor(xb, xb, gy[:], ALU.add).then_inc(x_updated, 1)

            def split_sides(b, side):
                if causal:
                    rope_sum(b, side)
                low_part(b, side)

            def first(b):
                nc.gpsimd.tensor_copy(v_aug[:].rearrange("p t h r -> p (t h) r"),
                                      k.c["den_col"][:, None, :].to_broadcast([P, NT * H, 32])).then_inc(init_done, 1)
                norm.inverse_deviation(pool, b)
                split_sides(b, 0)
                split_sides(b, 1)

            def slot(b, g, prev, following):
                for j in range(NT):
                    if not causal:
                        mask_diagonal(b, g, j)
                    if following and g == 1:
                        if j == 0:
                            norm.inverse_deviation(pool, b + 1)
                        if j == 2:
                            split_sides(b + 1, 0)
                        if j == 3:
                            split_sides(b + 1, 1)
                    if prev and (g, j) == (0, 1) and not causal:
                        update_x(b - 1)
                    if prev and (g, j) == (0, 3) and causal:
                        update_x(b - 1)

            run(pool, first, slot, update_x)


def experts_phase(k):
    nc = k.nc
    LAG, STEPS = 2, E * FT
    ROUTER_STEPS = 14
    with ExitStack() as ctx:
        def sb(name, shape, dt=F32):
            return k.sb(f"ex_{name}", shape, dt, ctx)

        def sem(name):
            return ctx.enter_context(nc.semaphore(f"ex_{name}"))

        def bank(name):
            return ctx.enter_context(nc.psum_tensor(f"ex_{name}", [P, 512], F32))

        gate_ps = [bank(f"gate{i}") for i in range(2)]
        up_ps = [bank(f"up{i}") for i in range(2)]
        down_ps = [bank(f"down{i}") for i in range(2)]
        norm_ps = bank("norm")
        logit_ps = bank("logit")

        raw = sb("w_raw", [P, 3, STEPS, D])
        w_t = sb("w_t", [P, 3, STEPS, D])
        hT = sb("hT", [P, T])
        th = sb("tanh", [P, 2, T])
        half = sb("half", [P, 2, T])
        hid = sb("hid", [P, 4, T])
        acc = sb("acc", [P, NT, D])
        shifted = sb("shifted", [P, NT, E])
        prob = sb("prob", [P, NT, E])
        top = sb("top", [P, NT])
        total = sb("total", [P, NT])
        above = sb("above", [P, NT, E, E])
        tied = sb("tied", [P, NT, E, E])
        rank = sb("rank", [P, NT, E])
        weight = sb("weight", [P, NT, E])
        norm = Norm(k, ctx, "ex")

        w_loaded = [sem(f"w_loaded{i}") for i in range(3)]
        w_turned = sem("w_turned")
        w_stored = [sem(f"w_stored{i}") for i in range(2)]
        hT_ready = sem("hT_ready")
        logits_ready = sem("logits_ready")
        exps_ready = sem("exps_ready")
        router_step = sem("router_step")
        gate_ready = sem("gate_ready")
        up_ready = sem("up_ready")
        tanh_ready = sem("tanh_ready")
        silu_ready = sem("silu_ready")
        hid_ready = sem("hid_ready")
        down_done = sem("down_done")
        combined = sem("combined")
        gated = sem("gated")
        x_updated = sem("x_updated")

        QUADS = 3 * STEPS // 4
        banks = gate_ps + up_ps

        def run(engine, body):
            body(0, True, True)
            with engine.Fori(1, B - 1) as b:
                body(b, False, True)
            body(B - 1, False, False)

        block = ctx.enter_context(nc.Block())

        @block.sync
        def _(sp):
            for i, name in enumerate(("gate", "up")):
                sp.dma_start(raw[:, i], k.a[f"L0_ffn_W_{name}"].rearrange("e (f p) d -> p (e f) d", p=P)).then_inc(w_loaded[i], 16)
            sp.dma_start(raw[:, 2].rearrange("p (e f) c -> p e (f c)", e=E),
                         k.a["L0_ffn_W_down"].rearrange("e d f -> d e f")).then_inc(w_loaded[2], 16)

        @block.tensor
        def _(pe):
            for q in range(QUADS):
                which, step = divmod(q * 4, STEPS)
                if step == 0:
                    pe.wait_ge(w_loaded[which], 16)
                if q >= 4:
                    pe.wait_ge(w_stored[q % 2], (q - 4) // 2 + 1)
                for i in range(4):
                    last = nc.tensor.transpose(banks[q % 4][:, i * P:(i + 1) * P], raw[:, which, step + i, :], k.c["ident"])
                last.then_inc(w_turned, 1)
            for i in range(2):
                pe.wait_ge(w_stored[i], QUADS // 2)

            def gate_up(b, n, warm):
                if warm:
                    pe.wait_ge(silu_ready, b * STEPS + n - 1)
                nc.tensor.matmul(gate_ps[n % 2][:], w_t[:, 0, n, :], hT[:], start=True, stop=True).then_inc(gate_ready, 1)
                if warm:
                    pe.wait_ge(hid_ready, b * STEPS + n - 1)
                nc.tensor.matmul(up_ps[n % 2][:], w_t[:, 1, n, :], hT[:], start=True, stop=True).then_inc(up_ready, 1)

            def down(b, n, warm):
                e, f = divmod(n, FT)
                if f == 0 and warm:
                    pe.wait_ge(combined, b * E + e - 1)
                pe.wait_ge(hid_ready, b * STEPS + n + 1)
                for t in range(NT):
                    last = nc.tensor.matmul(down_ps[e % 2][:, t * P:(t + 1) * P], hid[:, n % 4, t * P:(t + 1) * P], w_t[:, 2, n, :],
                                            start=(f == 0 and t == 0), stop=(f == FT - 1), skip_group_check=True)
                last.then_inc(down_done, 1)

            def body(b, first, following):
                if first:
                    norm.transpose(pe, b, norm_ps)
                pe.wait_ge(hT_ready, b + 1)
                for t in range(NT):
                    last = nc.tensor.matmul(logit_ps[:, t * E:(t + 1) * E], hT[:, t * P:(t + 1) * P], k.router[:], start=True, stop=True)
                last.then_inc(logits_ready, 1)
                for n in range(STEPS):
                    gate_up(b, n, not first or n >= 2)
                    if n >= LAG:
                        down(b, n - LAG, not first or n - LAG >= 2 * FT)
                    if n == STEPS // 2 and following:
                        norm.transpose(pe, b + 1, norm_ps)
                for n in range(STEPS - LAG, STEPS):
                    down(b, n, True)

            run(pe, body)

        @block.scalar
        def _(act):
            for q in range(1, QUADS, 2):
                which, step = divmod(q * 4, STEPS)
                act.wait_ge(w_turned, q + 1)
                nc.scalar.copy(w_t[:, which, step:step + 4, :], banks[q % 4][:].rearrange("p (i c) -> p i c", i=4)).then_inc(w_stored[1], 1)

            def body(b, first, following):
                act.wait_ge(norm.hn_transposed, b + 1)
                if not first:
                    act.wait_ge(up_ready, b * STEPS)
                lo = MOD_ROWS["ffn"]
                nc.scalar.activation(hT[:], norm_ps[:], ACT.Identity, bias=k.mod[0][:, lo[0], bass.ds(b, 1)],
                                     scale=k.mod[0][:, lo[1], bass.ds(b, 1)]).then_inc(hT_ready, 1)
                for n in range(STEPS):
                    act.wait_ge(gate_ready, b * STEPS + n + 1)
                    nc.scalar.activation(th[:, n % 2, :], gate_ps[n % 2][:], ACT.Tanh, scale=0.5).then_inc(tanh_ready, 1)
                    if n == 1:
                        act.wait_ge(router_step, b * ROUTER_STEPS + 2)
                        nc.scalar.activation(prob[:], shifted[:], ACT.Exp).then_inc(exps_ready, 1)

            run(act, body)

        @block.vector
        def _(dve):
            for q in range(0, QUADS, 2):
                which, step = divmod(q * 4, STEPS)
                dve.wait_ge(w_turned, q + 1)
                nc.vector.tensor_copy(w_t[:, which, step:step + 4, :], banks[q % 4][:].rearrange("p (i c) -> p i c", i=4)).then_inc(w_stored[0], 1)

            def silu_times_up(b, n, warm):
                dve.wait_ge(tanh_ready, b * STEPS + n + 1)
                nc.vector.scalar_tensor_tensor(half[:, n % 2, :], th[:, n % 2, :], 1.0, gate_ps[n % 2][:], ALU.add,
                                               ALU.mult).then_inc(silu_ready, 1)
                dve.wait_ge(silu_ready, b * STEPS + n + 1)
                dve.wait_ge(up_ready, b * STEPS + n + 1)
                if warm:
                    dve.wait_ge(down_done, b * STEPS + n - 3)
                nc.vector.tensor_tensor(hid[:, n % 4, :], half[:, n % 2, :], up_ps[n % 2][:], ALU.mult).then_inc(hid_ready, 1)

            def route(b, part):
                count = [0 if part == 0 else 2]

                def link(ins):
                    count[0] += 1
                    ins.then_inc(router_step, 1)
                    dve.wait_ge(router_step, b * ROUTER_STEPS + count[0])

                each = [P, NT, E]
                pairs = [P, NT, E, E]
                logits = logit_ps[:, 0:NT * E].rearrange("p (t e) -> p t e", t=NT)
                if part == 0:
                    dve.wait_ge(logits_ready, b + 1)
                    link(nc.vector.tensor_reduce(top[:], logits, AX.X, ALU.max))
                    link(nc.vector.tensor_tensor(shifted[:], logits, top[:, :, None].to_broadcast(each), ALU.subtract))
                    return
                dve.wait_ge(exps_ready, b + 1)
                link(nc.vector.tensor_reduce(total[:], prob[:], AX.X, ALU.add))
                link(nc.vector.reciprocal(total[:], total[:]))
                link(nc.vector.tensor_tensor(prob[:], prob[:], total[:, :, None].to_broadcast(each), ALU.mult))
                other = prob[:, :, None, :].to_broadcast(pairs)
                own = prob[:, :, :, None].to_broadcast(pairs)
                link(nc.vector.tensor_tensor(above[:], other, own, ALU.is_gt))
                link(nc.vector.tensor_tensor(tied[:], other, own, ALU.is_equal))
                link(nc.vector.tensor_tensor(tied[:], tied[:], k.c["before"].rearrange("p (e j) -> p e j", e=E)[:, None, :, :].to_broadcast(pairs),
                                             ALU.mult))
                link(nc.vector.tensor_tensor(above[:], above[:], tied[:], ALU.add))
                link(nc.vector.tensor_reduce(rank[:], above[:], AX.X, ALU.add))
                link(nc.vector.scalar_tensor_tensor(rank[:], rank[:], 2.0, prob[:], ALU.is_lt, ALU.mult))
                link(nc.vector.tensor_reduce(total[:], rank[:], AX.X, ALU.add))
                link(nc.vector.reciprocal(total[:], total[:]))
                link(nc.vector.scalar_tensor_tensor(weight[:], rank[:], 0.5, total[:, :, None].to_broadcast(each), ALU.mult, ALU.mult))

            def combine(b, e, first):
                dve.wait_ge(down_done, b * STEPS + (e + 1) * FT)
                if e == 0 and not first:
                    dve.wait_ge(x_updated, b)
                if e > 0:
                    dve.wait_ge(combined, b * E + e)
                for t in range(NT):
                    y = down_ps[e % 2][:, t * P:(t + 1) * P]
                    w = weight[:, t, e:e + 1]
                    if e == 0:
                        last = nc.vector.tensor_scalar(acc[:, t, :], y, w, None, ALU.mult)
                    else:
                        last = nc.vector.scalar_tensor_tensor(acc[:, t, :], y, w, acc[:, t, :], ALU.mult, ALU.add)
                last.then_inc(combined, 1)

            def body(b, first, following):
                if first:
                    norm.moments(dve, b)
                    norm.normalise(dve, b)
                route(b, 0)
                for n in range(STEPS):
                    silu_times_up(b, n, not first or n >= 4)
                    if n == 3:
                        route(b, 1)
                    if n >= 6 and (n - 6) % FT == 0:
                        combine(b, (n - 6) // FT, first)
                    if following and n == 8:
                        norm.moments(dve, b + 1)
                    if following and n == 12:
                        norm.normalise(dve, b + 1)
                combine(b, E - 1, first)

            run(dve, body)

        @block.gpsimd
        def _(pool):
            def body(b, first, following):
                if first:
                    norm.inverse_deviation(pool, b)
                if following:
                    norm.inverse_deviation(pool, b + 1)
                xb = k.x[:, bass.ds(b * NT, NT), :]
                pool.wait_ge(combined, (b + 1) * E)
                nc.gpsimd.tensor_tensor(acc[:], acc[:], k.gate[0][:, 1, bass.ds(b, 1), :].to_broadcast([P, NT, D]),
                                        ALU.mult).then_inc(gated, 1)
                pool.wait_ge(gated, b + 1)
                nc.gpsimd.tensor_tensor(xb, xb, acc[:], ALU.add).then_inc(x_updated, 1)

            run(pool, body)


def units_phase(k):
    nc = k.nc
    LAG = 2
    with ExitStack() as ctx:
        def sb(name, shape, dt=F32):
            return k.sb(f"un_{name}", shape, dt, ctx)

        def sem(name):
            return ctx.enter_context(nc.semaphore(f"un_{name}"))

        def bank(name):
            return ctx.enter_context(nc.psum_tensor(f"un_{name}", [P, 512], F32))

        unit_ps = [bank(f"unit{i}") for i in range(3)]
        out_ps = bank("out")
        norm_ps = bank("norm")
        hT = sb("hT", [P, T])
        relu = sb("relu", [P, 4, T])
        biased = sb("biased", [P, NT, D])
        norm = Norm(k, ctx, "un")
        hT_ready = sem("hT_ready")
        unit_ready = sem("unit_ready")
        relu_ready = sem("relu_ready")
        out_added = sem("out_added")
        biased_ready = sem("biased_ready")
        gated = sem("gated")
        x_updated = sem("x_updated")
        x_stored = sem("x_stored")

        def run(engine, body):
            body(0, True, True)
            with engine.Fori(1, B - 1) as b:
                body(b, False, True)
            body(B - 1, False, False)

        block = ctx.enter_context(nc.Block())

        @block.sync
        def _(sp):
            def body(b, first, following):
                sp.wait_ge(x_updated, b + 1)
                sp.dma_start(k.out[bass.ds(b, 1)].rearrange("b (t p) d -> p (b t) d", p=P),
                             k.x[:, bass.ds(b * NT, NT), :]).then_inc(x_stored, 16)

            run(sp, body)
            sp.wait_ge(x_stored, 16 * B)

        @block.tensor
        def _(pe):
            win = k.win_rep[:].rearrange("p m h -> p (m h)")

            def unit(b, j):
                i = j % 2
                pe.wait_ge(relu_ready, b * NJ + j - 1)
                nc.tensor.matmul(unit_ps[i][:], win[:, j * P:(j + 1) * P], hT[:], start=True, stop=True).then_inc(unit_ready, 1)

            def add_out(b, j, first):
                pe.wait_ge(relu_ready, b * NJ + j + 1)
                if j == 0 and not first:
                    pe.wait_ge(biased_ready, b)
                for t in range(NT):
                    last = nc.tensor.matmul(out_ps[:, t * P:(t + 1) * P], relu[:, j % 4, t * P:(t + 1) * P], k.wout_rep[:, j, :],
                                            start=(j == 0 and t == 0), stop=(j == NJ - 1), skip_group_check=True)
                last.then_inc(out_added, 1)

            def body(b, first, following):
                if first:
                    norm.transpose(pe, b, norm_ps)
                pe.wait_ge(hT_ready, b + 1)
                for j in range(NJ):
                    if first and j < 2:
                        nc.tensor.matmul(unit_ps[j % 2][:], win[:, j * P:(j + 1) * P], hT[:], start=True, stop=True).then_inc(unit_ready, 1)
                    else:
                        unit(b, j)
                    if j >= LAG:
                        add_out(b, j - LAG, first)
                    if following and j == NJ // 2:
                        norm.transpose(pe, b + 1, norm_ps)
                for j in range(NJ - LAG, NJ):
                    add_out(b, j, first)

            run(pe, body)

        @block.scalar
        def _(act):
            def body(b, first, following):
                act.wait_ge(norm.hn_transposed, b + 1)
                if not first:
                    act.wait_ge(unit_ready, b * NJ)
                lo = MOD_ROWS["ffn"]
                nc.scalar.activation(hT[:], norm_ps[:], ACT.Identity, bias=k.mod[1][:, lo[0], bass.ds(b, 1)],
                                     scale=k.mod[1][:, lo[1], bass.ds(b, 1)]).then_inc(hT_ready, 1)
                for j in range(NJ):
                    if not (first and j < 4):
                        act.wait_ge(out_added, b * NJ + j - 3)
                    act.wait_ge(unit_ready, b * NJ + j + 1)
                    nc.scalar.activation(relu[:, j % 4, :], unit_ps[j % 2][:], ACT.Relu, bias=k.b1c[:, j:j + 1],
                                         scale=k.w1c[:, j:j + 1]).then_inc(relu_ready, 1)

            run(act, body)

        @block.vector
        def _(dve):
            def body(b, first, following):
                if first:
                    norm.moments(dve, b)
                    norm.normalise(dve, b)
                if following:
                    norm.moments(dve, b + 1)
                    norm.normalise(dve, b + 1)
                every = [P, NT, D]
                xb = k.x[:, bass.ds(b * NT, NT), :]
                if not following:
                    dve.wait_ge(x_updated, b)
                dve.wait_ge(out_added, (b + 1) * NJ)
                nc.vector.tensor_tensor(biased[:], out_ps[:].rearrange("p (t d) -> p t d", t=NT), k.bout[:, None, :].to_broadcast(every),
                                        ALU.add).then_inc(biased_ready, 1)
                dve.wait_ge(biased_ready, b + 1)
                nc.vector.tensor_tensor(biased[:], biased[:], k.gate[1][:, 1, bass.ds(b, 1), :].to_broadcast(every),
                                        ALU.mult).then_inc(gated, 1)
                dve.wait_ge(gated, b + 1)
                nc.vector.tensor_tensor(xb, xb, biased[:], ALU.add).then_inc(x_updated, 1)

            run(dve, body)

        @block.gpsimd
        def _(pool):
            def body(b, first, following):
                if first:
                    norm.inverse_deviation(pool, b)
                if following:
                    norm.inverse_deviation(pool, b + 1)

            run(pool, body)


_INS = ["L0_attn_content", "L0_attn_Wq", "L0_attn_Wk", "L0_attn_Wv", "L0_ffn_W_router", "L0_ffn_W_gate", "L0_ffn_W_up",
        "L0_ffn_W_down", "L0_c", "L0_wmod", "L1_attn_W_Q", "L1_attn_W_K", "L1_attn_W_V", "L1_attn_W_O", "L1_ffn_Win",
        "L1_ffn_bin_", "L1_ffn_W1", "L1_ffn_b1", "L1_ffn_W2", "L1_ffn_b2", "L1_ffn_Wout", "L1_ffn_bout", "L1_c", "L1_wmod"]


def kernel(**inputs):
    import concourse.bacc as bacc
    from concourse.bass_utils import run_bass_kernel_spmd

    nc = bacc.Bacc("TRN2", target_bir_lowering=False, num_devices=1)
    packed, off, bf = constants()
    arrays = {f"in_{n}": np.ascontiguousarray(inputs[n]) for n in _INS}
    arrays["in_const_f32"], arrays["in_const_bf16"] = packed, bf
    aps = {n[3:]: nc.dram_tensor(n, v.shape, mybir.dt.from_np(v.dtype), kind="ExternalInput").ap() for n, v in arrays.items()}
    out = nc.dram_tensor("out_x", (B, T, D), F32, kind="ExternalOutput").ap()
    adaln_kernel(nc, aps, out, off)
    r = run_bass_kernel_spmd(nc, [arrays], core_ids=[0])
    return r.results[0]["out_x"]
```

```python
from contextlib import ExitStack, contextmanager

import numpy as np

import concourse.bass as bass
from concourse import mybir

F32 = mybir.dt.float32
BF16 = mybir.dt.bfloat16
F16 = mybir.dt.float16
ALU = mybir.AluOpType
ACT = mybir.ActivationFunctionType
AX = mybir.AxisListType

P = 128
B, T, D = 8, 512, 128
NT = T // P
H = 16
HD = D // H
HG = 4
NG = H // HG
E, F = 8, 512
FT = F // P
M, INNER = 64, 16
NJ = M * INNER // P
EPS = 1e-5
GATE_MIN = 0.25
MASKED = -1e30
SCALE = float(HD) ** -0.5
ROWS = 9 * HD
SHIFT = ROWS
LEAD = 7
MODS = 6
NORM1, NORM2 = (0, 1, 2), (3, 4, 5)


def constants():
    f32 = {}
    f32["ident"] = np.eye(P, dtype=np.float32)
    perm = np.zeros((P, P), np.float32)
    rot = np.zeros((P, P), np.float32)
    half = HD // 2
    for h in range(H):
        for d in range(HD):
            perm[h * HD + d, d * H + h] = 1.0
            if d < half:
                rot[h * HD + d + half, d * H + h] = -1.0
            else:
                rot[h * HD + d - half, d * H + h] = 1.0
    f32["perm"], f32["rot"] = perm, rot
    theta = (np.float32(1.0) / np.float32(10000.0) ** (np.arange(0, HD, 2, dtype=np.float32) / np.float32(HD))).astype(np.float32)
    angle = np.outer(np.arange(T, dtype=np.float32), theta).astype(np.float32)
    angle = np.concatenate([angle, angle], axis=-1)
    f32["cos"] = np.repeat(np.cos(angle).T.astype(np.float32), H, axis=0)
    f32["sin"] = np.repeat(np.sin(angle).T.astype(np.float32), H, axis=0)
    den = np.zeros((P, 32), np.float32)
    den[:, HD] = 1.0
    f32["den_col"] = den
    before = (np.arange(E)[None, :] < np.arange(E)[:, None]).astype(np.float32)
    f32["before"] = np.broadcast_to(before.reshape(1, -1), (P, E * E))
    k = np.arange(P)
    f32["causal_t"] = (k[:, None] <= k[None, :]).astype(np.float32)
    unit = np.zeros((P, NJ * P), np.float32)
    unit[(np.arange(NJ * P) // INNER), np.arange(NJ * P)] = 1.0
    f32["unit_of"] = unit
    off, cols = {}, 0
    for name, a in f32.items():
        off[name] = (cols, a.shape[1])
        cols += a.shape[1]
    packed = np.ascontiguousarray(np.concatenate(list(f32.values()), axis=1), dtype=np.float32)
    later = k[None, :] > k[:, None]
    bf = np.concatenate([np.eye(P), np.where(later, MASKED, 0.0), np.where(later.T, MASKED, 0.0)], axis=1)
    return packed, off, bf.astype(mybir.dt.np(BF16))


def adaln_kernel(nc, a, out, const_off):
    with ExitStack() as ctx:
        k = Kernel(nc, ctx, a, out, const_off)
        setup_phase(k)
        attention_phase(k, 0)
        experts_phase(k)
        attention_phase(k, 1)
        units_phase(k)


class Kernel:

    def __init__(self, nc, ctx, a, out, const_off):
        self.nc, self.ctx, self.a, self.out = nc, ctx, a, out
        self.x = self.sb("x_res", [P, B * NT, D], F32)
        width = sum(w for _, w in const_off.values())
        self.const = self.sb("consts", [P, width], F32)
        self.c = {n: self.const[:, o:o + w] for n, (o, w) in const_off.items()}
        self.cbf = self.sb("consts_bf16", [P, 3, P], BF16)
        self.eps = self.sb("eps", [P, NT], F32)
        self.minus_half = self.sb("minus_half", [P, NT], F32)
        self.mod = [self.sb(f"mod{l}", [P, 4, B], F32) for l in range(2)]
        self.gate = [self.sb(f"gate{l}", [P, 2, B, D], F32) for l in range(2)]
        self.w_qkv0 = self.sb("w_qkv0", [P, 3, D], F32)
        self.w_qk0 = self.sb("w_qk0", [P, 2, D], F32)
        self.w1 = self.sb("w1_proj", [P, 6, D], F32)
        self.router = self.sb("router_t", [P, E], F32)
        self.win_rep = self.sb("win_rep", [P, M, INNER], F32)
        self.w1c = self.sb("w1_col", [P, NJ], F32)
        self.b1c = self.sb("b1_col", [P, NJ], F32)
        self.wout_rep = self.sb("wout_rep", [P, NJ, D], F32)
        self.bout = self.sb("bout_all", [P, D], F32)

    def sb(self, name, shape, dt, ctx=None):
        return (ctx or self.ctx).enter_context(self.nc.sbuf_tensor(name, shape, dt))


MOD_ROWS = {"attn": (0, 1), "ffn": (2, 3)}


def setup_phase(k):
    nc, a = k.nc, k.a
    with ExitStack() as ctx:
        def sb(name, shape, dt=F32):
            return k.sb(name, shape, dt, ctx)

        def sem(name):
            return ctx.enter_context(nc.semaphore(name))

        ps = [ctx.enter_context(nc.psum_tensor(f"su_ps{i}", [P, 512], F32)) for i in range(4)]
        c_raw = sb("c_raw", [B, 2, D])
        wmod = sb("wmod", [P, 2, MODS * D])
        c_t = sb("c_t", [P, 2, B])
        c_e = sb("c_e", [P, 2, B])
        c_silu = sb("c_silu", [P, 2, B])
        c_all = sb("c_all", [P, 2, B, P])
        g_sign = sb("g_sign", [P, 2 * B * D])
        g_abs = sb("g_abs", [P, 2 * B * D])
        w_raw = sb("w_raw", [P, 4, D])
        router_raw = sb("router_raw", [E, D])
        win_raw = sb("win_raw", [P, M])
        wout_raw = sb("wout_raw", [M, D + 1])
        b2_raw = sb("b2_raw", [M, 1])
        unit_raw = sb("unit_raw", [NJ, 3, P])
        unit_col = sb("unit_col", [P, 3, NJ])
        bout_raw = sb("bout_raw", [P, D])

        s_const, s_c, s_wmod, s_x, s_w, s_kan = (sem(n) for n in ("su_const", "su_c", "su_wmod", "su_x", "su_w", "su_kan"))
        pe_done, dve_done, act_done, pool_done = (sem(n) for n in ("su_pe", "su_dve", "su_act", "su_pool"))

        with nc.Block() as block:
            @block.sync
            def _(sp):
                sp.dma_start(c_raw[:, 0, :], a["L0_c"]).then_inc(s_c, 16)
                sp.dma_start(c_raw[:, 1, :], a["L1_c"]).then_inc(s_c, 16)
                sp.dma_start(k.const[:], a["const_f32"]).then_inc(s_const, 16)
                sp.dma_start(wmod[:, 0, :], a["L0_wmod"]).then_inc(s_wmod, 16)
                sp.dma_start(wmod[:, 1, :], a["L1_wmod"]).then_inc(s_wmod, 16)
                for i, n in enumerate(("Q", "K", "V", "O")):
                    sp.dma_start(w_raw[:, i, :], a[f"L1_attn_W_{n}"]).then_inc(s_w, 16)
                sp.dma_start(router_raw[:], a["L0_ffn_W_router"]).then_inc(s_w, 16)
                for i, n in enumerate("qkv"):
                    sp.dma_start(k.w_qkv0[:, i, :], a[f"L0_attn_W{n}"]).then_inc(s_w, 16)
                sp.dma_start(k.cbf[:], a["const_bf16"].rearrange("p (i c) -> p i c", i=3)).then_inc(s_const, 16)
                sp.dma_start(k.x[:], a["L0_attn_content"].rearrange("b (t p) d -> p (b t) d", p=P)).then_inc(s_x, 16)
                sp.wait_ge(s_x, 16)

            @block.scalar
            def _(act):
                act.dma_start(win_raw[:], a["L1_ffn_Win"]).then_inc(s_kan, 16)
                act.dma_start(wout_raw[:, 0:D], a["L1_ffn_Wout"]).then_inc(s_kan, 16)
                act.dma_start(wout_raw[:, D:D + 1], a["L1_ffn_bin_"].rearrange("(m o) -> m o", o=1)).then_inc(s_kan, 16)
                act.dma_start(b2_raw[:], a["L1_ffn_b2"].rearrange("(m o) -> m o", o=1)).then_inc(s_kan, 16)
                for i, n in enumerate(("W1", "b1", "W2")):
                    act.dma_start(unit_raw[:, i, :], a[f"L1_ffn_{n}"].rearrange("(j a) h -> j (a h)", j=NJ)).then_inc(s_kan, 16)
                act.dma_start(bout_raw[:], a["L1_ffn_bout"].partition_broadcast(P)).then_inc(s_kan, 16)
                act.wait_ge(dve_done, 1)
                nc.scalar.activation(c_e[:], c_t[:], ACT.Exp, scale=-1.0).then_inc(act_done, 1)

            @block.gpsimd
            def _(pool):
                nc.gpsimd.memset(k.eps[:], EPS)
                nc.gpsimd.memset(k.minus_half[:], -0.5).then_inc(pool_done, 1)
                pool.wait_ge(s_kan, 128)
                nc.gpsimd.tensor_copy(k.win_rep[:], win_raw[:, :, None].to_broadcast([P, M, INNER])).then_inc(pool_done, 1)

            @block.tensor
            def _(pe):
                pe.wait_ge(s_const, 32)
                pe.wait_ge(s_c, 32)
                for l in range(2):
                    last = nc.tensor.transpose(ps[0][:, l * B:(l + 1) * B], c_raw[:, l, :], k.c["ident"][0:B, 0:B])
                last.then_inc(pe_done, 1)
                pe.wait_ge(s_w, 128)
                for n, (i, m) in enumerate(((0, "perm"), (0, "rot"), (1, "perm"), (1, "rot"))):
                    last = nc.tensor.matmul(ps[1][:, n * D:(n + 1) * D], w_raw[:, i, :], k.c[m], start=True, stop=True)
                last.then_inc(pe_done, 1)
                for n, i in enumerate((2, 3)):
                    nc.tensor.transpose(ps[2][:, n * D:(n + 1) * D], w_raw[:, i, :], k.c["ident"])
                nc.tensor.transpose(ps[2][:, 2 * D:2 * D + E], router_raw[:], k.c["ident"][0:E, 0:E])
                pe.wait_ge(s_kan, 128)
                for i in range(3):
                    last = nc.tensor.transpose(ps[2][:, 2 * D + E + i * NJ:2 * D + E + (i + 1) * NJ], unit_raw[:, i, :],
                                               k.c["ident"][0:NJ, 0:NJ])
                last.then_inc(pe_done, 1)
                for j in range(NJ):
                    if j >= 2:
                        pe.wait_ge(dve_done, 7 + 2 * (j - 2))
                    else:
                        pe.wait_ge(dve_done, 5)
                    nc.tensor.matmul(ps[1 + j % 2][:, 0:D + 1], k.c["unit_of"][0:M, j * P:(j + 1) * P], wout_raw[:],
                                     start=True, stop=True).then_inc(pe_done, 1)
                nc.tensor.matmul(ps[3][:, 0:D], b2_raw[:, 0:1].to_broadcast([M, P]), wout_raw[:, 0:D],
                                 start=True, stop=True).then_inc(pe_done, 1)
                pe.wait_ge(dve_done, 26)
                pe.wait_ge(s_wmod, 32)
                for l in range(2):
                    for n, j in enumerate((0, 1, 3, 4)):
                        last = nc.tensor.matmul(ps[0][:, (l * 4 + n) * B:(l * 4 + n + 1) * B], wmod[:, l, j * D:(j + 1) * D],
                                                c_silu[:, l, :], start=True, stop=True)
                last.then_inc(pe_done, 1)
                n = 0
                for l in range(2):
                    for gi, j in enumerate((2, 5)):
                        for hb in range(2):
                            pe.wait_ge(dve_done, 27 if n < 2 else 30 + n)
                            for q in range(4):
                                b = hb * 4 + q
                                last = nc.tensor.matmul(ps[1 + n % 2][:, q * D:(q + 1) * D], c_all[:, l, b, :],
                                                        wmod[:, l, j * D:(j + 1) * D], start=True, stop=True)
                            last.then_inc(pe_done, 1)
                            n += 1

            @block.vector
            def _(dve):
                n = [0]

                def link(ins):
                    n[0] += 1
                    ins.then_inc(dve_done, 1)
                    dve.wait_ge(dve_done, n[0])

                dve.wait_ge(pe_done, 1)
                link(nc.vector.tensor_copy(c_t[:], ps[0][:, 0:2 * B].rearrange("p (l b) -> p l b", l=2)))
                dve.wait_ge(pe_done, 3)
                link(nc.vector.tensor_copy(k.w1[:, 0:4, :], ps[1][:].rearrange("p (i d) -> p i d", i=4)))
                link(nc.vector.tensor_copy(k.w1[:, 4:6, :], ps[2][:, 0:2 * D].rearrange("p (i d) -> p i d", i=2)))
                link(nc.vector.tensor_copy(k.router[:], ps[2][:, 2 * D:2 * D + E]))
                link(nc.vector.tensor_copy(unit_col[:], ps[2][:, 2 * D + E:2 * D + E + 3 * NJ].rearrange("p (i j) -> p i j", i=3)))
                for j in range(NJ):
                    dve.wait_ge(pe_done, 4 + j)
                    pj = ps[1 + j % 2]
                    link(nc.vector.tensor_scalar(k.b1c[:, j:j + 1], pj[:, D:D + 1], unit_col[:, 0, j:j + 1], unit_col[:, 1, j:j + 1],
                                                 ALU.mult, ALU.add))
                    link(nc.vector.tensor_scalar(k.wout_rep[:, j, :], pj[:, 0:D], unit_col[:, 2, j:j + 1], None, ALU.mult))
                dve.wait_ge(pe_done, 4 + NJ)
                dve.wait_ge(s_kan, 128)
                link(nc.vector.tensor_copy(k.w1c[:], unit_col[:, 0, :]))
                link(nc.vector.tensor_tensor(k.bout[:], ps[3][:, 0:D], bout_raw[:], ALU.add))
                dve.wait_ge(act_done, 1)
                link(nc.vector.tensor_scalar(c_e[:], c_e[:], 1.0, None, ALU.add))
                link(nc.vector.reciprocal(c_e[:], c_e[:]))
                link(nc.vector.tensor_tensor(c_silu[:], c_t[:], c_e[:], ALU.mult))
                link(nc.vector.tensor_copy(c_all[:], c_silu[:, :, :, None].to_broadcast([P, 2, B, P])))
                dve.wait_ge(pe_done, 5 + NJ)
                for l in range(2):
                    v = ps[0][:, l * 4 * B:(l + 1) * 4 * B].rearrange("p (n b) -> p n b", n=4)
                    link(nc.vector.tensor_copy(k.mod[l][:], v))
                    link(nc.vector.tensor_scalar(k.mod[l][:, 1:4:2, :], k.mod[l][:, 1:4:2, :], 1.0, None, ALU.add))
                for n8 in range(8):
                    l, gi, hb = n8 // 4, n8 // 2 % 2, n8 % 2
                    dve.wait_ge(pe_done, 6 + NJ + n8)
                    link(nc.vector.tensor_copy(k.gate[l][:, gi, hb * 4:hb * 4 + 4, :],
                                               ps[1 + n8 % 2][:].rearrange("p (b d) -> p b d", b=4)))
                dve.wait_ge(s_w, 128)
                for i in range(2):
                    link(nc.vector.tensor_copy(k.w_qk0[:, i, :].rearrange("p (d h) -> p d h", h=H),
                                               k.w_qkv0[:, i, :].rearrange("p (h d) -> p d h", h=H)))
                for l in range(2):
                    g = k.gate[l][:].rearrange("p w b d -> p (w b d)")
                    link(nc.vector.tensor_scalar(g_sign[:], g, 0.0, 2.0, ALU.is_ge, ALU.mult))
                    link(nc.vector.scalar_tensor_tensor(g_abs[:], g, -1.0, g, ALU.mult, ALU.max))
                    link(nc.vector.tensor_scalar(g_abs[:], g_abs[:], GATE_MIN, None, ALU.max))
                    link(nc.vector.scalar_tensor_tensor(g, g_sign[:], -1.0, g_abs[:], ALU.add, ALU.mult))


class Norm:

    def __init__(self, k, ctx, tag):
        self.k = k

        def sem(name):
            return ctx.enter_context(k.nc.semaphore(f"{tag}_{name}"))

        self.stats = k.sb(f"{tag}_stats", [P, NT, 6], F32, ctx)
        self.mv = k.sb(f"{tag}_mean_var", [P, NT, 2], F32, ctx)
        self.rstd = k.sb(f"{tag}_rstd", [P, NT], F32, ctx)
        self.var_eps = k.sb(f"{tag}_var_eps", [P, NT], F32, ctx)
        self.hn = k.sb(f"{tag}_normed", [P, NT, D], F32, ctx)
        self.stats_seen = sem("stats_seen")
        self.stats_ready, self.mv_ready, self.eps_added, self.rstd_ready, self.hn_ready, self.hn_transposed = (
            sem(n) for n in ("stats", "mv", "eps", "rstd", "hn", "hn_transposed"))

    def moments(self, dve, b):
        nc, k = self.k.nc, self.k
        for t in range(NT):
            nc.vector.bn_stats(self.stats[:, t, :], k.x[:, b * NT + t, :]).then_inc(self.stats_ready, 1)
        dve.wait_ge(self.stats_ready, (b + 1) * NT)
        dve.sem_inc(self.stats_seen, 1)
        for t in range(NT):
            nc.vector.bn_aggr(self.mv[:, t, :], self.stats[:, t, :]).then_inc(self.mv_ready, 1)

    def inverse_deviation(self, pool, b):
        nc, k = self.k.nc, self.k
        pool.wait_ge(self.mv_ready, (b + 1) * NT)
        nc.gpsimd.tensor_tensor(self.var_eps[:], self.mv[:, :, 1], k.eps[:], ALU.add).then_inc(self.eps_added, 1)
        pool.wait_ge(self.eps_added, b + 1)
        nc.gpsimd.tensor_tensor(self.rstd[:], self.var_eps[:], k.minus_half[:], ALU.pow).then_inc(self.rstd_ready, 1)

    def normalise(self, dve, b):
        nc, k = self.k.nc, self.k
        dve.wait_ge(self.rstd_ready, b + 1)
        if not (isinstance(b, int) and b == 0):
            dve.wait_ge(self.hn_transposed, b)
        for t in range(NT):
            nc.vector.tensor_scalar(self.hn[:, t, :], k.x[:, b * NT + t, :], self.mv[:, t, 0:1], self.rstd[:, t:t + 1],
                                    ALU.subtract, ALU.mult).then_inc(self.hn_ready, 1)

    def transpose(self, pe, b, bank):
        nc, k = self.k.nc, self.k
        pe.wait_ge(self.hn_ready, (b + 1) * NT)
        for t in range(NT):
            last = nc.tensor.transpose(bank[:, t * P:(t + 1) * P], self.hn[:, t, :], k.c["ident"])
        last.then_inc(self.hn_transposed, 1)


def attention_phase(k, layer):
    nc = k.nc
    causal = layer == 1
    L = f"l{layer}"
    with ExitStack() as ctx:
        def sb(name, shape, dt=F32):
            return k.sb(f"{L}_{name}", shape, dt, ctx)

        def sem(name):
            return ctx.enter_context(nc.semaphore(f"{L}_{name}"))

        def bank(name):
            return ctx.enter_context(nc.psum_tensor(f"{L}_{name}", [P, 512], F32))

        score_ps = [bank(f"score{i}") for i in range(3)]
        shifted_ps = [bank(f"shifted{i}") for i in range(2)]
        o_ps = bank("o")
        proj_ps = bank("proj")
        turn_ps = bank("turn")

        q_stack = sb("q_stack", [P, H, T], BF16)
        k_stack = sb("k_stack", [P, H, T], BF16)
        hT = sb("hT", [P, T])
        parts = sb("parts", [P, 2, 3, T], BF16)
        rest = sb("rest", [P, 2, T])
        v_next = sb("v_next", [P, NT, D])
        v_aug = sb("v_aug", [P, NT, H, 32])
        probs = sb("probs", [P, NT, HG, T])
        mx = sb("mx", [P, 2, HG * NT])
        shift = sb("shift", [HG * NT, 3, P], BF16)
        shift_rest = sb("shift_rest", [HG * NT, P])
        o_sb = sb("o_sb", [P, T])
        rden = sb("rden", [P, NT, HG])
        y = sb("y", [P, NT, D])
        gy = sb("gy", [P, NT, D])
        if causal:
            rope_a = sb("rope_a", [P, 2, T])
            rope_b = sb("rope_b", [P, 2, T])
            turned = sb("turned", [P, 2, T])
            yT = sb("yT", [P, NT, P])
        else:
            masked = sb("masked", [P, NT, HG, P])
        parts_dram = nc.dram_tensor(f"{L}_parts_dram", [B, 2, 5, P, T], BF16).ap()
        norm = Norm(k, ctx, L)

        ones_loaded = sem("ones_loaded")
        v_aug_cleared = sem("v_aug_cleared")
        hT_ready = sem("hT_ready")
        proj_ready = sem("proj_ready")
        proj_taken = sem("proj_taken")
        v_ready = sem("v_ready")
        v_taken = sem("v_taken")
        v_stored = sem("v_stored")
        hi_ready = sem("hi_ready")
        rest_ready = sem("rest_ready")
        mid_ready = sem("mid_ready")
        lo_ready = sem("lo_ready")
        roped = sem("roped")
        parts_stored = sem("parts_stored")
        stacked = [sem(f"stacked{g}") for g in range(NG)]
        score_ready = sem("score_ready")
        max_taken = sem("max_taken")
        max_turned = sem("max_turned")
        shift_hi, shift_left, shift_mid, shift_ready = (sem(n) for n in ("shift_hi", "shift_left", "shift_mid", "shift_ready"))
        shift_stacked = [sem(f"shift_stacked{g}") for g in range(NG)]
        shifted_ready = sem("shifted_ready")
        exp_done = sem("exp_done")
        diag_masked = sem("diag_masked")
        summed = sem("summed")
        o_taken = sem("o_taken")
        o_turned = sem("o_turned")
        rden_ready = sem("rden_ready")
        y_ready = sem("y_ready")
        y_turned = sem("y_turned")
        yT_ready = sem("yT_ready")
        out_ready = sem("out_ready")
        gy_ready = sem("gy_ready")
        x_updated = sem("x_updated")

        NPROJ = 4 if causal else 2
        SCORE_BANK = [n % 3 for n in range(HG * NT - 1)] + [1]
        SCORE_REUSE = [next(d for d in range(1, 99) if SCORE_BANK[(n - d) % (HG * NT)] == SCORE_BANK[n]) for n in range(HG * NT)]
        UNITS, GROUPS, TILES = H * NT, NG, NG * NT

        def lead_head(b, g, j, following):
            h = HG * g + j + LEAD
            if h < H:
                return b, h
            return (b + 1, h - H) if following else None

        def lead_group(b, g, following):
            if g + 1 < NG:
                return b, g + 1
            return (b + 1, 0) if following else None

        def run(engine, first, slot, finish):
            first()
            slot(0, 0, False, True, True)
            with engine.Fori(0, B - 2) as b:
                for g in range(1, NG):
                    slot(b, g, True, True, True)
                slot(b + 1, 0, True, True, True)
            for g in range(1, NG):
                slot(B - 2, g, True, True, False)
            for g in range(NG):
                slot(B - 1, g, True, False, False)
            finish(B - 1)

        def fronted(b, g, following, ahead):
            if g < 2:
                return b + 1 if following else None
            return b + 2 if ahead else None

        def before(b, g):
            return b * GROUPS + g

        block = ctx.enter_context(nc.Block())

        @block.sync
        def _(sp):
            def store_parts(b):
                sp.wait_ge(lo_ready, (b + 1) * 2)
                sp.dma_start(parts_dram[b, 0, 0:3].rearrange("c p t -> p c t"), parts[:, 0]).then_inc(parts_stored, 16)
                sp.dma_start(parts_dram[b, 1, 0:3].rearrange("c p t -> p c t"), parts[:, 1]).then_inc(parts_stored, 16)
                sp.dma_start(parts_dram[b, 1, 3:5].rearrange("c p t -> p c t"), parts[:, 1, 0:2]).then_inc(parts_stored, 16)
                sp.wait_ge(parts_stored, (b + 1) * 48)

            def stack(b, g, prior):
                if prior:
                    sp.wait_ge(exp_done, (b - 1) * UNITS + (g + 1) * HG * NT)
                rows = 3 * HD
                for s in range(3):
                    for side, dst, first in ((0, q_stack, 0), (1, k_stack, s)):
                        src = parts_dram[b, side].rearrange("c (d h) t -> (c d) h t", d=HD)
                        sp.dma_start(dst[rows * s:rows * (s + 1), HG * g:HG * (g + 1), :],
                                     src[HD * first:HD * first + rows, HG * g:HG * (g + 1), :]).then_inc(stacked[g], 16)

            def stack_shift(b, g):
                sp.wait_ge(shift_ready, before(b, g) + 1)
                for c in range(3):
                    sp.dma_start(q_stack[SHIFT + c:SHIFT + c + 1, HG * g:HG * (g + 1), :].rearrange("c h (q t) -> c (h q) t", t=P),
                                 shift[:, c, :]).then_inc(shift_stacked[g], 16)

            def first():
                sp.dma_start(k_stack[SHIFT:SHIFT + 3], k.a["const_ones"]).then_inc(ones_loaded, 16)
                store_parts(0)
                for g in range(NG - 1):
                    stack(0, g, False)
                stack_shift(0, 0)

            def slot(b, g, prev, following, ahead):
                if g == 1 and following:
                    store_parts(b + 1)
                led = lead_group(b, g, following)
                if led:
                    stack_shift(*led)
                if g == 0:
                    stack(b, NG - 1, prev)
                elif following:
                    stack(b + 1, g - 1, True)

            run(sp, first, slot, lambda b: None)

        @block.tensor
        def _(pe):
            def project(w, taken_before):
                pe.wait_ge(proj_taken, taken_before)
                nc.tensor.matmul(proj_ps[:], w, hT[:], start=True, stop=True).then_inc(proj_ready, 1)

            if causal:
                weights = [k.w1[:, i, :] for i in range(4)]
                wv = k.w1[:, 4, :]
            else:
                weights = [k.w_qk0[:, i, :] for i in range(2)]
                wv = k.w_qkv0[:, 2, :]

            def turn_norm(b, prior):
                if prior:
                    pe.wait_ge(v_taken, b)
                norm.transpose(pe, b, proj_ps)

            def project_qk(b, which):
                if which == 0:
                    pe.wait_ge(hT_ready, b + 1)
                    nc.tensor.matmul(proj_ps[:], weights[0], hT[:], start=True, stop=True).then_inc(proj_ready, 1)
                else:
                    project(weights[which], b * NPROJ + which)

            def project_v(b):
                pe.wait_ge(proj_taken, (b + 1) * NPROJ)
                for t in range(NT):
                    last = nc.tensor.matmul(proj_ps[:, t * P:(t + 1) * P], hT[:, t * P:(t + 1) * P], wv, start=True, stop=True)
                last.then_inc(v_ready, 1)

            def score(b, h, qt, warm):
                n = b * UNITS + h * NT + qt
                if h % HG == 0 and qt == 0:
                    pe.wait_ge(stacked[h // HG], (b + 1) * 96)
                m = h % HG * NT + qt
                if warm:
                    pe.wait_ge(max_taken, n + 1 - SCORE_REUSE[m])
                cols = (qt + 1) * P if causal else T
                nc_out = score_ps[SCORE_BANK[m]]
                last = nc.tensor.matmul(nc_out[:, 0:cols], q_stack[0:ROWS, h, qt * P:(qt + 1) * P], k_stack[0:ROWS, h, 0:cols],
                                        start=True, stop=not causal)
                if causal:
                    last = nc.tensor.matmul(nc_out[:, qt * P:cols], k.cbf[:, 0, :], k.cbf[:, 1, :],
                                            start=False, stop=True)
                last.then_inc(score_ready, 1)

            def shifted(b, g, kt, i, warm):
                n = b * UNITS + g * HG * NT + kt * HG + i
                h = HG * g + i
                if kt == 0 and i == 0:
                    pe.wait_ge(shift_stacked[g], (b + 1) * 48)
                if warm:
                    pe.wait_ge(exp_done, n - 1)
                lo = kt * P if causal else 0
                dst = shifted_ps[i % 2]
                last = nc.tensor.matmul(dst[:, lo:T], k_stack[0:SHIFT + 3, h, kt * P:(kt + 1) * P], q_stack[0:SHIFT + 3, h, lo:T],
                                        start=True, stop=not causal)
                if causal:
                    last = nc.tensor.matmul(dst[:, lo:lo + P], k.cbf[:, 0, :], k.cbf[:, 2, :], start=False, stop=True)
                last.then_inc(shifted_ready, 1)

            def sum_tile(b, g, kt):
                u = b * TILES + g * NT + kt
                if kt == 0:
                    if g > 0 or not isinstance(b, int) or b > 0:
                        pe.wait_ge(o_taken, before(b, g))
                    if g == 0:
                        pe.wait_ge(v_stored, b + 1)
                pe.wait_ge(exp_done, (u + 1) * HG)

                def heads(lhs, rhs, lo, hi, m, start, stop):
                    for i in range(HG):
                        ins = nc.tensor.matmul(o_ps[32 * i:32 * i + m, lo:hi], lhs(i), rhs(i), start=start, stop=stop,
                                               skip_group_check=True, tile_position=(0, 32 * i))
                    return ins

                def values(i):
                    return v_aug[:, kt, HG * g + i, :]

                diag = kt * P
                if causal:
                    last = heads(values, lambda i: probs[:, kt, i, diag:T], diag, T, 32, kt == 0, kt == NT - 1)
                else:
                    last = heads(lambda i: k.c["den_col"], lambda i: probs[:, kt, i, 0:diag + P], 0, diag + P, 32, kt == 0, False)
                    if kt + 1 < NT:
                        last = heads(values, lambda i: probs[:, kt, i, diag + P:T], diag + P, T, 32, False, False)
                    pe.wait_ge(diag_masked, u + 1)
                    last = heads(lambda i: v_aug[:, kt, HG * g + i, 0:HD], lambda i: masked[:, kt, i, :], diag, diag + P, HD,
                                 False, kt == NT - 1)
                last.then_inc(summed, 1)

            def turn_max(b, g):
                pe.wait_ge(max_taken, b * UNITS + (g + 1) * HG * NT)
                nc.tensor.transpose(turn_ps[0:HG * NT, 0:P], mx[:, g % 2, :], k.c["ident"]).then_inc(max_turned, 1)

            def turn_sums(b, g):
                pe.wait_ge(o_taken, before(b, g) + 1)
                if isinstance(b, int) and b == B - 1 and g >= NG - 2:
                    pe.wait_ge(y_ready, before(b, g))
                else:
                    pe.wait_ge(shift_ready, before(b, g) + 3)
                for t in range(NT):
                    last = nc.tensor.transpose(turn_ps[:, t * P:(t + 1) * P], o_sb[:, t * P:(t + 1) * P], k.c["ident"])
                last.then_inc(o_turned, 1)

            def turn_y(b):
                pe.wait_ge(y_ready, (b + 1) * GROUPS)
                for t in range(NT):
                    last = nc.tensor.transpose(turn_ps[:, t * P:(t + 1) * P], y[:, t, :], k.c["ident"])
                last.then_inc(y_turned, 1)

            def project_out(b):
                pe.wait_ge(yT_ready, b + 1)
                for t in range(NT):
                    last = nc.tensor.matmul(turn_ps[:, t * P:(t + 1) * P], yT[:, t, :], k.w1[:, 5, :], start=True, stop=True)
                last.then_inc(out_ready, 1)

            def front(s, g, j):
                if (g, j) == (3, 1):
                    turn_norm(s, True)
                elif (g, j) == (3, 2):
                    project_qk(s, 0)
                elif causal and (g, j) in ((3, 3), (0, 0), (0, 1)):
                    project_qk(s, {(3, 3): 1, (0, 0): 2, (0, 1): 3}[g, j])
                elif not causal and (g, j) == (0, 0):
                    project_qk(s, 1)
                elif (g, j) == (0, 2):
                    project_v(s)

            def first():
                turn_norm(0, False)
                for which in range(NPROJ):
                    project_qk(0, which)
                project_v(0)
                for j in range(1, NT):
                    front(1, NG - 1, j)
                for h in range(LEAD):
                    for qt in range(NT):
                        score(0, h, qt, h * NT + qt >= 3)
                turn_max(0, 0)
                pe.wait_ge(ones_loaded, 16)

            def slot(b, g, prev, following, ahead):
                for j in range(NT):
                    warm = prev or j > 0
                    led = lead_head(b, g, j, following)

                    def lead(qt):
                        if led:
                            score(*led, qt, True)

                    shifted(b, g, j, 0, warm)
                    lead(0)
                    shifted(b, g, j, 1, warm)
                    lead(1)
                    if j == 1 and lead_group(b, g, following):
                        turn_max(*lead_group(b, g, following))
                    if j > 0:
                        sum_tile(b, g, j - 1)
                    elif prev:
                        sum_tile(*((b, g - 1) if g else (b - 1, NG - 1)), NT - 1)
                    shifted(b, g, j, 2, True)
                    lead(2)
                    shifted(b, g, j, 3, True)
                    lead(3)
                    if prev and j == 1:
                        turn_sums(*((b, g - 1) if g else (b - 1, NG - 1)))
                    s = fronted(b, g, following, ahead)
                    if s is not None:
                        front(s, g, j)
                    if causal and prev and g == 0:
                        if j == 2:
                            turn_y(b - 1)
                        if j == 3:
                            project_out(b - 1)

            def finish(b):
                sum_tile(b, NG - 1, NT - 1)
                turn_sums(b, NG - 1)
                if causal:
                    turn_y(b)
                    project_out(b)

            run(pe, first, slot, finish)

        @block.scalar
        def _(act):
            def store_hT(b):
                lo = MOD_ROWS["attn"]
                act.wait_ge(norm.hn_transposed, b + 1)
                nc.scalar.activation(hT[:], proj_ps[:], ACT.Identity, bias=k.mod[layer][:, lo[0], bass.ds(b, 1)],
                                     scale=k.mod[layer][:, lo[1], bass.ds(b, 1)]).then_inc(hT_ready, 1)

            def high_part(b, side):
                if causal:
                    act.wait_ge(roped, b * 2 + side + 1)
                    nc.scalar.copy(parts[:, side, 0, :], turned[:, side, :]).then_inc(hi_ready, 1)
                else:
                    act.wait_ge(proj_ready, b * NPROJ + side + 1)
                    nc.scalar.copy(parts[:, side, 0, :], proj_ps[:]).then_inc(hi_ready, 1)

            def store_v(b):
                act.wait_ge(v_taken, b + 1)
                nc.scalar.copy(v_aug[:, :, :, 0:HD], v_next[:].rearrange("p t (h d) -> p t h d", h=H)).then_inc(v_stored, 1)

            def take_v(b):
                act.wait_ge(v_ready, b + 1)
                nc.scalar.copy(v_next[:], proj_ps[:].rearrange("p (t d) -> p t d", t=NT)).then_inc(v_taken, 1)

            def take_sums(b, g):
                act.wait_ge(summed, (before(b, g) + 1) * NT)
                nc.scalar.copy(o_sb[:], o_ps[:]).then_inc(o_taken, 1)

            def exponential(b, g, kt, i, warm):
                n = b * UNITS + g * HG * NT + kt * HG + i
                if i == 0 and warm:
                    act.wait_ge(summed, before(b, g) * NT + kt - NT + 1)
                act.wait_ge(shifted_ready, n + 1)
                lo = kt * P if causal else 0
                nc.scalar.activation(probs[:, kt, i, lo:T], shifted_ps[i % 2][:, lo:T], ACT.Exp,
                                     scale=SCALE).then_inc(exp_done, 1)

            def store_yT(b):
                act.wait_ge(y_turned, b + 1)
                nc.scalar.copy(yT[:], turn_ps[:].rearrange("p (t q) -> p t q", t=NT)).then_inc(yT_ready, 1)

            def front(s, g, j):
                if (g, j) == (3, 1):
                    store_hT(s)
                if (g, j) == ((0, 0) if causal else (3, 2)):
                    high_part(s, 0)
                if (g, j) == ((0, 2) if causal else (0, 0)):
                    high_part(s, 1)
                if (g, j) == ((0, 3) if causal else (0, 2)):
                    take_v(s)

            def first():
                store_hT(0)
                high_part(0, 0)
                high_part(0, 1)
                take_v(0)
                act.wait_ge(parts_stored, 48)
                for j in range(NT):
                    front(1, NG - 1, j)
                act.wait_ge(v_aug_cleared, 1)

            def slot(b, g, prev, following, ahead):
                for j in range(NT):
                    for i in range(HG):
                        exponential(b, g, j, i, prev)
                    if j == 0:
                        if prev:
                            take_sums(*((b, g - 1) if g else (b - 1, NG - 1)))
                        if g == 0:
                            store_v(b)
                    s = fronted(b, g, following, ahead)
                    if s is not None:
                        front(s, g, j)
                    if causal and prev and (g, j) == (0, 2):
                        store_yT(b - 1)

            def finish(b):
                take_sums(b, NG - 1)
                if causal:
                    store_yT(b)

            run(act, first, slot, finish)

        @block.vector
        def _(dve):
            def row_max(b, h, qt):
                dve.wait_ge(score_ready, b * UNITS + h * NT + qt + 1)
                cols = (qt + 1) * P if causal else T
                g, i = h // HG, h % HG
                nc.vector.tensor_reduce(mx[:, g % 2, i * NT + qt:i * NT + qt + 1], score_ps[SCORE_BANK[i * NT + qt]][:, 0:cols],
                                        AX.X, ALU.max).then_inc(max_taken, 1)

            def split_shift(b, g, prior):
                n = before(b, g)
                dve.wait_ge(max_turned, n + 1)
                if prior:
                    prior_b, prior_g = (b, g - 1) if g else (b - 1, NG - 1)
                    dve.wait_ge(shift_stacked[prior_g], (prior_b + 1) * 48)
                m = turn_ps[0:HG * NT, 0:P]
                nc.vector.tensor_scalar(shift[:, 0, :], m, -1.0, None, ALU.mult).then_inc(shift_hi, 1)
                dve.wait_ge(shift_hi, n + 1)
                nc.vector.scalar_tensor_tensor(shift_rest[:], m, -1.0, shift[:, 0, :], ALU.mult,
                                               ALU.subtract).then_inc(shift_left, 1)
                dve.wait_ge(shift_left, n + 1)
                nc.vector.tensor_copy(shift[:, 1, :], shift_rest[:]).then_inc(shift_mid, 1)
                dve.wait_ge(shift_mid, n + 1)
                nc.vector.tensor_tensor(shift[:, 2, :], shift_rest[:], shift[:, 1, :], ALU.subtract).then_inc(shift_ready, 1)

            def divide(b, g):
                n = before(b, g)
                dve.wait_ge(o_turned, n + 1)
                s = turn_ps[:].rearrange("p (t i r) -> p t i r", t=NT, i=HG)
                nc.vector.reciprocal(rden[:], s[:, :, :, HD]).then_inc(rden_ready, 1)
                dve.wait_ge(rden_ready, n + 1)
                nc.vector.tensor_tensor(y[:].rearrange("p t (h d) -> p t h d", h=H)[:, :, HG * g:HG * (g + 1), :], s[:, :, :, 0:HD],
                                        rden[:, :, :, None].to_broadcast([P, NT, HG, HD]), ALU.mult).then_inc(y_ready, 1)

            def rope_product(b, which):
                dst, factor = ((rope_a, k.c["cos"]), (rope_b, k.c["sin"]))[which % 2]
                dve.wait_ge(proj_ready, b * NPROJ + which + 1)
                nc.vector.tensor_tensor(dst[:, which // 2, :], proj_ps[:], factor, ALU.mult).then_inc(proj_taken, 1)

            def what_is_left(b, side):
                dve.wait_ge(hi_ready, b * 2 + side + 1)
                nc.vector.tensor_tensor(rest[:, side, :], proj_ps[:], parts[:, side, 0, :], ALU.subtract).then_inc(proj_taken, 1)

            def middle_part(b, side):
                n = b * 2 + side
                if causal:
                    dve.wait_ge(rest_ready, n + 1)
                else:
                    dve.wait_ge(proj_taken, n + 1)
                nc.vector.tensor_copy(parts[:, side, 1, :], rest[:, side, :]).then_inc(mid_ready, 1)

            def scale_out(b):
                if isinstance(b, int):
                    dve.wait_ge(x_updated, b)
                dve.wait_ge(out_ready, b + 1)
                nc.vector.tensor_tensor(gy[:], turn_ps[:].rearrange("p (t d) -> p t d", t=NT),
                                        k.gate[layer][:, 0, bass.ds(b, 1), :].to_broadcast([P, NT, D]), ALU.mult).then_inc(gy_ready, 1)

            def front(s, g, j):
                if (g, j) == (2, 3):
                    norm.moments(dve, s)
                if (g, j) == (3, 0):
                    norm.normalise(dve, s)
                if causal:
                    if (g, j) in ((3, 2), (3, 3), (0, 0), (0, 1)):
                        rope_product(s, {(3, 2): 0, (3, 3): 1, (0, 0): 2, (0, 1): 3}[g, j])
                    if (g, j) == (0, 1):
                        middle_part(s, 0)
                    if (g, j) == (0, 3):
                        middle_part(s, 1)
                elif (g, j) in ((3, 2), (0, 0)):
                    side = 0 if g else 1
                    what_is_left(s, side)
                    middle_part(s, side)

            def first():
                norm.moments(dve, 0)
                norm.normalise(dve, 0)
                norm.moments(dve, 1)
                for side in range(2):
                    if causal:
                        rope_product(0, 2 * side)
                        rope_product(0, 2 * side + 1)
                    else:
                        what_is_left(0, side)
                        middle_part(0, side)
                if causal:
                    middle_part(0, 0)
                    middle_part(0, 1)
                dve.wait_ge(parts_stored, 48)
                for j in range(NT):
                    front(1, NG - 1, j)
                for h in range(LEAD):
                    for qt in range(NT):
                        row_max(0, h, qt)
                split_shift(0, 0, False)

            def slot(b, g, prev, following, ahead):
                for j in range(NT):
                    led = lead_head(b, g, j, following)
                    for qt in range(NT):
                        if led:
                            row_max(*led, qt)
                        if j == 1 and qt == 1 and lead_group(b, g, following):
                            split_shift(*lead_group(b, g, following), True)
                    if prev and j == 1:
                        divide(*((b, g - 1) if g else (b - 1, NG - 1)))
                    s = fronted(b, g, following, ahead)
                    if s is not None:
                        front(s, g, j)
                    if prev and (g, j) == (0, 3):
                        if causal:
                            scale_out(b - 1)
                        else:
                            dve.wait_ge(gy_ready, b)

            def finish(b):
                divide(b, NG - 1)
                if causal:
                    scale_out(b)

            run(dve, first, slot, finish)

        @block.gpsimd
        def _(pool):
            def mask_diagonal(b, g, kt):
                pool.wait_ge(exp_done, (b * TILES + g * NT + kt + 1) * HG)
                nc.gpsimd.tensor_tensor(masked[:, kt], probs[:, kt, :, kt * P:(kt + 1) * P],
                                        k.c["causal_t"][:, None, :].to_broadcast([P, HG, P]), ALU.mult).then_inc(diag_masked, 1)

            def low_part(b, side):
                n = b * 2 + side
                pool.wait_ge(mid_ready, n + 1)
                nc.gpsimd.tensor_tensor(parts[:, side, 2, :], rest[:, side, :], parts[:, side, 1, :], ALU.subtract).then_inc(lo_ready, 1)

            def rope_sum(b, side):
                n = b * 2 + side
                pool.wait_ge(proj_taken, b * NPROJ + 2 * side + 2)
                nc.gpsimd.tensor_tensor(turned[:, side, :], rope_a[:, side, :], rope_b[:, side, :], ALU.add).then_inc(roped, 1)
                pool.wait_ge(hi_ready, n + 1)
                nc.gpsimd.tensor_tensor(rest[:, side, :], turned[:, side, :], parts[:, side, 0, :], ALU.subtract).then_inc(rest_ready, 1)

            def update_x(b):
                xb = k.x[:, bass.ds(b * NT, NT), :]
                if not causal:
                    pool.wait_ge(y_ready, (b + 1) * GROUPS)
                    nc.gpsimd.tensor_tensor(gy[:], y[:], k.gate[layer][:, 0, bass.ds(b, 1), :].to_broadcast([P, NT, D]),
                                            ALU.mult).then_inc(gy_ready, 1)
                pool.wait_ge(gy_ready, b + 1)
                nc.gpsimd.tensor_tensor(xb, xb, gy[:], ALU.add).then_inc(x_updated, 1)

            def split_side(b, side):
                if causal:
                    rope_sum(b, side)
                low_part(b, side)

            def front(s, g, j):
                if (g, j) == (2, 3):
                    norm.inverse_deviation(pool, s)
                if (g, j) == ((0, 0) if causal else (3, 2)):
                    split_side(s, 0)
                if (g, j) == ((0, 2) if causal else (0, 0)):
                    split_side(s, 1)

            def first():
                norm.inverse_deviation(pool, 0)
                norm.inverse_deviation(pool, 1)
                split_side(0, 0)
                split_side(0, 1)
                for j in range(1, NT):
                    front(1, NG - 1, j)
                nc.gpsimd.tensor_copy(v_aug[:].rearrange("p t h r -> p (t h) r"),
                                      k.c["den_col"][:, None, :].to_broadcast([P, NT * H, 32])).then_inc(v_aug_cleared, 1)

            def slot(b, g, prev, following, ahead):
                for j in range(NT):
                    if not causal:
                        mask_diagonal(b, g, j)
                    s = fronted(b, g, following, ahead)
                    if s is not None:
                        front(s, g, j)
                    if prev and (g, j) == (0, 1) and not causal:
                        update_x(b - 1)
                    if prev and (g, j) == (0, 3) and causal:
                        update_x(b - 1)

            run(pool, first, slot, update_x)


def experts_phase(k):
    nc = k.nc
    LAG, STEPS = 3, E * FT
    H_SCALE, W_SCALE, HID_SCALE = 8.0, 64.0, 2.0
    PROJ_SCALE = H_SCALE * W_SCALE
    ROUTER_STEPS = 14
    with ExitStack() as ctx:
        def sb(name, shape, dt=F32):
            return k.sb(f"ex_{name}", shape, dt, ctx)

        def sem(name):
            return ctx.enter_context(nc.semaphore(f"ex_{name}"))

        def bank(name):
            return ctx.enter_context(nc.psum_tensor(f"ex_{name}", [P, 512], F32))

        gate_ps = [bank(f"gate{i}") for i in range(2)]
        up_ps = [bank(f"up{i}") for i in range(2)]
        down_ps = [bank(f"down{i}") for i in range(2)]
        norm_ps = bank("norm")
        logit_ps = bank("logit")

        raw = sb("w_raw", [P, 3, STEPS, D])
        w_hi = sb("w_hi", [P, 3, STEPS, D], F16)
        w_lo = sb("w_lo", [P, 3, STEPS, D], F16)
        hT = sb("hT", [P, T])
        h_hi = sb("h_hi", [P, T], F16)
        h_lo = sb("h_lo", [P, T], F16)
        th = sb("tanh", [P, 2, T])
        half = sb("half", [P, 2, T])
        hid = sb("hid", [P, 2, T])
        hid_hi = sb("hid_hi", [P, 4, T], F16)
        hid_lo = sb("hid_lo", [P, 4, T], F16)
        acc = sb("acc", [P, NT, D])
        shifted = sb("shifted", [P, NT, E])
        prob = sb("prob", [P, NT, E])
        top = sb("top", [P, NT])
        total = sb("total", [P, NT])
        above = sb("above", [P, NT, E, E])
        tied = sb("tied", [P, NT, E, E])
        rank = sb("rank", [P, NT, E])
        weight = sb("weight", [P, NT, E])
        norm = Norm(k, ctx, "ex")

        w_loaded = [sem(f"w_loaded{i}") for i in range(3)]
        w_turned = sem("w_turned")
        w_hi_stored = sem("w_hi_stored")
        w_lo_stored = sem("w_lo_stored")
        hT_ready = sem("hT_ready")
        logits_ready = sem("logits_ready")
        exps_ready = sem("exps_ready")
        router_step = sem("router_step")
        gate_ready = sem("gate_ready")
        up_ready = sem("up_ready")
        tanh_ready = sem("tanh_ready")
        silu_ready = sem("silu_ready")
        hid_ready = sem("hid_ready")
        hid_hi_ready = sem("hid_hi_ready")
        hid_lo_ready = sem("hid_lo_ready")
        h_hi_ready = sem("h_hi_ready")
        h_lo_ready = sem("h_lo_ready")
        down_done = sem("down_done")
        combined = sem("combined")
        gated = sem("gated")
        x_updated = sem("x_updated")

        QUADS = 3 * STEPS // 4
        banks = gate_ps + up_ps

        def run(engine, body):
            body(0, True, True)
            with engine.Fori(1, B - 1) as b:
                body(b, False, True)
            body(B - 1, False, False)

        block = ctx.enter_context(nc.Block())

        @block.sync
        def _(sp):
            for i, name in enumerate(("gate", "up")):
                sp.dma_start(raw[:, i], k.a[f"L0_ffn_W_{name}"].rearrange("e (f p) d -> p (e f) d", p=P)).then_inc(w_loaded[i], 16)
            sp.dma_start(raw[:, 2].rearrange("p (e f) c -> p e (f c)", e=E),
                         k.a["L0_ffn_W_down"].rearrange("e d f -> d e f")).then_inc(w_loaded[2], 16)

        @block.tensor
        def _(pe):
            for q in range(QUADS):
                which, step = divmod(q * 4, STEPS)
                if step == 0:
                    pe.wait_ge(w_loaded[which], 16)
                if q >= 4:
                    pe.wait_ge(w_lo_stored, q - 3)
                for i in range(4):
                    last = nc.tensor.transpose(banks[q % 4][:, i * P:(i + 1) * P], raw[:, which, step + i, :], k.c["ident"])
                last.then_inc(w_turned, 1)
            pe.wait_ge(w_lo_stored, QUADS)

            def project(bank, which, n):
                nc.tensor.matmul(bank[:], w_lo[:, which, n, :], h_hi[:], start=True, stop=False)
                nc.tensor.matmul(bank[:], w_hi[:, which, n, :], h_lo[:], start=False, stop=False)
                return nc.tensor.matmul(bank[:], w_hi[:, which, n, :], h_hi[:], start=False, stop=True)

            def gate_up(b, n, warm):
                if warm:
                    pe.wait_ge(silu_ready, b * STEPS + n - 1)
                project(gate_ps[n % 2], 0, n).then_inc(gate_ready, 1)
                if warm:
                    pe.wait_ge(hid_ready, b * STEPS + n - 1)
                project(up_ps[n % 2], 1, n).then_inc(up_ready, 1)

            def down(b, n, warm):
                e, f = divmod(n, FT)
                if f == 0 and warm:
                    pe.wait_ge(combined, b * E + e - 1)
                pe.wait_ge(hid_lo_ready, b * STEPS + n + 1)
                for t in range(NT):
                    tokens = slice(t * P, (t + 1) * P)
                    y = down_ps[e % 2][:, tokens]
                    nc.tensor.matmul(y, hid_lo[:, n % 4, tokens], w_hi[:, 2, n, :], start=(f == 0 and t == 0), stop=False,
                                     skip_group_check=True)
                    nc.tensor.matmul(y, hid_hi[:, n % 4, tokens], w_lo[:, 2, n, :], start=False, stop=False, skip_group_check=True)
                    last = nc.tensor.matmul(y, hid_hi[:, n % 4, tokens], w_hi[:, 2, n, :], start=False, stop=(f == FT - 1),
                                            skip_group_check=True)
                last.then_inc(down_done, 1)

            def body(b, first, following):
                if first:
                    norm.transpose(pe, b, norm_ps)
                pe.wait_ge(hT_ready, b + 1)
                for t in range(NT):
                    last = nc.tensor.matmul(logit_ps[:, t * E:(t + 1) * E], hT[:, t * P:(t + 1) * P], k.router[:], start=True, stop=True)
                last.then_inc(logits_ready, 1)
                pe.wait_ge(h_lo_ready, b + 1)
                for n in range(STEPS):
                    gate_up(b, n, not first or n >= 2)
                    if n >= LAG:
                        down(b, n - LAG, not first or n - LAG >= 2 * FT)
                    if n == STEPS // 2 and following:
                        norm.transpose(pe, b + 1, norm_ps)
                for n in range(STEPS - LAG, STEPS):
                    down(b, n, True)

            run(pe, body)

        @block.scalar
        def _(act):
            for q in range(QUADS):
                which, step = divmod(q * 4, STEPS)
                act.wait_ge(w_turned, q + 1)
                nc.scalar.activation(w_hi[:, which, step:step + 4, :], banks[q % 4][:].rearrange("p (i c) -> p i c", i=4), ACT.Copy,
                                     scale=W_SCALE).then_inc(w_hi_stored, 1)

            def body(b, first, following):
                act.wait_ge(norm.hn_transposed, b + 1)
                if not first:
                    act.wait_ge(up_ready, b * STEPS)
                lo = MOD_ROWS["ffn"]
                nc.scalar.activation(hT[:], norm_ps[:], ACT.Identity, bias=k.mod[0][:, lo[0], bass.ds(b, 1)],
                                     scale=k.mod[0][:, lo[1], bass.ds(b, 1)]).then_inc(hT_ready, 1)
                act.wait_ge(hT_ready, b + 1)
                nc.scalar.activation(h_hi[:], hT[:], ACT.Copy, scale=H_SCALE).then_inc(h_hi_ready, 1)

                def high_part(n, warm):
                    if warm:
                        act.wait_ge(down_done, b * STEPS + n - 3)
                    act.wait_ge(hid_ready, b * STEPS + n + 1)
                    nc.scalar.copy(hid_hi[:, n % 4, :], hid[:, n % 2, :]).then_inc(hid_hi_ready, 1)

                for n in range(STEPS):
                    act.wait_ge(gate_ready, b * STEPS + n + 1)
                    nc.scalar.activation(th[:, n % 2, :], gate_ps[n % 2][:], ACT.Tanh, scale=0.5 / PROJ_SCALE).then_inc(tanh_ready, 1)
                    if n >= 1:
                        high_part(n - 1, not first or n - 1 >= 4)
                    if n == 1:
                        act.wait_ge(router_step, b * ROUTER_STEPS + 2)
                        nc.scalar.activation(prob[:], shifted[:], ACT.Exp).then_inc(exps_ready, 1)
                high_part(STEPS - 1, True)

            run(act, body)

        @block.vector
        def _(dve):
            for q in range(QUADS):
                which, step = divmod(q * 4, STEPS)
                dve.wait_ge(w_hi_stored, q + 1)
                nc.vector.scalar_tensor_tensor(w_lo[:, which, step:step + 4, :], banks[q % 4][:].rearrange("p (i c) -> p i c", i=4), W_SCALE,
                                               w_hi[:, which, step:step + 4, :], ALU.mult, ALU.subtract).then_inc(w_lo_stored, 1)

            def silu_times_up(b, n, warm):
                dve.wait_ge(tanh_ready, b * STEPS + n + 1)
                nc.vector.scalar_tensor_tensor(half[:, n % 2, :], th[:, n % 2, :], 1.0, gate_ps[n % 2][:], ALU.add,
                                               ALU.mult).then_inc(silu_ready, 1)
                dve.wait_ge(silu_ready, b * STEPS + n + 1)
                dve.wait_ge(up_ready, b * STEPS + n + 1)
                if warm:
                    dve.wait_ge(hid_lo_ready, b * STEPS + n - 1)
                nc.vector.scalar_tensor_tensor(hid[:, n % 2, :], half[:, n % 2, :], HID_SCALE / PROJ_SCALE ** 2, up_ps[n % 2][:],
                                               ALU.mult, ALU.mult).then_inc(hid_ready, 1)

            def route(b, part):
                count = [0 if part == 0 else 2]

                def link(ins):
                    count[0] += 1
                    ins.then_inc(router_step, 1)
                    dve.wait_ge(router_step, b * ROUTER_STEPS + count[0])

                each = [P, NT, E]
                pairs = [P, NT, E, E]
                logits = logit_ps[:, 0:NT * E].rearrange("p (t e) -> p t e", t=NT)
                if part == 0:
                    dve.wait_ge(logits_ready, b + 1)
                    link(nc.vector.tensor_reduce(top[:], logits, AX.X, ALU.max))
                    link(nc.vector.tensor_tensor(shifted[:], logits, top[:, :, None].to_broadcast(each), ALU.subtract))
                    return
                dve.wait_ge(exps_ready, b + 1)
                link(nc.vector.tensor_reduce(total[:], prob[:], AX.X, ALU.add))
                link(nc.vector.reciprocal(total[:], total[:]))
                link(nc.vector.tensor_tensor(prob[:], prob[:], total[:, :, None].to_broadcast(each), ALU.mult))
                other = prob[:, :, None, :].to_broadcast(pairs)
                own = prob[:, :, :, None].to_broadcast(pairs)
                link(nc.vector.tensor_tensor(above[:], other, own, ALU.is_gt))
                link(nc.vector.tensor_tensor(tied[:], other, own, ALU.is_equal))
                link(nc.vector.tensor_tensor(tied[:], tied[:], k.c["before"].rearrange("p (e j) -> p e j", e=E)[:, None, :, :].to_broadcast(pairs),
                                             ALU.mult))
                link(nc.vector.tensor_tensor(above[:], above[:], tied[:], ALU.add))
                link(nc.vector.tensor_reduce(rank[:], above[:], AX.X, ALU.add))
                link(nc.vector.scalar_tensor_tensor(rank[:], rank[:], 2.0, prob[:], ALU.is_lt, ALU.mult))
                link(nc.vector.tensor_reduce(total[:], rank[:], AX.X, ALU.add))
                link(nc.vector.reciprocal(total[:], total[:]))
                link(nc.vector.scalar_tensor_tensor(weight[:], rank[:], 0.5 / (HID_SCALE * W_SCALE), total[:, :, None].to_broadcast(each), ALU.mult, ALU.mult))

            def combine(b, e, first):
                dve.wait_ge(down_done, b * STEPS + (e + 1) * FT)
                if e == 0 and not first:
                    dve.wait_ge(x_updated, b)
                if e > 0:
                    dve.wait_ge(combined, b * E + e)
                for t in range(NT):
                    y = down_ps[e % 2][:, t * P:(t + 1) * P]
                    w = weight[:, t, e:e + 1]
                    if e == 0:
                        last = nc.vector.tensor_scalar(acc[:, t, :], y, w, None, ALU.mult)
                    else:
                        last = nc.vector.scalar_tensor_tensor(acc[:, t, :], y, w, acc[:, t, :], ALU.mult, ALU.add)
                last.then_inc(combined, 1)

            def body(b, first, following):
                if first:
                    norm.moments(dve, b)
                    norm.normalise(dve, b)
                dve.wait_ge(h_hi_ready, b + 1)
                nc.vector.scalar_tensor_tensor(h_lo[:], hT[:], H_SCALE, h_hi[:], ALU.mult, ALU.subtract).then_inc(h_lo_ready, 1)
                route(b, 0)
                for n in range(STEPS):
                    silu_times_up(b, n, not first or n >= 2)
                    if n == 3:
                        route(b, 1)
                    if n >= 7 and (n - 7) % FT == 0:
                        combine(b, (n - 7) // FT, first)
                    if following and n == 8:
                        norm.moments(dve, b + 1)
                    if following and n == 12:
                        norm.normalise(dve, b + 1)
                combine(b, E - 1, first)

            run(dve, body)

        @block.gpsimd
        def _(pool):
            def body(b, first, following):
                if first:
                    norm.inverse_deviation(pool, b)
                for n in range(STEPS):
                    pool.wait_ge(hid_hi_ready, b * STEPS + n + 1)
                    nc.gpsimd.tensor_tensor(hid_lo[:, n % 4, :], hid[:, n % 2, :], hid_hi[:, n % 4, :],
                                            ALU.subtract).then_inc(hid_lo_ready, 1)
                    if n == 10 and following:
                        norm.inverse_deviation(pool, b + 1)
                xb = k.x[:, bass.ds(b * NT, NT), :]
                pool.wait_ge(combined, (b + 1) * E)
                nc.gpsimd.tensor_tensor(acc[:], acc[:], k.gate[0][:, 1, bass.ds(b, 1), :].to_broadcast([P, NT, D]),
                                        ALU.mult).then_inc(gated, 1)
                pool.wait_ge(gated, b + 1)
                nc.gpsimd.tensor_tensor(xb, xb, acc[:], ALU.add).then_inc(x_updated, 1)

            run(pool, body)


def units_phase(k):
    nc = k.nc
    LAG = 2
    with ExitStack() as ctx:
        def sb(name, shape, dt=F32):
            return k.sb(f"un_{name}", shape, dt, ctx)

        def sem(name):
            return ctx.enter_context(nc.semaphore(f"un_{name}"))

        def bank(name):
            return ctx.enter_context(nc.psum_tensor(f"un_{name}", [P, 512], F32))

        unit_ps = [bank(f"unit{i}") for i in range(3)]
        out_ps = bank("out")
        norm_ps = bank("norm")
        hT = sb("hT", [P, T])
        relu = sb("relu", [P, 4, T])
        biased = sb("biased", [P, NT, D])
        norm = Norm(k, ctx, "un")
        hT_ready = sem("hT_ready")
        unit_ready = sem("unit_ready")
        relu_ready = sem("relu_ready")
        out_added = sem("out_added")
        biased_ready = sem("biased_ready")
        gated = sem("gated")
        x_updated = sem("x_updated")
        x_stored = sem("x_stored")

        def run(engine, body):
            body(0, True, True)
            with engine.Fori(1, B - 1) as b:
                body(b, False, True)
            body(B - 1, False, False)

        block = ctx.enter_context(nc.Block())

        @block.sync
        def _(sp):
            def body(b, first, following):
                sp.wait_ge(x_updated, b + 1)
                sp.dma_start(k.out[bass.ds(b, 1)].rearrange("b (t p) d -> p (b t) d", p=P),
                             k.x[:, bass.ds(b * NT, NT), :]).then_inc(x_stored, 16)

            run(sp, body)
            sp.wait_ge(x_stored, 16 * B)

        @block.tensor
        def _(pe):
            win = k.win_rep[:].rearrange("p m h -> p (m h)")

            def unit(b, j):
                i = j % 2
                pe.wait_ge(relu_ready, b * NJ + j - 1)
                nc.tensor.matmul(unit_ps[i][:], win[:, j * P:(j + 1) * P], hT[:], start=True, stop=True).then_inc(unit_ready, 1)

            def add_out(b, j, first):
                pe.wait_ge(relu_ready, b * NJ + j + 1)
                if j == 0 and not first:
                    pe.wait_ge(biased_ready, b)
                for t in range(NT):
                    last = nc.tensor.matmul(out_ps[:, t * P:(t + 1) * P], relu[:, j % 4, t * P:(t + 1) * P], k.wout_rep[:, j, :],
                                            start=(j == 0 and t == 0), stop=(j == NJ - 1), skip_group_check=True)
                last.then_inc(out_added, 1)

            def body(b, first, following):
                if first:
                    norm.transpose(pe, b, norm_ps)
                pe.wait_ge(hT_ready, b + 1)
                for j in range(NJ):
                    if first and j < 2:
                        nc.tensor.matmul(unit_ps[j % 2][:], win[:, j * P:(j + 1) * P], hT[:], start=True, stop=True).then_inc(unit_ready, 1)
                    else:
                        unit(b, j)
                    if j >= LAG:
                        add_out(b, j - LAG, first)
                    if following and j == NJ // 2:
                        norm.transpose(pe, b + 1, norm_ps)
                for j in range(NJ - LAG, NJ):
                    add_out(b, j, first)

            run(pe, body)

        @block.scalar
        def _(act):
            def body(b, first, following):
                act.wait_ge(norm.hn_transposed, b + 1)
                if not first:
                    act.wait_ge(unit_ready, b * NJ)
                lo = MOD_ROWS["ffn"]
                nc.scalar.activation(hT[:], norm_ps[:], ACT.Identity, bias=k.mod[1][:, lo[0], bass.ds(b, 1)],
                                     scale=k.mod[1][:, lo[1], bass.ds(b, 1)]).then_inc(hT_ready, 1)
                for j in range(NJ):
                    if not (first and j < 4):
                        act.wait_ge(out_added, b * NJ + j - 3)
                    act.wait_ge(unit_ready, b * NJ + j + 1)
                    nc.scalar.activation(relu[:, j % 4, :], unit_ps[j % 2][:], ACT.Relu, bias=k.b1c[:, j:j + 1],
                                         scale=k.w1c[:, j:j + 1]).then_inc(relu_ready, 1)

            run(act, body)

        @block.vector
        def _(dve):
            def body(b, first, following):
                if first:
                    norm.moments(dve, b)
                    norm.normalise(dve, b)
                if following:
                    norm.moments(dve, b + 1)
                    norm.normalise(dve, b + 1)
                every = [P, NT, D]
                xb = k.x[:, bass.ds(b * NT, NT), :]
                if not following:
                    dve.wait_ge(x_updated, b)
                dve.wait_ge(out_added, (b + 1) * NJ)
                nc.vector.tensor_tensor(biased[:], out_ps[:].rearrange("p (t d) -> p t d", t=NT), k.bout[:, None, :].to_broadcast(every),
                                        ALU.add).then_inc(biased_ready, 1)
                dve.wait_ge(biased_ready, b + 1)
                nc.vector.tensor_tensor(biased[:], biased[:], k.gate[1][:, 1, bass.ds(b, 1), :].to_broadcast(every),
                                        ALU.mult).then_inc(gated, 1)
                dve.wait_ge(gated, b + 1)
                nc.vector.tensor_tensor(xb, xb, biased[:], ALU.add).then_inc(x_updated, 1)

            run(dve, body)

        @block.gpsimd
        def _(pool):
            def body(b, first, following):
                if first:
                    norm.inverse_deviation(pool, b)
                if following:
                    norm.inverse_deviation(pool, b + 1)

            run(pool, body)


_INS = ["L0_attn_content", "L0_attn_Wq", "L0_attn_Wk", "L0_attn_Wv", "L0_ffn_W_router", "L0_ffn_W_gate", "L0_ffn_W_up",
        "L0_ffn_W_down", "L0_c", "L0_wmod", "L1_attn_W_Q", "L1_attn_W_K", "L1_attn_W_V", "L1_attn_W_O", "L1_ffn_Win",
        "L1_ffn_bin_", "L1_ffn_W1", "L1_ffn_b1", "L1_ffn_W2", "L1_ffn_b2", "L1_ffn_Wout", "L1_ffn_bout", "L1_c", "L1_wmod"]


def kernel(**inputs):
    import concourse.bacc as bacc
    from concourse.bass_utils import run_bass_kernel_spmd

    nc = bacc.Bacc("TRN2", target_bir_lowering=False, num_devices=1)
    packed, off, bf = constants()
    arrays = {f"in_{n}": np.ascontiguousarray(inputs[n]) for n in _INS}
    arrays["in_const_f32"], arrays["in_const_bf16"] = packed, bf
    arrays["in_const_ones"] = np.ones((3, H, T), mybir.dt.np(BF16))
    aps = {n[3:]: nc.dram_tensor(n, v.shape, mybir.dt.from_np(v.dtype), kind="ExternalInput").ap() for n, v in arrays.items()}
    out = nc.dram_tensor("out_x", (B, T, D), F32, kind="ExternalOutput").ap()
    adaln_kernel(nc, aps, out, off)
    r = run_bass_kernel_spmd(nc, [arrays], core_ids=[0])
    return r.results[0]["out_x"]
```

```python
from contextlib import ExitStack

import numpy as np

import concourse.bass as bass
from concourse import mybir

F32 = mybir.dt.float32
BF16 = mybir.dt.bfloat16
F16 = mybir.dt.float16
ALU = mybir.AluOpType
ACT = mybir.ActivationFunctionType
AX = mybir.AxisListType

P = 128
B, T, D = 8, 512, 128
NT = T // P
H = 16
HD = D // H
HG = 4
NG = H // HG
E, F = 8, 512
FT = F // P
M, INNER = 64, 16
NJ = M * INNER // P
EPS = 1e-5
GATE_MIN = 0.25
MASKED = -1e30
SCALE = float(HD) ** -0.5
ROWS = 9 * HD
SHIFT = ROWS
LEAD = 7
MODS = 6


def constants():
    f32 = {}
    f32["ident"] = np.eye(P, dtype=np.float32)
    perm = np.zeros((P, P), np.float32)
    rot = np.zeros((P, P), np.float32)
    half = HD // 2
    for h in range(H):
        for d in range(HD):
            perm[h * HD + d, d * H + h] = 1.0
            if d < half:
                rot[h * HD + d + half, d * H + h] = -1.0
            else:
                rot[h * HD + d - half, d * H + h] = 1.0
    f32["perm"], f32["rot"] = perm, rot
    theta = (np.float32(1.0) / np.float32(10000.0) ** (np.arange(0, HD, 2, dtype=np.float32) / np.float32(HD))).astype(np.float32)
    angle = np.outer(np.arange(T, dtype=np.float32), theta).astype(np.float32)
    angle = np.concatenate([angle, angle], axis=-1)
    f32["cos"] = np.repeat(np.cos(angle).T.astype(np.float32), H, axis=0)
    f32["sin"] = np.repeat(np.sin(angle).T.astype(np.float32), H, axis=0)
    den = np.zeros((P, 32), np.float32)
    den[:, HD] = 1.0
    f32["den_col"] = den
    before = (np.arange(E)[None, :] < np.arange(E)[:, None]).astype(np.float32)
    f32["before"] = np.broadcast_to(before.reshape(1, -1), (P, E * E))
    k = np.arange(P)
    f32["causal_t"] = (k[:, None] <= k[None, :]).astype(np.float32)
    unit = np.zeros((M, NJ * P), np.float32)
    unit[(np.arange(NJ * P) // INNER), np.arange(NJ * P)] = 1.0
    off, cols = {}, 0
    for name, a in f32.items():
        off[name] = (cols, a.shape[1])
        cols += a.shape[1]
    packed = np.ascontiguousarray(np.concatenate(list(f32.values()), axis=1), dtype=np.float32)
    later = k[None, :] > k[:, None]
    bf = np.concatenate([np.eye(P), np.where(later, MASKED, 0.0), np.where(later.T, MASKED, 0.0)], axis=1)
    return off, {"const_f32": packed, "const_bf16": bf.astype(mybir.dt.np(BF16)), "const_unit_of": unit,
                 "const_select": np.concatenate([unit, unit]).astype(np.float16),
                 "const_ones": np.ones((3, H, T), mybir.dt.np(BF16))}


def adaln_kernel(nc, a, out, const_off):
    with ExitStack() as ctx:
        k = Kernel(nc, ctx, a, out, const_off)
        with ExitStack() as experts_ctx:
            k.expert_raw = k.sb("expert_raw", [P, 3, E * FT, D], F32, experts_ctx)
            k.expert_loaded = [ctx.enter_context(nc.semaphore(f"expert_loaded{i}")) for i in range(3)]
            k.gates_loaded = ctx.enter_context(nc.semaphore("gates_loaded"))
            k.x_loaded = ctx.enter_context(nc.semaphore("x_loaded"))
            setup_phase(k)
            attention_phase(k, 0)
            experts_phase(k)
        attention_phase(k, 1)
        units_phase(k)


class Kernel:

    def __init__(self, nc, ctx, a, out, const_off):
        self.nc, self.ctx, self.a, self.out = nc, ctx, a, out
        self.x = self.sb("x_res", [P, B * NT, D], F32)
        width = sum(w for _, w in const_off.values())
        self.const = self.sb("consts", [P, width], F32)
        self.c = {n: self.const[:, o:o + w] for n, (o, w) in const_off.items()}
        self.cbf = self.sb("consts_bf16", [P, 3, P], BF16)
        self.eps = self.sb("eps", [P, NT], F32)
        self.minus_half = self.sb("minus_half", [P, NT], F32)
        self.mod = [self.sb(f"mod{l}", [P, 4, B], F32) for l in range(2)]
        self.gate = [self.sb(f"gate{l}", [P, 2, B, D], F32) for l in range(2)]
        self.w_qkv0 = self.sb("w_qkv0", [P, 3, D], F32)
        self.w_qk0 = self.sb("w_qk0", [P, 2, D], F32)
        self.w1 = self.sb("w1_proj", [P, 6, D], F32)
        self.router = self.sb("router_t", [P, E], F32)
        self.win_twice = self.sb("win_twice", [P, 2, M], F32)
        self.w1c = self.sb("w1_col", [P, NJ], F32)
        self.b1c = self.sb("b1_col", [P, NJ], F32)
        self.wout_rep = self.sb("wout_rep", [P, NJ, D], F32)
        self.bout = self.sb("bout_all", [P, D], F32)
        self.norm_buffers = [self.sb(f"norm_{name}", [P, NT, *rest], F32)
                             for name, rest in (("stats", [6]), ("mv", [2]), ("rstd", []), ("var_eps", []), ("normed", [D]))]
        self.norms = [Norm(self, ctx, tag) for tag in ("l0", "ex", "l1", "un")]

    def sb(self, name, shape, dt, ctx=None):
        return (ctx or self.ctx).enter_context(self.nc.sbuf_tensor(name, shape, dt))


MOD_ROWS = {"attn": (0, 1), "ffn": (2, 3)}


def setup_phase(k):
    nc, a = k.nc, k.a
    with ExitStack() as ctx:
        def sb(name, shape, dt=F32):
            return k.sb(name, shape, dt, ctx)

        def sem(name):
            return ctx.enter_context(nc.semaphore(name))

        ps = [ctx.enter_context(nc.psum_tensor(f"su_ps{i}", [P, 512], F32)) for i in range(4)]
        c_raw = sb("c_raw", [B, 2, D])
        wmod = sb("wmod", [P, 2, MODS * D])
        c_t = sb("c_t", [P, 2, B])
        c_e = sb("c_e", [P, 2, B])
        c_silu = sb("c_silu", [P, 2, B])
        gate_rows = sb("gate_rows", [B, 2, 2, D])
        gate_sign = sb("gate_sign", [B, 2, 2, D])
        gates_dram = nc.dram_tensor("gates_dram", [2, 2, B, D], F32).ap()
        w_raw = sb("w_raw", [P, 4, D])
        router_raw = sb("router_raw", [E, D])
        win_raw = sb("win_raw", [P, M])
        wout_raw = sb("wout_raw", [M, D + 1])
        b2_raw = sb("b2_raw", [M, 1])
        unit_raw = sb("unit_raw", [NJ, 3, P])
        unit_col = sb("unit_col", [P, 3, NJ])
        bout_raw = sb("bout_raw", [P, D])
        unit_of = sb("unit_of", [M, NJ * P])

        s_ident, s_const, s_c, s_wmod, s_x, s_w0, s_w, s_units, s_gates = (
            sem(f"su_{n}") for n in ("ident", "const", "c", "wmod", "x", "w0", "w", "units", "gates"))
        pe_done, dve_done, act_done, norm_constants = (sem(f"su_{n}") for n in ("pe", "dve", "act", "norm_constants"))
        PE_C, PE_MOD, PE_GATES, PE_QK, PE_TURNED, PE_UNITS = 1, 2, 3, 4, 5, 6
        DVE_C, DVE_SILU, DVE_GATES, DVE_TURNED, DVE_UNITS = 1, 4, 12, 17, 18

        with nc.Block() as block:
            @block.sync
            def _(sp):
                ident = P
                sp.dma_start(c_raw[:, 0, :], a["L0_c"]).then_inc(s_c, 16)
                sp.dma_start(c_raw[:, 1, :], a["L1_c"]).then_inc(s_c, 16)
                sp.dma_start(k.const[:, 0:ident], a["const_f32"][:, 0:ident]).then_inc(s_ident, 16)
                for l in range(2):
                    sp.dma_start(wmod[:, l, :], a[f"L{l}_wmod"]).then_inc(s_wmod, 16)
                for i, n in enumerate("qkv"):
                    sp.dma_start(k.w_qkv0[:, i, :], a[f"L0_attn_W{n}"]).then_inc(s_w0, 16)
                sp.dma_start(k.x[:, 0:NT, :], a["L0_attn_content"][0].rearrange("(t p) d -> p t d", p=P)).then_inc(s_x, 16)
                for i, n in enumerate(("Q", "K", "V", "O")):
                    sp.dma_start(w_raw[:, i, :], a[f"L1_attn_W_{n}"]).then_inc(s_w, 16)
                sp.dma_start(router_raw[:], a["L0_ffn_W_router"]).then_inc(s_w, 16)
                sp.dma_start(k.const[:, ident:], a["const_f32"][:, ident:]).then_inc(s_const, 16)
                sp.dma_start(k.cbf[:], a["const_bf16"].rearrange("p (i c) -> p i c", i=3)).then_inc(s_const, 16)
                sp.dma_start(k.x[:, NT:, :], a["L0_attn_content"][1:].rearrange("b (t p) d -> p (b t) d", p=P)).then_inc(k.x_loaded, 16)
                sp.wait_ge(dve_done, DVE_GATES)
                sp.dma_start(gates_dram.rearrange("l w b d -> b l w d"), gate_rows[:]).then_inc(s_gates, 16)
                sp.wait_ge(s_gates, 16)
                for l in range(2):
                    sp.dma_start(k.gate[l][:].rearrange("p w b d -> p (w b d)"),
                                 gates_dram[l].rearrange("w b d -> (w b d)").partition_broadcast(P)).then_inc(k.gates_loaded, 16)
                sp.wait_ge(s_x, 16)
                sp.wait_ge(s_const, 32)
                sp.wait_ge(s_w0, 48)

            @block.scalar
            def _(act):
                act.dma_start(win_raw[:], a["L1_ffn_Win"]).then_inc(s_units, 16)
                act.dma_start(unit_of[:], a["const_unit_of"]).then_inc(s_units, 16)
                act.dma_start(wout_raw[:, 0:D], a["L1_ffn_Wout"]).then_inc(s_units, 16)
                act.dma_start(wout_raw[:, D:D + 1], a["L1_ffn_bin_"].rearrange("(m o) -> m o", o=1)).then_inc(s_units, 16)
                act.dma_start(b2_raw[:], a["L1_ffn_b2"].rearrange("(m o) -> m o", o=1)).then_inc(s_units, 16)
                act.wait_ge(dve_done, DVE_C)
                nc.scalar.activation(c_e[:], c_t[:], ACT.Exp, scale=-1.0).then_inc(act_done, 1)
                for i, n in enumerate(("W1", "b1", "W2")):
                    act.dma_start(unit_raw[:, i, :], a[f"L1_ffn_{n}"].rearrange("(j a) h -> j (a h)", j=NJ)).then_inc(s_units, 16)
                act.dma_start(bout_raw[:], a["L1_ffn_bout"].partition_broadcast(P)).then_inc(s_units, 16)
                act.wait_ge(s_w0, 48)
                for i, scale in enumerate((SCALE, 1.0)):
                    nc.scalar.activation(k.w_qk0[:, i, :].rearrange("p (d h) -> p d h", h=H),
                                         k.w_qkv0[:, i, :].rearrange("p (h d) -> p d h", h=H), ACT.Copy, scale=scale).then_inc(act_done, 1)

            @block.gpsimd
            def _(pool):
                nc.gpsimd.memset(k.eps[:], EPS).then_inc(norm_constants, 1)
                nc.gpsimd.memset(k.minus_half[:], -0.5).then_inc(norm_constants, 1)
                pool.wait_ge(s_units, 144)
                nc.gpsimd.tensor_copy(k.win_twice[:], win_raw[:, None, :].to_broadcast([P, 2, M]))
                pool.wait_ge(norm_constants, 2)
                k.norms[0].inverse_deviation(pool, 0)

            @block.tensor
            def _(pe):
                pe.wait_ge(s_ident, 16)
                pe.wait_ge(s_c, 32)
                for l in range(2):
                    last = nc.tensor.transpose(ps[0][:, l * B:(l + 1) * B], c_raw[:, l, :], k.c["ident"][0:B, 0:B])
                last.then_inc(pe_done, 1)
                pe.wait_ge(dve_done, DVE_SILU)
                pe.wait_ge(s_wmod, 32)
                for l in range(2):
                    for n, j in enumerate((0, 1, 3, 4)):
                        last = nc.tensor.matmul(ps[0][:, (l * 4 + n) * B:(l * 4 + n + 1) * B], wmod[:, l, j * D:(j + 1) * D],
                                                c_silu[:, l, :], start=True, stop=True)
                last.then_inc(pe_done, 1)
                for l in range(2):
                    for w, j in enumerate((2, 5)):
                        last = nc.tensor.matmul(ps[3][0:B, (l * 2 + w) * D:(l * 2 + w + 1) * D], c_silu[:, l, :],
                                                wmod[:, l, j * D:(j + 1) * D], start=True, stop=True)
                last.then_inc(pe_done, 1)
                pe.wait_ge(s_w, 80)
                pe.wait_ge(s_const, 32)
                for n, (i, m) in enumerate(((0, "perm"), (0, "rot"), (1, "perm"), (1, "rot"))):
                    last = nc.tensor.matmul(ps[1][:, n * D:(n + 1) * D], w_raw[:, i, :], k.c[m], start=True, stop=True)
                last.then_inc(pe_done, 1)
                for n, i in enumerate((2, 3)):
                    nc.tensor.transpose(ps[2][:, n * D:(n + 1) * D], w_raw[:, i, :], k.c["ident"])
                nc.tensor.transpose(ps[2][:, 2 * D:2 * D + E], router_raw[:], k.c["ident"][0:E, 0:E])
                pe.wait_ge(s_units, 144)
                for i in range(3):
                    last = nc.tensor.transpose(ps[2][:, 2 * D + E + i * NJ:2 * D + E + (i + 1) * NJ], unit_raw[:, i, :],
                                               k.c["ident"][0:NJ, 0:NJ])
                last.then_inc(pe_done, 1)
                for j in range(NJ):
                    pe.wait_ge(dve_done, DVE_UNITS + 2 * (j - 2) + 1 if j >= 2 else DVE_TURNED)
                    nc.tensor.matmul(ps[1 + j % 2][:, 0:D + 1], unit_of[:, j * P:(j + 1) * P], wout_raw[:],
                                     start=True, stop=True).then_inc(pe_done, 1)
                nc.tensor.matmul(ps[3][:, 0:D], b2_raw[:, 0:1].to_broadcast([M, P]), wout_raw[:, 0:D],
                                 start=True, stop=True).then_inc(pe_done, 1)

            @block.vector
            def _(dve):
                n = [0]

                def link(ins):
                    n[0] += 1
                    ins.then_inc(dve_done, 1)
                    dve.wait_ge(dve_done, n[0])

                dve.wait_ge(pe_done, PE_C)
                link(nc.vector.tensor_copy(c_t[:], ps[0][:, 0:2 * B].rearrange("p (l b) -> p l b", l=2)))
                assert n[0] == DVE_C
                dve.wait_ge(act_done, 1)
                link(nc.vector.tensor_scalar(c_e[:], c_e[:], 1.0, None, ALU.add))
                link(nc.vector.reciprocal(c_e[:], c_e[:]))
                link(nc.vector.tensor_tensor(c_silu[:], c_t[:], c_e[:], ALU.mult))
                assert n[0] == DVE_SILU
                dve.wait_ge(pe_done, PE_MOD)
                for l in range(2):
                    v = ps[0][:, l * 4 * B:(l + 1) * 4 * B].rearrange("p (n b) -> p n b", n=4)
                    link(nc.vector.tensor_copy(k.mod[l][:], v))
                    link(nc.vector.tensor_scalar(k.mod[l][:, 1:4:2, :], k.mod[l][:, 1:4:2, :], 1.0, None, ALU.add))
                dve.wait_ge(pe_done, PE_GATES)
                g = ps[3][0:B, :].rearrange("b (l w d) -> b l w d", l=2, w=2)
                link(nc.vector.tensor_scalar(gate_sign[:], g, 0.0, 2.0, ALU.is_ge, ALU.mult))
                link(nc.vector.tensor_scalar(gate_rows[:], g, -1.0, GATE_MIN, ALU.mult, ALU.max))
                link(nc.vector.tensor_tensor(gate_rows[:], g, gate_rows[:], ALU.max))
                link(nc.vector.scalar_tensor_tensor(gate_rows[:], gate_sign[:], -1.0, gate_rows[:], ALU.add, ALU.mult))
                assert n[0] == DVE_GATES
                dve.wait_ge(s_x, 16)
                k.norms[0].moments(dve, 0)
                dve.wait_ge(pe_done, PE_TURNED)
                link(nc.vector.tensor_scalar(k.w1[:, 0:2, :], ps[1][:, 0:2 * D].rearrange("p (i d) -> p i d", i=2), SCALE, None, ALU.mult))
                link(nc.vector.tensor_copy(k.w1[:, 2:4, :], ps[1][:, 2 * D:].rearrange("p (i d) -> p i d", i=2)))
                link(nc.vector.tensor_copy(k.w1[:, 4:6, :], ps[2][:, 0:2 * D].rearrange("p (i d) -> p i d", i=2)))
                link(nc.vector.tensor_copy(k.router[:], ps[2][:, 2 * D:2 * D + E]))
                link(nc.vector.tensor_copy(unit_col[:], ps[2][:, 2 * D + E:2 * D + E + 3 * NJ].rearrange("p (i j) -> p i j", i=3)))
                assert n[0] == DVE_TURNED
                for j in range(NJ):
                    dve.wait_ge(pe_done, PE_UNITS + j)
                    pj = ps[1 + j % 2]
                    nc.vector.tensor_scalar(k.b1c[:, j:j + 1], pj[:, D:D + 1], unit_col[:, 0, j:j + 1], unit_col[:, 1, j:j + 1],
                                            ALU.mult, ALU.add).then_inc(dve_done, 1)
                    nc.vector.tensor_scalar(k.wout_rep[:, j, :], pj[:, 0:D], unit_col[:, 2, j:j + 1], None, ALU.mult).then_inc(dve_done, 1)
                n[0] += 2 * NJ
                dve.wait_ge(pe_done, PE_UNITS + NJ)
                dve.wait_ge(s_units, 144)
                link(nc.vector.tensor_copy(k.w1c[:], unit_col[:, 0, :]))
                link(nc.vector.tensor_tensor(k.bout[:], ps[3][:, 0:D], bout_raw[:], ALU.add))
                k.norms[0].normalise(dve, 0)


class Norm:

    def __init__(self, k, ctx, tag):
        self.k = k

        def sem(name):
            return ctx.enter_context(k.nc.semaphore(f"{tag}_{name}"))

        self.stats, self.mv, self.rstd, self.var_eps, self.hn = k.norm_buffers
        self.stats_seen = sem("stats_seen")
        self.stats_ready, self.mv_ready, self.eps_added, self.rstd_ready, self.hn_ready, self.hn_transposed = (
            sem(n) for n in ("stats", "mv", "eps", "rstd", "hn", "hn_transposed"))

    def moments_ahead(self, dve, last, x_updated):
        dve.wait_ge(last.hn_transposed, B)
        dve.wait_ge(x_updated, 1)
        self.moments(dve, 0)

    def moments(self, dve, b):
        nc, k = self.k.nc, self.k
        for t in range(NT):
            nc.vector.bn_stats(self.stats[:, t, :], k.x[:, b * NT + t, :]).then_inc(self.stats_ready, 1)
        dve.wait_ge(self.stats_ready, (b + 1) * NT)
        dve.sem_inc(self.stats_seen, 1)
        for t in range(NT):
            nc.vector.bn_aggr(self.mv[:, t, :], self.stats[:, t, :]).then_inc(self.mv_ready, 1)

    def inverse_deviation(self, pool, b):
        nc, k = self.k.nc, self.k
        pool.wait_ge(self.mv_ready, (b + 1) * NT)
        nc.gpsimd.tensor_tensor(self.var_eps[:], self.mv[:, :, 1], k.eps[:], ALU.add).then_inc(self.eps_added, 1)
        pool.wait_ge(self.eps_added, b + 1)
        nc.gpsimd.tensor_tensor(self.rstd[:], self.var_eps[:], k.minus_half[:], ALU.pow).then_inc(self.rstd_ready, 1)

    def normalise(self, dve, b):
        nc, k = self.k.nc, self.k
        dve.wait_ge(self.rstd_ready, b + 1)
        if not (isinstance(b, int) and b == 0):
            dve.wait_ge(self.hn_transposed, b)
        for t in range(NT):
            nc.vector.tensor_scalar(self.hn[:, t, :], k.x[:, b * NT + t, :], self.mv[:, t, 0:1], self.rstd[:, t:t + 1],
                                    ALU.subtract, ALU.mult).then_inc(self.hn_ready, 1)

    def transpose(self, pe, b, bank):
        nc, k = self.k.nc, self.k
        pe.wait_ge(self.hn_ready, (b + 1) * NT)
        for t in range(NT):
            last = nc.tensor.transpose(bank[:, t * P:(t + 1) * P], self.hn[:, t, :], k.c["ident"])
        last.then_inc(self.hn_transposed, 1)


def attention_phase(k, layer):
    nc = k.nc
    causal = layer == 1
    LATE = 0 if causal else 1
    L = f"l{layer}"
    with ExitStack() as ctx:
        def sb(name, shape, dt=F32):
            return k.sb(f"{L}_{name}", shape, dt, ctx)

        def sem(name):
            return ctx.enter_context(nc.semaphore(f"{L}_{name}"))

        def bank(name):
            return ctx.enter_context(nc.psum_tensor(f"{L}_{name}", [P, 512], F32))

        SCORE_BANKS = 3 if causal else 4
        score_ps = [bank(f"score{i}") for i in range(SCORE_BANKS)]
        shifted_ps = [bank(f"shifted{i}") for i in range(2)]
        o_ps = bank("o")
        proj_ps = bank("proj")
        turn_ps = bank("turn") if causal else proj_ps

        q_stack = sb("q_stack", [P, H, T], BF16)
        k_stack = sb("k_stack", [P, H, T], BF16)
        hT = sb("hT", [P, T])
        parts = sb("parts", [P, 2, 3, T], BF16)
        rest = sb("rest", [P, 2, T])
        v_next = sb("v_next", [P, NT, D])
        v_aug = sb("v_aug", [P, NT, H, 32])
        probs = sb("probs", [P, NT, HG, T])
        mx = sb("mx", [P, 2, HG * NT])
        shift = sb("shift", [HG * NT, 3, P], BF16)
        shift_rest = sb("shift_rest", [HG * NT, P])
        o_sb = sb("o_sb", [P, T])
        rden = sb("rden", [P, NT, HG])
        y = sb("y", [P, NT, D])
        gy = sb("gy", [P, NT, D])
        if causal:
            rope_a = sb("rope_a", [P, 2, T])
            rope_b = sb("rope_b", [P, 2, T])
            turned = sb("turned", [P, 2, T])
            yT = sb("yT", [P, NT, P])
        else:
            masked = sb("masked", [P, 2, HG, P])
            late_exp = sb("late_exp", [P, 2, (NT - 1) * P], BF16)
            late_sum = sb("late_sum", [P, NG, NT, HG])
            den = sb("den", [P, NT, HG])
        parts_dram = nc.dram_tensor(f"{L}_parts_dram", [B, 2, 5, P, T], BF16).ap()
        norm, next_norm = k.norms[2 * layer], k.norms[2 * layer + 1]

        ones_loaded = sem("ones_loaded")
        v_aug_cleared = sem("v_aug_cleared")
        hT_ready = sem("hT_ready")
        proj_ready = sem("proj_ready")
        proj_taken = sem("proj_taken")
        v_ready = sem("v_ready")
        v_taken = sem("v_taken")
        v_stored = sem("v_stored")
        hi_ready = sem("hi_ready")
        mid_ready = sem("mid_ready")
        lo_ready = sem("lo_ready")
        parts_stored = sem("parts_stored")
        stacked = [sem(f"stacked{g}") for g in range(NG)]
        score_ready = sem("score_ready")
        max_taken = sem("max_taken")
        max_turned = sem("max_turned")
        shift_step = sem("shift_step")
        shift_stacked = [sem(f"shift_stacked{g}") for g in range(NG)]
        shifted_ready = sem("shifted_ready")
        exp_done = sem("exp_done")
        summed = sem("summed")
        o_taken = sem("o_taken")
        o_turned = sem("o_turned")
        rden_ready = sem("rden_ready")
        y_ready = sem("y_ready")
        gy_ready = sem("gy_ready")
        x_updated = sem("x_updated")
        if causal:
            roped = sem("roped")
            rest_ready = sem("rest_ready")
            y_turned = sem("y_turned")
            yT_ready = sem("yT_ready")
            out_ready = sem("out_ready")
        else:
            diag_masked = sem("diag_masked")
            late_cleared = sem("late_cleared")
            late_done = sem("late_done")
            den_ready = sem("den_ready")

        NPROJ = 4 if causal else 2
        SCORE_BANK = [n % 3 for n in range(HG * NT - 1)] + [1] if causal else [n % SCORE_BANKS for n in range(HG * NT)]
        SCORE_REUSE = [next(d for d in range(1, 99) if SCORE_BANK[(n - d) % (HG * NT)] == SCORE_BANK[n]) for n in range(HG * NT)]
        UNITS, GROUPS, TILES = H * NT, NG, NG * NT
        MOMENTS, NORMALISE, TURN_NORM = ((2, 3), (3, 0), (3, 1)) if causal else ((2, 2), (2, 3), (3, 0))

        def lead_head(b, g, j, following):
            h = HG * g + j + LEAD
            if h < H:
                return b, h
            return (b + 1, h - H) if following else None

        def lead_group(b, g, following):
            if g + 1 < NG:
                return b, g + 1
            return (b + 1, 0) if following else None

        def run(engine, first, slot, finish):
            first()
            slot(0, 0, False, True, True)
            with engine.Fori(0, B - 2) as b:
                for g in range(1, NG):
                    slot(b, g, True, True, True)
                slot(b + 1, 0, True, True, True)
            for g in range(1, NG):
                slot(B - 2, g, True, True, False)
            for g in range(NG):
                slot(B - 1, g, True, False, False)
            finish(B - 1)

        def fronted(b, g, following, ahead):
            if g < 2:
                return b + 1 if following else None
            return b + 2 if ahead else None

        FIRST_BANKS = (score_ps + shifted_ps)[:NPROJ]

        def before(b, g):
            return b * GROUPS + g

        def rope_sum(engine, math, b, side):
            engine.wait_ge(proj_taken, b * NPROJ + 2 * side + 2)
            math.tensor_tensor(turned[:, side, :], rope_a[:, side, :], rope_b[:, side, :], ALU.add).then_inc(roped, 1)

        def rope_rest(engine, math, b, side):
            engine.wait_ge(hi_ready, b * 2 + side + 1)
            math.tensor_tensor(rest[:, side, :], turned[:, side, :], parts[:, side, 0, :], ALU.subtract).then_inc(rest_ready, 1)

        def low_part(engine, math, b, side):
            engine.wait_ge(mid_ready, b * 2 + side + 1)
            math.tensor_tensor(parts[:, side, 2, :], rest[:, side, :], parts[:, side, 1, :], ALU.subtract).then_inc(lo_ready, 1)

        block = ctx.enter_context(nc.Block())

        @block.sync
        def _(sp):
            def store_parts(b):
                sp.wait_ge(lo_ready, b * 2 + 1)
                sp.dma_start(parts_dram[b, 0, 0:3].rearrange("c p t -> p c t"), parts[:, 0]).then_inc(parts_stored, 16)
                sp.wait_ge(lo_ready, b * 2 + 2)
                sp.dma_start(parts_dram[b, 1, 0:3].rearrange("c p t -> p c t"), parts[:, 1]).then_inc(parts_stored, 16)
                sp.dma_start(parts_dram[b, 1, 3:5].rearrange("c p t -> p c t"), parts[:, 1, 0:2]).then_inc(parts_stored, 16)
                sp.wait_ge(parts_stored, (b + 1) * 48)

            def stack(b, g, prior):
                if prior:
                    sp.wait_ge(exp_done, (b - 1) * UNITS + (g + 1) * HG * NT)
                rows = 3 * HD
                for s in range(3):
                    for side, dst, first in ((0, q_stack, 0), (1, k_stack, s)):
                        src = parts_dram[b, side].rearrange("c (d h) t -> (c d) h t", d=HD)
                        sp.dma_start(dst[rows * s:rows * (s + 1), HG * g:HG * (g + 1), :],
                                     src[HD * first:HD * first + rows, HG * g:HG * (g + 1), :]).then_inc(stacked[g], 16)

            def stack_shift(b, g):
                sp.wait_ge(shift_step, 4 * before(b, g) + 4)
                for c in range(3):
                    sp.dma_start(q_stack[SHIFT + c:SHIFT + c + 1, HG * g:HG * (g + 1), :].rearrange("c h (q t) -> c (h q) t", t=P),
                                 shift[:, c, :]).then_inc(shift_stacked[g], 16)

            def load_experts(sp):
                for i, name in enumerate(("gate", "up")):
                    sp.dma_start(k.expert_raw[:, i], k.a[f"L0_ffn_W_{name}"].rearrange("e (f p) d -> p (e f) d",
                                                                                       p=P)).then_inc(k.expert_loaded[i], 16)
                sp.dma_start(k.expert_raw[:, 2].rearrange("p (e f) c -> p e (f c)", e=E),
                             k.a["L0_ffn_W_down"].rearrange("e d f -> d e f")).then_inc(k.expert_loaded[2], 16)

            def first():
                sp.dma_start(k_stack[SHIFT:SHIFT + 3], k.a["const_ones"]).then_inc(ones_loaded, 16)
                store_parts(0)
                for g in range(NG - 1):
                    stack(0, g, False)
                stack_shift(0, 0)
                if layer == 0:
                    load_experts(sp)

            def slot(b, g, prev, following, ahead):
                if g == 1 and following:
                    store_parts(b + 1)
                led = lead_group(b, g, following)
                if led:
                    stack_shift(*led)
                if g == 0:
                    stack(b, NG - 1, prev)
                elif following:
                    stack(b + 1, g - 1, True)

            run(sp, first, slot, lambda b: None)

        @block.tensor
        def _(pe):
            if causal:
                weights = [k.w1[:, i, :] for i in range(4)]
                wv = k.w1[:, 4, :]
            else:
                weights = [k.w_qk0[:, i, :] for i in range(2)]
                wv = k.w_qkv0[:, 2, :]

            def turn_norm(b, prior):
                if prior:
                    pe.wait_ge(v_taken, b)
                norm.transpose(pe, b, proj_ps)

            def project_qk(b, which, bank=proj_ps, warm=True):
                if which == 0:
                    pe.wait_ge(hT_ready, b + 1)
                elif warm:
                    pe.wait_ge(proj_taken, b * NPROJ + which)
                nc.tensor.matmul(bank[:], weights[which], hT[:], start=True, stop=True).then_inc(proj_ready, 1)

            def project_v(b, warm=True):
                if warm:
                    pe.wait_ge(proj_taken, (b + 1) * NPROJ)
                for t in range(NT):
                    last = nc.tensor.matmul(proj_ps[:, t * P:(t + 1) * P], hT[:, t * P:(t + 1) * P], wv, start=True, stop=True)
                last.then_inc(v_ready, 1)

            def score(b, h, qt, warm):
                n = b * UNITS + h * NT + qt
                if h % HG == 0 and qt == 0:
                    pe.wait_ge(stacked[h // HG], (b + 1) * 96)
                m = h % HG * NT + qt
                if warm:
                    back = SCORE_REUSE[m]
                    if (m - back) % NT < LATE:
                        pe.wait_ge(late_done, (b * H + h + (qt - back) // NT) * LATE + (qt - back) % NT + 1)
                    else:
                        pe.wait_ge(max_taken, n + 1 - back)
                cols = (qt + 1) * P if causal else T
                bank_of_unit = score_ps[SCORE_BANK[m]]
                last = nc.tensor.matmul(bank_of_unit[:, 0:cols], q_stack[0:ROWS, h, qt * P:(qt + 1) * P], k_stack[0:ROWS, h, 0:cols],
                                        start=True, stop=not causal)
                if causal:
                    last = nc.tensor.matmul(bank_of_unit[:, qt * P:cols], k.cbf[:, 0, :], k.cbf[:, 1, :],
                                            start=False, stop=True)
                last.then_inc(score_ready, 1)

            def shifted(b, g, kt, i, warm):
                n = b * UNITS + g * HG * NT + kt * HG + i
                h = HG * g + i
                if kt == 0 and i == 0:
                    pe.wait_ge(shift_stacked[g], (b + 1) * 48)
                if warm:
                    pe.wait_ge(exp_done, n - 1)
                lo = kt * P if causal else min(kt, LATE) * P
                dst = shifted_ps[i % 2]
                last = nc.tensor.matmul(dst[:, lo:T], k_stack[0:SHIFT + 3, h, kt * P:(kt + 1) * P], q_stack[0:SHIFT + 3, h, lo:T],
                                        start=True, stop=not causal)
                if causal:
                    last = nc.tensor.matmul(dst[:, lo:lo + P], k.cbf[:, 0, :], k.cbf[:, 2, :], start=False, stop=True)
                last.then_inc(shifted_ready, 1)

            def sum_tile(b, g, kt):
                u = b * TILES + g * NT + kt
                if kt == 0:
                    if g > 0 or not isinstance(b, int) or b > 0:
                        pe.wait_ge(o_taken, before(b, g))
                    if g == 0:
                        pe.wait_ge(v_stored, b + 1)
                pe.wait_ge(exp_done, (u + 1) * HG)

                def heads(lhs, rhs, lo, hi, m, start, stop):
                    for i in range(HG):
                        ins = nc.tensor.matmul(o_ps[32 * i:32 * i + m, lo:hi], lhs(i), rhs(i), start=start, stop=stop,
                                               skip_group_check=True, tile_position=(0, 32 * i))
                    return ins

                def values(i):
                    return v_aug[:, kt, HG * g + i, :]

                diag = kt * P
                if causal:
                    last = heads(values, lambda i: probs[:, kt, i, diag:T], diag, T, 32, kt == 0, kt == NT - 1)
                else:
                    lo = min(kt, LATE) * P
                    last = heads(lambda i: k.c["den_col"], lambda i: probs[:, kt, i, lo:diag + P], lo, diag + P, 32, kt == 0, False)
                    if kt + 1 < NT:
                        last = heads(values, lambda i: probs[:, kt, i, diag + P:T], diag + P, T, 32, False, False)
                    pe.wait_ge(diag_masked, u + 1)
                    last = heads(lambda i: v_aug[:, kt, HG * g + i, 0:HD], lambda i: masked[:, kt % 2, i, :], diag, diag + P, HD,
                                 False, kt == NT - 1)
                last.then_inc(summed, 1)

            def turn_max(b, g):
                pe.wait_ge(max_taken, b * UNITS + (g + 1) * HG * NT)
                nc.tensor.transpose(turn_ps[0:HG * NT, 0:P], mx[:, g % 2, :], k.c["ident"]).then_inc(max_turned, 1)

            def turn_sums(b, g):
                pe.wait_ge(o_taken, before(b, g) + 1)
                if isinstance(b, int) and b == B - 1 and g >= NG - 2:
                    pe.wait_ge(y_ready, before(b, g))
                else:
                    pe.wait_ge(shift_step, 4 * before(b, g) + 12)
                for t in range(NT):
                    last = nc.tensor.transpose(turn_ps[:, t * P:(t + 1) * P], o_sb[:, t * P:(t + 1) * P], k.c["ident"])
                last.then_inc(o_turned, 1)

            def turn_y(b):
                pe.wait_ge(y_ready, (b + 1) * GROUPS)
                for t in range(NT):
                    last = nc.tensor.transpose(turn_ps[:, t * P:(t + 1) * P], y[:, t, :], k.c["ident"])
                last.then_inc(y_turned, 1)

            def project_out(b):
                pe.wait_ge(yT_ready, b + 1)
                for t in range(NT):
                    last = nc.tensor.matmul(turn_ps[:, t * P:(t + 1) * P], yT[:, t, :], k.w1[:, 5, :], start=True, stop=True)
                last.then_inc(out_ready, 1)

            def front(s, g, j):
                if (g, j) == TURN_NORM:
                    turn_norm(s, True)
                elif (g, j) == (3, 2):
                    if not causal and not (isinstance(s, int) and s == 1):
                        pe.wait_ge(y_ready, before(s - 2, 3))
                    project_qk(s, 0)
                elif causal and (g, j) in ((3, 3), (0, 0), (0, 1)):
                    project_qk(s, {(3, 3): 1, (0, 0): 2, (0, 1): 3}[g, j])
                elif not causal and (g, j) == (0, 0):
                    project_qk(s, 1)
                elif (g, j) == (0, 2):
                    if not causal and isinstance(s, int) and s == 1:
                        pe.wait_ge(shift_step, 8)
                    elif not causal:
                        pe.wait_ge(y_ready, before(s - 1, 0))
                    project_v(s)

            def first():
                turn_norm(0, False)
                for which in range(NPROJ):
                    project_qk(0, which, FIRST_BANKS[which], False)
                project_v(0, False)
                for j in range(NT):
                    front(1, NG - 1, j)
                pe.wait_ge(proj_taken, NPROJ)
                for h in range(LEAD):
                    for qt in range(NT):
                        score(0, h, qt, h * NT + qt >= 3)
                    if h == HG:
                        if not causal:
                            pe.wait_ge(proj_taken, NPROJ + 1)
                        turn_max(0, 0)
                pe.wait_ge(ones_loaded, 16)

            def slot(b, g, prev, following, ahead):
                for j in range(NT):
                    warm = prev or j > 0
                    led = lead_head(b, g, j, following)

                    def lead(qt):
                        if led:
                            score(*led, qt, True)

                    shifted(b, g, j, 0, warm)
                    lead(0)
                    shifted(b, g, j, 1, warm)
                    lead(1)
                    s = fronted(b, g, following, ahead)
                    if j == 1 and lead_group(b, g, following):
                        if not causal and s is not None:
                            if g == 3:
                                pe.wait_ge(hT_ready, s + 1)
                            if g == 0:
                                pe.wait_ge(proj_taken, (s + 1) * NPROJ)
                            if g == 1:
                                pe.wait_ge(v_taken, s + 1)
                        turn_max(*lead_group(b, g, following))
                    if j > 0:
                        sum_tile(b, g, j - 1)
                    elif prev:
                        sum_tile(*((b, g - 1) if g else (b - 1, NG - 1)), NT - 1)
                    shifted(b, g, j, 2, True)
                    lead(2)
                    shifted(b, g, j, 3, True)
                    lead(3)
                    if prev and j == 1:
                        turn_sums(*((b, g - 1) if g else (b - 1, NG - 1)))
                    if s is not None:
                        front(s, g, j)
                    if causal and prev and g == 0:
                        if j == 2:
                            turn_y(b - 1)
                        if j == 3:
                            project_out(b - 1)

            def finish(b):
                sum_tile(b, NG - 1, NT - 1)
                turn_sums(b, NG - 1)
                if causal:
                    turn_y(b)
                    project_out(b)

            run(pe, first, slot, finish)

        @block.scalar
        def _(act):
            def store_hT(b):
                lo = MOD_ROWS["attn"]
                act.wait_ge(norm.hn_transposed, b + 1)
                nc.scalar.activation(hT[:], proj_ps[:], ACT.Identity, bias=k.mod[layer][:, lo[0], bass.ds(b, 1)],
                                     scale=k.mod[layer][:, lo[1], bass.ds(b, 1)]).then_inc(hT_ready, 1)

            def high_part(b, side, bank=proj_ps):
                if causal:
                    act.wait_ge(roped, b * 2 + side + 1)
                    nc.scalar.copy(parts[:, side, 0, :], turned[:, side, :]).then_inc(hi_ready, 1)
                else:
                    act.wait_ge(proj_ready, b * NPROJ + side + 1)
                    nc.scalar.copy(parts[:, side, 0, :], bank[:]).then_inc(hi_ready, 1)

            def store_v(b):
                act.wait_ge(v_taken, b + 1)
                nc.scalar.copy(v_aug[:, :, :, 0:HD], v_next[:].rearrange("p t (h d) -> p t h d", h=H)).then_inc(v_stored, 1)

            def take_v(b):
                act.wait_ge(v_ready, b + 1)
                nc.scalar.copy(v_next[:], proj_ps[:].rearrange("p (t d) -> p t d", t=NT)).then_inc(v_taken, 1)

            def take_sums(b, g):
                act.wait_ge(summed, (before(b, g) + 1) * NT)
                nc.scalar.copy(o_sb[:], o_ps[:]).then_inc(o_taken, 1)

            def exponential(b, g, kt, i, warm):
                n = b * UNITS + g * HG * NT + kt * HG + i
                if i == 0 and warm:
                    act.wait_ge(summed, before(b, g) * NT + kt - NT + 1)
                act.wait_ge(shifted_ready, n + 1)
                lo = kt * P if causal else min(kt, LATE) * P
                nc.scalar.activation(probs[:, kt, i, lo:T], shifted_ps[i % 2][:, lo:T], ACT.Exp).then_inc(exp_done, 1)

            def late_keys(b, h, qt):
                g, i = h // HG, h % HG
                act.wait_ge(max_taken, b * UNITS + h * NT + qt + 1)
                nc.scalar.activation(late_exp[:, qt % 2, 0:T - (qt + 1) * P], score_ps[SCORE_BANK[i * NT + qt]][:, (qt + 1) * P:], ACT.Exp,
                                     bias=mx[:, g % 2, i * NT + qt:i * NT + qt + 1],
                                     accum_out=late_sum[:, g, qt, i:i + 1]).then_inc(late_done, 1)

            def store_yT(b):
                act.wait_ge(y_turned, b + 1)
                nc.scalar.copy(yT[:], turn_ps[:].rearrange("p (t q) -> p t q", t=NT)).then_inc(yT_ready, 1)

            def front(s, g, j):
                if (g, j) == TURN_NORM:
                    store_hT(s)
                if (g, j) == ((0, 0) if causal else (3, 2)):
                    high_part(s, 0)
                if (g, j) == ((0, 2) if causal else (0, 0)):
                    high_part(s, 1)
                if (g, j) == ((0, 3) if causal else (0, 2)):
                    take_v(s)

            def first():
                store_hT(0)
                high_part(0, 0, FIRST_BANKS[0])
                if causal:
                    take_v(0)
                high_part(0, 1, FIRST_BANKS[1])
                if not causal:
                    take_v(0)
                if not causal:
                    act.wait_ge(parts_stored, 48)
                for j in range(NT):
                    front(1, NG - 1, j)
                if not causal:
                    act.wait_ge(late_cleared, 1)
                for h in range(LEAD):
                    for qt in range(LATE):
                        late_keys(0, h, qt)
                act.wait_ge(v_aug_cleared, 1)

            def slot(b, g, prev, following, ahead):
                for j in range(NT):
                    led = lead_head(b, g, j, following)
                    for i in range(HG):
                        exponential(b, g, j, i, prev)
                        if led and 1 <= i <= LATE:
                            late_keys(*led, i - 1)
                    if j == 0:
                        if prev:
                            take_sums(*((b, g - 1) if g else (b - 1, NG - 1)))
                        if g == 0:
                            store_v(b)
                    s = fronted(b, g, following, ahead)
                    if s is not None:
                        front(s, g, j)
                    if causal and prev and (g, j) == (0, 2):
                        store_yT(b - 1)

            def finish(b):
                take_sums(b, NG - 1)
                if causal:
                    store_yT(b)

            run(act, first, slot, finish)

        @block.vector
        def _(dve):
            def row_max(b, h, qt):
                dve.wait_ge(score_ready, b * UNITS + h * NT + qt + 1)
                cols = (qt + 1) * P if causal else T
                g, i = h // HG, h % HG
                nc.vector.tensor_reduce(mx[:, g % 2, i * NT + qt:i * NT + qt + 1], score_ps[SCORE_BANK[i * NT + qt]][:, 0:cols],
                                        AX.X, ALU.max, negate=True).then_inc(max_taken, 1)

            def split_shift(b, g, prior):
                n = before(b, g)
                dve.wait_ge(max_turned, n + 1)
                if prior:
                    prior_b, prior_g = (b, g - 1) if g else (b - 1, NG - 1)
                    dve.wait_ge(shift_stacked[prior_g], (prior_b + 1) * 48)
                m = turn_ps[0:HG * NT, 0:P]
                nc.vector.tensor_copy(shift[:, 0, :], m).then_inc(shift_step, 1)
                dve.wait_ge(shift_step, 4 * n + 1)
                nc.vector.tensor_tensor(shift_rest[:], m, shift[:, 0, :], ALU.subtract).then_inc(shift_step, 1)
                dve.wait_ge(shift_step, 4 * n + 2)
                nc.vector.tensor_copy(shift[:, 1, :], shift_rest[:]).then_inc(shift_step, 1)
                dve.wait_ge(shift_step, 4 * n + 3)
                nc.vector.tensor_tensor(shift[:, 2, :], shift_rest[:], shift[:, 1, :], ALU.subtract).then_inc(shift_step, 1)

            def divide(b, g):
                n = before(b, g)
                dve.wait_ge(o_turned, n + 1)
                s = turn_ps[:].rearrange("p (t i r) -> p t i r", t=NT, i=HG)
                sums = s[:, :, :, HD]
                if LATE:
                    nc.vector.tensor_tensor(den[:], sums, late_sum[:, g], ALU.add).then_inc(den_ready, 1)
                    dve.wait_ge(den_ready, n + 1)
                    sums = den[:]
                nc.vector.reciprocal(rden[:], sums).then_inc(rden_ready, 1)
                dve.wait_ge(rden_ready, n + 1)
                nc.vector.tensor_tensor(y[:].rearrange("p t (h d) -> p t h d", h=H)[:, :, HG * g:HG * (g + 1), :], s[:, :, :, 0:HD],
                                        rden[:, :, :, None].to_broadcast([P, NT, HG, HD]), ALU.mult).then_inc(y_ready, 1)

            def rope_product(b, which, bank=proj_ps):
                dst, factor = ((rope_a, k.c["cos"]), (rope_b, k.c["sin"]))[which % 2]
                dve.wait_ge(proj_ready, b * NPROJ + which + 1)
                nc.vector.tensor_tensor(dst[:, which // 2, :], bank[:], factor, ALU.mult).then_inc(proj_taken, 1)

            def what_is_left(b, side, bank=proj_ps):
                dve.wait_ge(hi_ready, b * 2 + side + 1)
                nc.vector.tensor_tensor(rest[:, side, :], bank[:], parts[:, side, 0, :], ALU.subtract).then_inc(proj_taken, 1)

            def middle_part(b, side):
                n = b * 2 + side
                if causal:
                    dve.wait_ge(rest_ready, n + 1)
                else:
                    dve.wait_ge(proj_taken, n + 1)
                nc.vector.tensor_copy(parts[:, side, 1, :], rest[:, side, :]).then_inc(mid_ready, 1)

            def scale_out(b):
                if isinstance(b, int):
                    dve.wait_ge(x_updated, b)
                dve.wait_ge(out_ready, b + 1)
                nc.vector.tensor_tensor(gy[:], turn_ps[:].rearrange("p (t d) -> p t d", t=NT),
                                        k.gate[layer][:, 0, bass.ds(b, 1), :].to_broadcast([P, NT, D]), ALU.mult).then_inc(gy_ready, 1)

            def front(s, g, j):
                if (g, j) == MOMENTS:
                    norm.moments(dve, s)
                if (g, j) == NORMALISE:
                    norm.normalise(dve, s)
                if causal:
                    if (g, j) in ((3, 2), (3, 3), (0, 0), (0, 1)):
                        rope_product(s, {(3, 2): 0, (3, 3): 1, (0, 0): 2, (0, 1): 3}[g, j])
                    if (g, j) == (0, 1):
                        middle_part(s, 0)
                    if (g, j) == (0, 3):
                        middle_part(s, 1)
                elif (g, j) in ((3, 2), (0, 0)):
                    side = 0 if g else 1
                    what_is_left(s, side)
                    middle_part(s, side)

            def first():
                if not causal:
                    nc.vector.memset(late_sum[:], 0.0).then_inc(late_cleared, 1)
                    dve.wait_ge(k.x_loaded, 16)
                norm.moments(dve, 1)
                if causal:
                    norm.normalise(dve, 1)
                    for side in range(2):
                        rope_product(0, 2 * side, FIRST_BANKS[2 * side])
                        rope_product(0, 2 * side + 1, FIRST_BANKS[2 * side + 1])
                        rope_sum(dve, nc.vector, 0, side)
                    for side in range(2):
                        rope_rest(dve, nc.vector, 0, side)
                        middle_part(0, side)
                        low_part(dve, nc.vector, 0, side)
                    dve.wait_ge(rest_ready, 2)
                else:
                    for side in range(2):
                        what_is_left(0, side, FIRST_BANKS[side])
                        middle_part(0, side)
                        low_part(dve, nc.vector, 0, side)
                    norm.normalise(dve, 1)
                    dve.wait_ge(parts_stored, 48)
                for j in range(1, NT):
                    front(1, NG - 1, j)
                for h in range(LEAD):
                    for qt in range(NT):
                        row_max(0, h, qt)
                    if h == HG:
                        split_shift(0, 0, False)

            def slot(b, g, prev, following, ahead):
                for j in range(NT):
                    led = lead_head(b, g, j, following)
                    for qt in range(NT):
                        if led:
                            row_max(*led, qt)
                        if j == 1 and qt == 1 and lead_group(b, g, following):
                            split_shift(*lead_group(b, g, following), True)
                    if prev and j == 1:
                        divide(*((b, g - 1) if g else (b - 1, NG - 1)))
                    s = fronted(b, g, following, ahead)
                    if s is not None:
                        front(s, g, j)
                    if prev and (g, j) == (0, 3):
                        if causal:
                            scale_out(b - 1)
                        else:
                            dve.wait_ge(gy_ready, b)

                    if not following and (g, j) == (3, 2):
                        next_norm.moments_ahead(dve, norm, x_updated)
                    if not following and (g, j) == (3, 3):
                        next_norm.normalise(dve, 0)

            def finish(b):
                divide(b, NG - 1)
                if causal:
                    scale_out(b)

            run(dve, first, slot, finish)

        @block.gpsimd
        def _(pool):
            def mask_diagonal(b, g, kt):
                pool.wait_ge(exp_done, (b * TILES + g * NT + kt + 1) * HG)
                nc.gpsimd.tensor_tensor(masked[:, kt % 2], probs[:, kt, :, kt * P:(kt + 1) * P],
                                        k.c["causal_t"][:, None, :].to_broadcast([P, HG, P]), ALU.mult).then_inc(diag_masked, 1)

            def update_x(b):
                xb = k.x[:, bass.ds(b * NT, NT), :]
                if not causal:
                    pool.wait_ge(y_ready, (b + 1) * GROUPS)
                    nc.gpsimd.tensor_tensor(gy[:], y[:], k.gate[layer][:, 0, bass.ds(b, 1), :].to_broadcast([P, NT, D]),
                                            ALU.mult).then_inc(gy_ready, 1)
                pool.wait_ge(gy_ready, b + 1)
                nc.gpsimd.tensor_tensor(xb, xb, gy[:], ALU.add).then_inc(x_updated, 1)

            def split_side(b, side):
                if causal:
                    rope_sum(pool, nc.gpsimd, b, side)
                    rope_rest(pool, nc.gpsimd, b, side)
                low_part(pool, nc.gpsimd, b, side)

            def front(s, g, j):
                if (g, j) == MOMENTS:
                    norm.inverse_deviation(pool, s)
                if (g, j) == ((0, 0) if causal else (3, 2)):
                    split_side(s, 0)
                if (g, j) == ((0, 2) if causal else (0, 0)):
                    split_side(s, 1)

            def first():
                if not causal:
                    pool.wait_ge(k.gates_loaded, 32)
                norm.inverse_deviation(pool, 1)
                for j in range(1, NT):
                    front(1, NG - 1, j)
                nc.gpsimd.tensor_copy(v_aug[:].rearrange("p t h r -> p (t h) r"),
                                      k.c["den_col"][:, None, :].to_broadcast([P, NT * H, 32])).then_inc(v_aug_cleared, 1)

            def slot(b, g, prev, following, ahead):
                for j in range(NT):
                    if not causal:
                        mask_diagonal(b, g, j)
                    s = fronted(b, g, following, ahead)
                    if s is not None:
                        front(s, g, j)
                    if prev and (g, j) == (0, 1) and not causal:
                        update_x(b - 1)
                    if prev and (g, j) == (0, 3) and causal:
                        update_x(b - 1)
                    if not following and (g, j) == (3, 2):
                        next_norm.inverse_deviation(pool, 0)

            run(pool, first, slot, update_x)


def experts_phase(k):
    nc = k.nc
    LAG, STEPS = 3, E * FT
    H_SCALE, W_SCALE, HID_SCALE = 8.0, 64.0, 2.0
    PROJ_SCALE = H_SCALE * W_SCALE
    ROUTER_STEPS = 14
    with ExitStack() as ctx:
        def sb(name, shape, dt=F32):
            return k.sb(f"ex_{name}", shape, dt, ctx)

        def sem(name):
            return ctx.enter_context(nc.semaphore(f"ex_{name}"))

        def bank(name):
            return ctx.enter_context(nc.psum_tensor(f"ex_{name}", [P, 512], F32))

        gate_ps = [bank(f"gate{i}") for i in range(2)]
        up_ps = [bank(f"up{i}") for i in range(2)]
        down_ps = [bank(f"down{i}") for i in range(2)]
        norm_ps = bank("norm")
        logit_ps = bank("logit")

        raw = k.expert_raw
        w_hi = sb("w_hi", [P, 3, STEPS, D], F16)
        w_lo = sb("w_lo", [P, 3, STEPS, D], F16)
        hT = sb("hT", [P, T])
        h_hi = sb("h_hi", [P, 2, T], F16)
        h_lo = sb("h_lo", [P, 2, T], F16)
        th = sb("tanh", [P, 2, T])
        half = sb("half", [P, 2, T])
        hid = sb("hid", [P, 2, T])
        hid_hi = sb("hid_hi", [P, 4, T], F16)
        hid_lo = sb("hid_lo", [P, 4, T], F16)
        acc = sb("acc", [P, NT, D])
        shifted = sb("shifted", [P, NT, E])
        prob = sb("prob", [P, NT, E])
        top = sb("top", [P, NT])
        total = sb("total", [P, NT])
        above = sb("above", [P, NT, E, E])
        tied = sb("tied", [P, NT, E, E])
        rank = sb("rank", [P, NT, E])
        weight = sb("weight", [P, 2, NT, E])
        norm, next_norm = k.norms[1], k.norms[2]

        w_turned = sem("w_turned")
        w_hi_stored = sem("w_hi_stored")
        w_lo_stored = sem("w_lo_stored")
        hT_ready = sem("hT_ready")
        logits_ready = sem("logits_ready")
        exps_ready = sem("exps_ready")
        router_step = sem("router_step")
        gate_ready = sem("gate_ready")
        up_ready = sem("up_ready")
        tanh_ready = sem("tanh_ready")
        silu_ready = sem("silu_ready")
        hid_ready = sem("hid_ready")
        hid_hi_ready = sem("hid_hi_ready")
        hid_lo_ready = sem("hid_lo_ready")
        h_hi_ready = sem("h_hi_ready")
        h_lo_ready = sem("h_lo_ready")
        down_done = sem("down_done")
        combined = sem("combined")
        gated = sem("gated")
        x_updated = sem("x_updated")

        QUADS = 3 * STEPS // 4
        banks = gate_ps + up_ps

        def run(engine, body):
            body(0, 0, True, True)
            with engine.Fori(0, (B - 2) // 2) as pair:
                body(pair * 2 + 1, 1, False, True)
                body(pair * 2 + 2, 0, False, True)
            body(B - 1, (B - 1) % 2, False, False)

        block = ctx.enter_context(nc.Block())

        @block.tensor
        def _(pe):
            for q in range(QUADS):
                which, step = divmod(q * 4, STEPS)
                if step == 0:
                    pe.wait_ge(k.expert_loaded[which], 16)
                if q >= 4:
                    pe.wait_ge(w_lo_stored, q - 3)
                for i in range(4):
                    last = nc.tensor.transpose(banks[q % 4][:, i * P:(i + 1) * P], raw[:, which, step + i, :], k.c["ident"])
                last.then_inc(w_turned, 1)
                if q == 4:
                    norm.transpose(pe, 0, norm_ps)
            pe.wait_ge(w_lo_stored, QUADS)

            def project(bank, which, n, odd):
                nc.tensor.matmul(bank[:], w_lo[:, which, n, :], h_hi[:, odd, :], start=True, stop=False)
                nc.tensor.matmul(bank[:], w_hi[:, which, n, :], h_lo[:, odd, :], start=False, stop=False)
                return nc.tensor.matmul(bank[:], w_hi[:, which, n, :], h_hi[:, odd, :], start=False, stop=True)

            def gate_up(b, n, warm, odd):
                if warm:
                    pe.wait_ge(silu_ready, b * STEPS + n - 1)
                project(gate_ps[n % 2], 0, n, odd).then_inc(gate_ready, 1)
                if warm:
                    pe.wait_ge(hid_ready, b * STEPS + n - 1)
                project(up_ps[n % 2], 1, n, odd).then_inc(up_ready, 1)

            def down(b, n, warm):
                e, f = divmod(n, FT)
                if f == 0 and warm:
                    pe.wait_ge(combined, b * E + e - 1)
                pe.wait_ge(hid_lo_ready, b * STEPS + n + 1)
                for t in range(NT):
                    tokens = slice(t * P, (t + 1) * P)
                    y = down_ps[e % 2][:, tokens]
                    nc.tensor.matmul(y, hid_lo[:, n % 4, tokens], w_hi[:, 2, n, :], start=(f == 0 and t == 0), stop=False,
                                     skip_group_check=True)
                    nc.tensor.matmul(y, hid_hi[:, n % 4, tokens], w_lo[:, 2, n, :], start=False, stop=False, skip_group_check=True)
                    last = nc.tensor.matmul(y, hid_hi[:, n % 4, tokens], w_hi[:, 2, n, :], start=False, stop=(f == FT - 1),
                                            skip_group_check=True)
                last.then_inc(down_done, 1)

            def route(b):
                pe.wait_ge(hT_ready, b + 1)
                for t in range(NT):
                    last = nc.tensor.matmul(logit_ps[:, t * E:(t + 1) * E], hT[:, t * P:(t + 1) * P], k.router[:], start=True, stop=True)
                last.then_inc(logits_ready, 1)

            def body(b, odd, first, following):
                if first:
                    route(b)
                pe.wait_ge(h_lo_ready, b + 1)
                for n in range(STEPS):
                    gate_up(b, n, not first or n >= 2, odd)
                    if n >= LAG:
                        down(b, n - LAG, not first or n - LAG >= 2 * FT)
                    elif not first:
                        down(b - 1, STEPS - LAG + n, True)
                    if following:
                        if n == 16:
                            norm.transpose(pe, b + 1, norm_ps)
                        if n == 22:
                            route(b + 1)
                if not following:
                    for n in range(STEPS - LAG, STEPS):
                        down(b, n, True)

            run(pe, body)

        @block.scalar
        def _(act):
            def store_hT(b, odd):
                act.wait_ge(norm.hn_transposed, b + 1)
                if not (isinstance(b, int) and b == 0):
                    act.wait_ge(logits_ready, b)
                lo = MOD_ROWS["ffn"]
                nc.scalar.activation(hT[:], norm_ps[:], ACT.Identity, bias=k.mod[0][:, lo[0], bass.ds(b, 1)],
                                     scale=k.mod[0][:, lo[1], bass.ds(b, 1)]).then_inc(hT_ready, 1)
                act.wait_ge(hT_ready, b + 1)
                nc.scalar.activation(h_hi[:, odd, :], hT[:], ACT.Copy, scale=H_SCALE).then_inc(h_hi_ready, 1)

            def exponentials(b):
                act.wait_ge(router_step, b * ROUTER_STEPS + 2)
                nc.scalar.activation(prob[:], shifted[:], ACT.Exp).then_inc(exps_ready, 1)

            for q in range(QUADS):
                which, step = divmod(q * 4, STEPS)
                act.wait_ge(w_turned, q + 1)
                nc.scalar.activation(w_hi[:, which, step:step + 4, :], banks[q % 4][:].rearrange("p (i c) -> p i c", i=4), ACT.Copy,
                                     scale=W_SCALE).then_inc(w_hi_stored, 1)
            store_hT(0, 0)

            def high_part(b, n, warm):
                if warm:
                    act.wait_ge(down_done, b * STEPS + n - 3)
                act.wait_ge(hid_ready, b * STEPS + n + 1)
                nc.scalar.copy(hid_hi[:, n % 4, :], hid[:, n % 2, :]).then_inc(hid_hi_ready, 1)

            def body(b, odd, first, following):
                for n in range(STEPS):
                    act.wait_ge(gate_ready, b * STEPS + n + 1)
                    nc.scalar.activation(th[:, n % 2, :], gate_ps[n % 2][:], ACT.Tanh, scale=0.5 / PROJ_SCALE).then_inc(tanh_ready, 1)
                    if n >= 1:
                        high_part(b, n - 1, not first or n - 1 >= 4)
                    elif not first:
                        high_part(b - 1, STEPS - 1, True)
                    if first and n == 1:
                        exponentials(b)
                    if following:
                        if n == 18:
                            store_hT(b + 1, 1 - odd)
                        if n == 25:
                            exponentials(b + 1)
                if not following:
                    high_part(b, STEPS - 1, True)

            run(act, body)

        @block.vector
        def _(dve):
            for q in range(QUADS):
                which, step = divmod(q * 4, STEPS)
                dve.wait_ge(w_hi_stored, q + 1)
                nc.vector.scalar_tensor_tensor(w_lo[:, which, step:step + 4, :], banks[q % 4][:].rearrange("p (i c) -> p i c", i=4), W_SCALE,
                                               w_hi[:, which, step:step + 4, :], ALU.mult, ALU.subtract).then_inc(w_lo_stored, 1)

            def silu_times_up(b, n, warm):
                dve.wait_ge(tanh_ready, b * STEPS + n + 1)
                nc.vector.scalar_tensor_tensor(half[:, n % 2, :], th[:, n % 2, :], 1.0, gate_ps[n % 2][:], ALU.add,
                                               ALU.mult).then_inc(silu_ready, 1)
                dve.wait_ge(silu_ready, b * STEPS + n + 1)
                dve.wait_ge(up_ready, b * STEPS + n + 1)
                if warm:
                    dve.wait_ge(hid_lo_ready, b * STEPS + n - 1)
                nc.vector.scalar_tensor_tensor(hid[:, n % 2, :], half[:, n % 2, :], HID_SCALE / PROJ_SCALE ** 2, up_ps[n % 2][:],
                                               ALU.mult, ALU.mult).then_inc(hid_ready, 1)

            def route(b, part, odd):
                count = [(0, 2, 5, 8, 11)[part]]

                def link(ins):
                    count[0] += 1
                    ins.then_inc(router_step, 1)
                    dve.wait_ge(router_step, b * ROUTER_STEPS + count[0])

                each = [P, NT, E]
                pairs = [P, NT, E, E]
                logits = logit_ps[:, 0:NT * E].rearrange("p (t e) -> p t e", t=NT)
                other = prob[:, :, None, :].to_broadcast(pairs)
                own = prob[:, :, :, None].to_broadcast(pairs)
                if part == 0:
                    dve.wait_ge(logits_ready, b + 1)
                    link(nc.vector.tensor_reduce(top[:], logits, AX.X, ALU.max))
                    link(nc.vector.tensor_tensor(shifted[:], logits, top[:, :, None].to_broadcast(each), ALU.subtract))
                elif part == 1:
                    dve.wait_ge(exps_ready, b + 1)
                    link(nc.vector.tensor_reduce(total[:], prob[:], AX.X, ALU.add))
                    link(nc.vector.reciprocal(total[:], total[:]))
                    link(nc.vector.tensor_tensor(prob[:], prob[:], total[:, :, None].to_broadcast(each), ALU.mult))
                elif part == 2:
                    link(nc.vector.tensor_tensor(above[:], other, own, ALU.is_gt))
                    link(nc.vector.tensor_tensor(tied[:], other, own, ALU.is_equal))
                    link(nc.vector.tensor_tensor(tied[:], tied[:], k.c["before"].rearrange("p (e j) -> p e j", e=E)[:, None, :, :].to_broadcast(pairs),
                                                 ALU.mult))
                elif part == 3:
                    link(nc.vector.tensor_tensor(above[:], above[:], tied[:], ALU.add))
                    link(nc.vector.tensor_reduce(rank[:], above[:], AX.X, ALU.add))
                    link(nc.vector.scalar_tensor_tensor(rank[:], rank[:], 2.0, prob[:], ALU.is_lt, ALU.mult))
                else:
                    link(nc.vector.tensor_reduce(total[:], rank[:], AX.X, ALU.add))
                    link(nc.vector.reciprocal(total[:], total[:]))
                    link(nc.vector.scalar_tensor_tensor(weight[:, odd], rank[:], 0.5 / (HID_SCALE * W_SCALE),
                                                        total[:, :, None].to_broadcast(each), ALU.mult, ALU.mult))

            def combine(b, e, first, odd):
                dve.wait_ge(down_done, b * STEPS + (e + 1) * FT)
                if e == 0 and not first:
                    dve.wait_ge(x_updated, b)
                if e > 0:
                    dve.wait_ge(combined, b * E + e)
                for t in range(NT):
                    y = down_ps[e % 2][:, t * P:(t + 1) * P]
                    w = weight[:, odd, t, e:e + 1]
                    if e == 0:
                        last = nc.vector.tensor_scalar(acc[:, t, :], y, w, None, ALU.mult)
                    else:
                        last = nc.vector.scalar_tensor_tensor(acc[:, t, :], y, w, acc[:, t, :], ALU.mult, ALU.add)
                last.then_inc(combined, 1)

            def low_part(b, odd):
                dve.wait_ge(h_hi_ready, b + 1)
                nc.vector.scalar_tensor_tensor(h_lo[:, odd, :], hT[:], H_SCALE, h_hi[:, odd, :], ALU.mult,
                                               ALU.subtract).then_inc(h_lo_ready, 1)

            def body(b, odd, first, following):
                if first:
                    low_part(b, odd)
                    route(b, 0, odd)
                for n in range(STEPS):
                    silu_times_up(b, n, not first or n >= 2)
                    if first and 2 <= n < 6:
                        route(b, n - 1, odd)
                    if n >= 7 and (n - 7) % FT == 0:
                        combine(b, (n - 7) // FT, first, odd)
                    if n == 3 and not first:
                        combine(b - 1, E - 1, first, 1 - odd)
                    if following:
                        if n == 8:
                            norm.moments(dve, b + 1)
                        if n == 12:
                            norm.normalise(dve, b + 1)
                        if n == 20:
                            low_part(b + 1, 1 - odd)
                        if n == 24:
                            route(b + 1, 0, 1 - odd)
                        if n in (26, 28, 29, 30):
                            route(b + 1, {26: 1, 28: 2, 29: 3, 30: 4}[n], 1 - odd)
                    if not following and n == 20:
                        next_norm.moments_ahead(dve, norm, x_updated)
                    if not following and n == 24:
                        next_norm.normalise(dve, 0)
                if not following:
                    combine(b, E - 1, first, odd)

            run(dve, body)

        @block.gpsimd
        def _(pool):
            def update_x(b):
                xb = k.x[:, bass.ds(b * NT, NT), :]
                pool.wait_ge(combined, (b + 1) * E)
                nc.gpsimd.tensor_tensor(acc[:], acc[:], k.gate[0][:, 1, bass.ds(b, 1), :].to_broadcast([P, NT, D]),
                                        ALU.mult).then_inc(gated, 1)
                pool.wait_ge(gated, b + 1)
                nc.gpsimd.tensor_tensor(xb, xb, acc[:], ALU.add).then_inc(x_updated, 1)

            def body(b, odd, first, following):
                for n in range(STEPS):
                    if not following and n == 22:
                        next_norm.inverse_deviation(pool, 0)
                    pool.wait_ge(hid_hi_ready, b * STEPS + n + 1)
                    nc.gpsimd.tensor_tensor(hid_lo[:, n % 4, :], hid[:, n % 2, :], hid_hi[:, n % 4, :],
                                            ALU.subtract).then_inc(hid_lo_ready, 1)
                    if n == 3 and not first:
                        update_x(b - 1)
                    if n == 10 and following:
                        norm.inverse_deviation(pool, b + 1)
                if not following:
                    update_x(b)

            run(pool, body)


def units_phase(k):
    nc = k.nc
    LAG = 2
    with ExitStack() as ctx:
        def sb(name, shape, dt=F32):
            return k.sb(f"un_{name}", shape, dt, ctx)

        def sem(name):
            return ctx.enter_context(nc.semaphore(f"un_{name}"))

        def bank(name):
            return ctx.enter_context(nc.psum_tensor(f"un_{name}", [P, 512], F32))

        unit_ps = [bank(f"unit{i}") for i in range(4)]
        out_ps = [bank(f"out{i}") for i in range(2)]
        norm_ps = bank("norm")
        s_ps = bank("s")
        hT = sb("hT", [P, T])
        select = sb("select", [P, NJ * P], F16)
        s_parts = sb("s_parts", [P, 2, T], F16)
        relu = sb("relu", [P, 4, T])
        gated_bias = sb("gated_bias", [P, D])
        gated_out = sb("gated_out", [P, NT, D])
        norm = k.norms[3]
        select_loaded = sem("select_loaded")
        hT_ready = sem("hT_ready")
        s_ready = sem("s_ready")
        s_rounded = sem("s_rounded")
        s_split = sem("s_split")
        unit_ready = sem("unit_ready")
        relu_ready = sem("relu_ready")
        out_added = sem("out_added")
        bias_gated = sem("bias_gated")
        bias_added = sem("bias_added")
        out_gated = sem("out_gated")
        x_updated = sem("x_updated")
        x_stored = sem("x_stored")

        def run(engine, body):
            body(0, 0, True, True)
            with engine.Fori(0, (B - 2) // 2) as pair:
                body(pair * 2 + 1, 1, False, True)
                body(pair * 2 + 2, 0, False, True)
            body(B - 1, (B - 1) % 2, False, False)

        block = ctx.enter_context(nc.Block())

        @block.sync
        def _(sp):
            sp.dma_start(select[:], k.a["const_select"]).then_inc(select_loaded, 16)

            def body(b, odd, first, following):
                sp.wait_ge(x_updated, b + 1)
                sp.dma_start(k.out[bass.ds(b, 1)].rearrange("b (t p) d -> p (b t) d", p=P),
                             k.x[:, bass.ds(b * NT, NT), :]).then_inc(x_stored, 16)

            run(sp, body)
            sp.wait_ge(x_stored, 16 * B)

        @block.tensor
        def _(pe):
            def make_s(b):
                pe.wait_ge(hT_ready, b + 1)
                if not (isinstance(b, int) and b == 0):
                    pe.wait_ge(s_split, b)
                nc.tensor.matmul(s_ps[:], k.win_twice[:].rearrange("p i m -> p (i m)"), hT[:], start=True,
                                 stop=True).then_inc(s_ready, 1)

            def unit(b, odd, j, warm):
                if warm:
                    pe.wait_ge(relu_ready, b * NJ + j - 3)
                nc.tensor.matmul(unit_ps[j % 4][:], select[:, j * P:(j + 1) * P], s_parts[:, odd, :], start=True,
                                 stop=True).then_inc(unit_ready, 1)

            def add_out(b, odd, j, warm):
                pe.wait_ge(relu_ready, b * NJ + j + 1)
                if j == 0 and warm:
                    pe.wait_ge(out_gated, b - 1)
                for t in range(NT):
                    last = nc.tensor.matmul(out_ps[odd][:, t * P:(t + 1) * P], relu[:, j % 4, t * P:(t + 1) * P], k.wout_rep[:, j, :],
                                            start=(j == 0 and t == 0), stop=(j == NJ - 1), skip_group_check=True)
                last.then_inc(out_added, 1)

            def body(b, odd, first, following):
                if first:
                    norm.transpose(pe, b, norm_ps)
                    make_s(b)
                    pe.wait_ge(select_loaded, 16)
                pe.wait_ge(s_split, b + 1)
                for j in range(NJ):
                    unit(b, odd, j, not first or j >= 4)
                    if j >= LAG:
                        add_out(b, odd, j - LAG, not (isinstance(b, int) and b == 0))
                    elif not first:
                        add_out(b - 1, 1 - odd, NJ - LAG + j, True)
                    if following and j == 2:
                        norm.transpose(pe, b + 1, norm_ps)
                    if following and j == 4:
                        make_s(b + 1)
                if not following:
                    for j in range(NJ - LAG, NJ):
                        add_out(b, odd, j, True)

            run(pe, body)

        @block.scalar
        def _(act):
            def store_hT(b):
                act.wait_ge(norm.hn_transposed, b + 1)
                if not (isinstance(b, int) and b == 0):
                    act.wait_ge(s_ready, b)
                lo = MOD_ROWS["ffn"]
                nc.scalar.activation(hT[:], norm_ps[:], ACT.Identity, bias=k.mod[1][:, lo[0], bass.ds(b, 1)],
                                     scale=k.mod[1][:, lo[1], bass.ds(b, 1)]).then_inc(hT_ready, 1)

            def round_s(b, odd):
                act.wait_ge(s_ready, b + 1)
                nc.scalar.copy(s_parts[:, odd, :], s_ps[:]).then_inc(s_rounded, 1)

            def body(b, odd, first, following):
                if first:
                    store_hT(b)
                    round_s(b, odd)
                for j in range(NJ):
                    if not (first and j < 4):
                        act.wait_ge(out_added, b * NJ + j - 3)
                    act.wait_ge(unit_ready, b * NJ + j + 1)
                    nc.scalar.activation(relu[:, j % 4, :], unit_ps[j % 4][:], ACT.Relu, bias=k.b1c[:, j:j + 1],
                                         scale=k.w1c[:, j:j + 1]).then_inc(relu_ready, 1)
                    if following and j == 2:
                        store_hT(b + 1)
                    if following and j == 5:
                        round_s(b + 1, 1 - odd)

            run(act, body)

        @block.vector
        def _(dve):
            def split_s(b, odd):
                dve.wait_ge(s_rounded, b + 1)
                nc.vector.tensor_tensor(s_parts[M:2 * M, odd, :], s_ps[M:2 * M, :], s_parts[M:2 * M, odd, :],
                                        ALU.subtract).then_inc(s_split, 1)

            def update_x(b, odd):
                if not (isinstance(b, int) and b == 0):
                    dve.wait_ge(x_updated, b)
                dve.wait_ge(out_added, (b + 1) * NJ)
                nc.vector.tensor_tensor(gated_out[:], out_ps[odd][:].rearrange("p (t d) -> p t d", t=NT),
                                        k.gate[1][:, 1, bass.ds(b, 1), :].to_broadcast([P, NT, D]), ALU.mult).then_inc(out_gated, 1)
                dve.wait_ge(out_gated, b + 1)
                dve.wait_ge(bias_added, b + 1)
                xb = k.x[:, bass.ds(b * NT, NT), :]
                nc.vector.tensor_tensor(xb, xb, gated_out[:], ALU.add).then_inc(x_updated, 1)

            def body(b, odd, first, following):
                if first:
                    split_s(b, odd)
                if following:
                    norm.moments(dve, b + 1)
                    norm.normalise(dve, b + 1)
                if not first:
                    update_x(b - 1, 1 - odd)
                if following:
                    split_s(b + 1, 1 - odd)
                else:
                    update_x(b, odd)

            run(dve, body)

        @block.gpsimd
        def _(pool):
            def add_bias(b):
                if not (isinstance(b, int) and b == 0):
                    pool.wait_ge(bias_added, b)
                nc.gpsimd.tensor_tensor(gated_bias[:], k.bout[:], k.gate[1][:, 1, b, :], ALU.mult).then_inc(bias_gated, 1)
                pool.wait_ge(bias_gated, b + 1)
                pool.wait_ge(norm.hn_ready, (b + 1) * NT)
                xb = k.x[:, bass.ds(b * NT, NT), :]
                nc.gpsimd.tensor_tensor(xb, xb, gated_bias[:, None, :].to_broadcast([P, NT, D]), ALU.add).then_inc(bias_added, 1)

            def body(b, odd, first, following):
                if following:
                    norm.inverse_deviation(pool, b + 1)
                add_bias(b)

            run(pool, body)


_INS = ["L0_attn_content", "L0_attn_Wq", "L0_attn_Wk", "L0_attn_Wv", "L0_ffn_W_router", "L0_ffn_W_gate", "L0_ffn_W_up",
        "L0_ffn_W_down", "L0_c", "L0_wmod", "L1_attn_W_Q", "L1_attn_W_K", "L1_attn_W_V", "L1_attn_W_O", "L1_ffn_Win",
        "L1_ffn_bin_", "L1_ffn_W1", "L1_ffn_b1", "L1_ffn_W2", "L1_ffn_b2", "L1_ffn_Wout", "L1_ffn_bout", "L1_c", "L1_wmod"]


def kernel(**inputs):
    import concourse.bacc as bacc
    from concourse.bass_utils import run_bass_kernel_spmd

    nc = bacc.Bacc("TRN2", target_bir_lowering=False, num_devices=1)
    off, shape_constants = constants()
    arrays = {f"in_{n}": np.ascontiguousarray(inputs[n]) for n in _INS}
    arrays.update({f"in_{n}": v for n, v in shape_constants.items()})
    aps = {n[3:]: nc.dram_tensor(n, v.shape, mybir.dt.from_np(v.dtype), kind="ExternalInput").ap() for n, v in arrays.items()}
    out = nc.dram_tensor("out_x", (B, T, D), F32, kind="ExternalOutput").ap()
    adaln_kernel(nc, aps, out, off)
    r = run_bass_kernel_spmd(nc, [arrays], core_ids=[0])
    return r.results[0]["out_x"]
```
